# Optimizing a Trainium2 kernel written in Bass

```python
import numpy as np
import jax
import jax.numpy as jnp

def _softmax(x, axis=-1):
    return jax.nn.softmax(x, axis=axis)

def _gelu(x):
    return jax.nn.gelu(x, approximate=True)

def _silu(x):
    return jax.nn.silu(x)

def _sigmoid(x):
    return jax.nn.sigmoid(x)

def _layernorm(x, axis=-1, eps=1e-05):
    m = jnp.mean(x, axis=axis, keepdims=True)
    v = jnp.var(x, axis=axis, keepdims=True)
    return (x - m) / jnp.sqrt(v + eps)

def _scatter_add(tgt, idx, src, axis=0):
    return tgt.at[idx].add(src)

def _segment_sum(src, seg, n):
    return jax.ops.segment_sum(src, seg, n)
kernel_name = 'mk_gnn_preln_d2_gnn_r8_fc5fcf'

def setup_inputs(seed: int=0):
    np.random.seed(seed)
    _w = jnp.asarray

    def _rec_inputs():
        import jax
        import jax.numpy as jnp
        _gk = jax.random.key(seed)
        x = -0.000202 + 1 * jax.random.normal(jax.random.fold_in(_gk, 1), (12500, 128), jnp.float32)
        src = jax.random.randint(jax.random.fold_in(_gk, 2), (200000,), 0, 12500, jnp.int32)
        dst = jnp.minimum((12500 * jax.random.uniform(jax.random.fold_in(_gk, 3), (200000,)) ** 2.0).astype(jnp.int32), 99999)
        _o = jnp.argsort(dst, stable=True)
        src = src[_o]
        dst = dst[_o]
        edge_attr_9 = 0.000458729 + 1.00015 * jax.random.normal(jax.random.fold_in(_gk, 11), (200000, 9), jnp.float32)
        edge_weight = jax.random.uniform(jax.random.fold_in(_gk, 13), (200000,), jnp.float32, 0.0, 1)
        return (x, src, dst, edge_attr_9, edge_weight)
    x, src, dst, edge_attr_9, edge_weight = _rec_inputs()

    def _L0_gnn_setup():
        import jax, jax.numpy as jnp
        import numpy as np
        N, E, IN_DIM, OUT_DIM, HEADS = (6250, 100000, 128, 32, 4)

        def _linear_params(key, fan_in, fan_out, bias=True):
            kw, kb = jax.random.split(key)
            s = 1.0 / np.sqrt(fan_in)
            W = jax.random.uniform(kw, (fan_in, fan_out), jnp.float32, -s, s)
            b = jax.random.uniform(kb, (fan_out,), jnp.float32, -s, s) if bias else None
            return (W, b)

        def _transformer_conv(x, src, dst, ea, Wq, bq, Wk, bk, Wv, bv, We, Ws, bs, H, C):
            n = x.shape[0]
            q = (x @ Wq + bq).reshape(n, H, C)
            k = (x @ Wk + bk).reshape(n, H, C)
            v = (x @ Wv + bv).reshape(n, H, C)
            e = (ea @ We).reshape(-1, H, C)
            kj = k[src] + e
            vj = v[src] + e
            alpha = jnp.einsum('ehc,ehc->eh', q[dst], kj) / jnp.sqrt(jnp.asarray(C, x.dtype))
            amax = jax.ops.segment_max(alpha, dst, num_segments=n)
            p = jnp.exp(alpha - amax[dst])
            denom = jax.ops.segment_sum(p, dst, num_segments=n)
            w = p / denom[dst]
            msg = (vj * w[..., None]).reshape(-1, H * C)
            out = jax.ops.segment_sum(msg, dst, num_segments=n)
            return out + x @ Ws + bs
        key = jax.random.key(seed)
        ks = jax.random.split(key, 24)
        H, C = (HEADS, OUT_DIM)
        inp = {'x': jax.random.normal(ks[0], (N, IN_DIM), jnp.float32), 'edge_weight': jax.random.uniform(ks[1], (E,), jnp.float32)}
        for li, fan_in in ((1, IN_DIM), (2, H * C)):
            base = 2 + (li - 1) * 10
            inp[f'Wq{li}'], inp[f'bq{li}'] = _linear_params(ks[base + 0], fan_in, H * C)
            inp[f'Wk{li}'], inp[f'bk{li}'] = _linear_params(ks[base + 1], fan_in, H * C)
            inp[f'Wv{li}'], inp[f'bv{li}'] = _linear_params(ks[base + 2], fan_in, H * C)
            We, _ = _linear_params(ks[base + 3], 1, H * C, bias=False)
            inp[f'We{li}'] = We
            inp[f'Ws{li}'], inp[f'bs{li}'] = _linear_params(ks[base + 4], fan_in, H * C)
        inp['edge_index'] = jax.random.randint(ks[22], (2, E), 0, N, jnp.int64)
        return inp
    _L0_gnn_all = _L0_gnn_setup()
    _L0_gnn_in = {k: v for k, v in _L0_gnn_all.items() if k in ('Wq1', 'bq1', 'Wk1', 'bk1', 'Wv1', 'bv1', 'We1', 'Ws1', 'bs1', 'Wq2', 'bq2', 'Wk2', 'bk2', 'Wv2', 'bv2', 'We2', 'Ws2', 'bs2')}
    del _L0_gnn_all

    def _L1_gnn_setup():
        import jax, jax.numpy as jnp
        import numpy as np
        from fractions import Fraction
        from math import factorial

        def _su2_cg_coeff(j1, m1, j2, m2, j3, m3):
            if m3 != m1 + m2:
                return 0.0
            vmin = int(max(-j1 + j2 + m3, -j1 + m1, 0))
            vmax = int(min(j2 + j3 + m1, j3 - j1 + j2, j3 + m3))
            f = lambda n: factorial(round(n))
            C = ((2.0 * j3 + 1.0) * Fraction(f(j3 + j1 - j2) * f(j3 - j1 + j2) * f(j1 + j2 - j3) * f(j3 + m3) * f(j3 - m3), f(j1 + j2 + j3 + 1) * f(j1 - m1) * f(j1 + m1) * f(j2 - m2) * f(j2 + m2))) ** 0.5
            S = 0
            for v in range(vmin, vmax + 1):
                S += (-1) ** (v + j2 + m2) * Fraction(f(j2 + j3 + m1 - v) * f(j1 - m1 + v), f(v) * f(j3 - j1 + j2 - v) * f(j3 + m3 - v) * f(v + j1 - j2 - m3))
            return float(C * S)

        def _change_basis_real_to_complex(l):
            q = np.zeros((2 * l + 1, 2 * l + 1), dtype=np.complex128)
            for m in range(-l, 0):
                q[l + m, l + abs(m)] = 1 / np.sqrt(2)
                q[l + m, l - abs(m)] = -1j / np.sqrt(2)
            q[l, l] = 1
            for m in range(1, l + 1):
                q[l + m, l + abs(m)] = (-1) ** m / np.sqrt(2)
                q[l + m, l - abs(m)] = 1j * (-1) ** m / np.sqrt(2)
            return (-1j) ** l * q

        def wigner_3j(l1, l2, l3):
            C = np.zeros((2 * l1 + 1, 2 * l2 + 1, 2 * l3 + 1))
            for m1 in range(-l1, l1 + 1):
                for m2 in range(-l2, l2 + 1):
                    m3 = m1 + m2
                    if abs(m3) <= l3:
                        C[l1 + m1, l2 + m2, l3 + m3] = _su2_cg_coeff(l1, m1, l2, m2, l3, m3)
            Q1 = _change_basis_real_to_complex(l1)
            Q2 = _change_basis_real_to_complex(l2)
            Q3 = _change_basis_real_to_complex(l3)
            Cc = np.einsum('ij,kl,mn,ikn->jlm', Q1, Q2, np.conj(Q3.T), C.astype(np.complex128))
            Cr = np.real(Cc)
            return Cr / np.linalg.norm(Cr)
        MUL = 32
        IRREPS_IN = [(MUL, 0, 1), (MUL, 1, -1)]
        IRREPS_SH = [(1, 0, 1), (1, 1, -1), (1, 2, 1)]
        IRREPS_OUT = [(MUL, 0, 1), (MUL, 1, -1)]
        NUM_NEIGHBORS = 10.0
        N_NODES, N_EDGES = (1250, 12500)

        def _dim(irreps):
            return sum((m * (2 * l + 1) for m, l, _ in irreps))

        def _slices(irreps):
            s, out = (0, [])
            for m, l, _ in irreps:
                d = m * (2 * l + 1)
                out.append((s, s + d))
                s += d
            return out

        def _instructions():
            ins = []
            for i1, (m1, l1, p1) in enumerate(IRREPS_IN):
                for i2, (m2, l2, p2) in enumerate(IRREPS_SH):
                    for io, (mo, lo, po) in enumerate(IRREPS_OUT):
                        if abs(l1 - l2) <= lo <= l1 + l2 and p1 * p2 == po:
                            ins.append((i1, i2, io))
            return ins
        _INSTR = _instructions()
        _SL_IN, _SL_SH, _SL_OUT = (_slices(IRREPS_IN), _slices(IRREPS_SH), _slices(IRREPS_OUT))
        _W3J = [jnp.asarray(wigner_3j(IRREPS_IN[i1][1], IRREPS_SH[i2][1], IRREPS_OUT[io][1]), dtype=jnp.float32) for i1, i2, io in _INSTR]
        _NORM = []
        for _i1, _i2, _io in _INSTR:
            _alpha = 2 * IRREPS_OUT[_io][1] + 1
            _x = sum((IRREPS_IN[j1][0] * IRREPS_SH[j2][0] for j1, j2, jo in _INSTR if jo == _io))
            _NORM.append(float(np.sqrt(_alpha / _x)))

        def _tensor_product(x1, x2, weights):
            E = x1.shape[0]
            out = jnp.zeros((E, _dim(IRREPS_OUT)), dtype=x1.dtype)
            for k, (i1, i2, io) in enumerate(_INSTR):
                m1, l1, _ = IRREPS_IN[i1]
                m2, l2, _ = IRREPS_SH[i2]
                mo, lo, _ = IRREPS_OUT[io]
                a, b = _SL_IN[i1]
                c, d = _SL_SH[i2]
                e, f = _SL_OUT[io]
                x1s = x1[:, a:b].reshape(E, m1, 2 * l1 + 1)
                x2s = x2[:, c:d].reshape(E, m2, 2 * l2 + 1)
                seg = jnp.einsum('uvw,ijk,eui,evj->ewk', weights[k], _W3J[k], x1s, x2s, optimize='optimal') * _NORM[k]
                out = out.at[:, e:f].add(seg.reshape(E, mo * (2 * lo + 1)))
            return out
        key = jax.random.key(seed)
        ks = jax.random.split(key, 8)
        x = jax.random.normal(ks[0], (N_NODES, _dim(IRREPS_IN)), dtype=jnp.float32)
        edge_index = jax.random.randint(ks[1], (2, N_EDGES), 0, N_NODES)
        edge_attr = jax.random.normal(ks[2], (N_EDGES, _dim(IRREPS_SH)), dtype=jnp.float32)
        ws = {f'w{k}': jax.random.normal(ks[3 + k], (MUL, 1, MUL), dtype=jnp.float32) for k in range(len(_INSTR))}
        return {'x': x, 'edge_index': edge_index, 'edge_attr': edge_attr, **ws}
    _L1_gnn_all = _L1_gnn_setup()
    _L1_gnn_in = {k: v for k, v in _L1_gnn_all.items() if k in ('w0', 'w1', 'w2', 'w3', 'w4')}
    del _L1_gnn_all
    return {'x': x, 'src': src, 'dst': dst, 'edge_attr_9': edge_attr_9, 'edge_weight': edge_weight, 'L0_gnn_Wq1': _L0_gnn_in['Wq1'], 'L0_gnn_bq1': _L0_gnn_in['bq1'], 'L0_gnn_Wk1': _L0_gnn_in['Wk1'], 'L0_gnn_bk1': _L0_gnn_in['bk1'], 'L0_gnn_Wv1': _L0_gnn_in['Wv1'], 'L0_gnn_bv1': _L0_gnn_in['bv1'], 'L0_gnn_We1': _L0_gnn_in['We1'], 'L0_gnn_Ws1': _L0_gnn_in['Ws1'], 'L0_gnn_bs1': _L0_gnn_in['bs1'], 'L0_gnn_Wq2': _L0_gnn_in['Wq2'], 'L0_gnn_bq2': _L0_gnn_in['bq2'], 'L0_gnn_Wk2': _L0_gnn_in['Wk2'], 'L0_gnn_bk2': _L0_gnn_in['bk2'], 'L0_gnn_Wv2': _L0_gnn_in['Wv2'], 'L0_gnn_bv2': _L0_gnn_in['bv2'], 'L0_gnn_We2': _L0_gnn_in['We2'], 'L0_gnn_Ws2': _L0_gnn_in['Ws2'], 'L0_gnn_bs2': _L0_gnn_in['bs2'], 'L1_gnn_w0': _L1_gnn_in['w0'], 'L1_gnn_w1': _L1_gnn_in['w1'], 'L1_gnn_w2': _L1_gnn_in['w2'], 'L1_gnn_w3': _L1_gnn_in['w3'], 'L1_gnn_w4': _L1_gnn_in['w4']}

def reference(x, src, dst, edge_attr_9, edge_weight, L0_gnn_Wq1, L0_gnn_bq1, L0_gnn_Wk1, L0_gnn_bk1, L0_gnn_Wv1, L0_gnn_bv1, L0_gnn_We1, L0_gnn_Ws1, L0_gnn_bs1, L0_gnn_Wq2, L0_gnn_bq2, L0_gnn_Wk2, L0_gnn_bk2, L0_gnn_Wv2, L0_gnn_bv2, L0_gnn_We2, L0_gnn_Ws2, L0_gnn_bs2, L1_gnn_w0, L1_gnn_w1, L1_gnn_w2, L1_gnn_w3, L1_gnn_w4):
    import jax
    import jax.numpy as jnp

    def _L0_gnn_ref(x, edge_weight, Wq1, bq1, Wk1, bk1, Wv1, bv1, We1, Ws1, bs1, Wq2, bq2, Wk2, bk2, Wv2, bv2, We2, Ws2, bs2, edge_index):
        import jax, jax.numpy as jnp
        import numpy as np
        N, E, IN_DIM, OUT_DIM, HEADS = (6250, 100000, 128, 32, 4)

        def _linear_params(key, fan_in, fan_out, bias=True):
            kw, kb = jax.random.split(key)
            s = 1.0 / np.sqrt(fan_in)
            W = jax.random.uniform(kw, (fan_in, fan_out), jnp.float32, -s, s)
            b = jax.random.uniform(kb, (fan_out,), jnp.float32, -s, s) if bias else None
            return (W, b)

        def _transformer_conv(x, src, dst, ea, Wq, bq, Wk, bk, Wv, bv, We, Ws, bs, H, C):
            n = x.shape[0]
            q = (x @ Wq + bq).reshape(n, H, C)
            k = (x @ Wk + bk).reshape(n, H, C)
            v = (x @ Wv + bv).reshape(n, H, C)
            e = (ea @ We).reshape(-1, H, C)
            kj = k[src] + e
            vj = v[src] + e
            alpha = jnp.einsum('ehc,ehc->eh', q[dst], kj) / jnp.sqrt(jnp.asarray(C, x.dtype))
            amax = jax.ops.segment_max(alpha, dst, num_segments=n)
            p = jnp.exp(alpha - amax[dst])
            denom = jax.ops.segment_sum(p, dst, num_segments=n)
            w = p / denom[dst]
            msg = (vj * w[..., None]).reshape(-1, H * C)
            out = jax.ops.segment_sum(msg, dst, num_segments=n)
            return out + x @ Ws + bs
        src, dst = (edge_index[0], edge_index[1])
        ea = edge_weight[:, None]
        h = _transformer_conv(x, src, dst, ea, Wq1, bq1, Wk1, bk1, Wv1, bv1, We1, Ws1, bs1, HEADS, OUT_DIM)
        out = _transformer_conv(h, src, dst, ea, Wq2, bq2, Wk2, bk2, Wv2, bv2, We2, Ws2, bs2, HEADS, OUT_DIM)
        return out

    def _L1_gnn_ref(x, edge_index, edge_attr, w0, w1, w2, w3, w4):
        import jax, jax.numpy as jnp
        import numpy as np
        from fractions import Fraction
        from math import factorial

        def _su2_cg_coeff(j1, m1, j2, m2, j3, m3):
            if m3 != m1 + m2:
                return 0.0
            vmin = int(max(-j1 + j2 + m3, -j1 + m1, 0))
            vmax = int(min(j2 + j3 + m1, j3 - j1 + j2, j3 + m3))
            f = lambda n: factorial(round(n))
            C = ((2.0 * j3 + 1.0) * Fraction(f(j3 + j1 - j2) * f(j3 - j1 + j2) * f(j1 + j2 - j3) * f(j3 + m3) * f(j3 - m3), f(j1 + j2 + j3 + 1) * f(j1 - m1) * f(j1 + m1) * f(j2 - m2) * f(j2 + m2))) ** 0.5
            S = 0
            for v in range(vmin, vmax + 1):
                S += (-1) ** (v + j2 + m2) * Fraction(f(j2 + j3 + m1 - v) * f(j1 - m1 + v), f(v) * f(j3 - j1 + j2 - v) * f(j3 + m3 - v) * f(v + j1 - j2 - m3))
            return float(C * S)

        def _change_basis_real_to_complex(l):
            q = np.zeros((2 * l + 1, 2 * l + 1), dtype=np.complex128)
            for m in range(-l, 0):
                q[l + m, l + abs(m)] = 1 / np.sqrt(2)
                q[l + m, l - abs(m)] = -1j / np.sqrt(2)
            q[l, l] = 1
            for m in range(1, l + 1):
                q[l + m, l + abs(m)] = (-1) ** m / np.sqrt(2)
                q[l + m, l - abs(m)] = 1j * (-1) ** m / np.sqrt(2)
            return (-1j) ** l * q

        def wigner_3j(l1, l2, l3):
            C = np.zeros((2 * l1 + 1, 2 * l2 + 1, 2 * l3 + 1))
            for m1 in range(-l1, l1 + 1):
                for m2 in range(-l2, l2 + 1):
                    m3 = m1 + m2
                    if abs(m3) <= l3:
                        C[l1 + m1, l2 + m2, l3 + m3] = _su2_cg_coeff(l1, m1, l2, m2, l3, m3)
            Q1 = _change_basis_real_to_complex(l1)
            Q2 = _change_basis_real_to_complex(l2)
            Q3 = _change_basis_real_to_complex(l3)
            Cc = np.einsum('ij,kl,mn,ikn->jlm', Q1, Q2, np.conj(Q3.T), C.astype(np.complex128))
            Cr = np.real(Cc)
            return Cr / np.linalg.norm(Cr)
        MUL = 32
        IRREPS_IN = [(MUL, 0, 1), (MUL, 1, -1)]
        IRREPS_SH = [(1, 0, 1), (1, 1, -1), (1, 2, 1)]
        IRREPS_OUT = [(MUL, 0, 1), (MUL, 1, -1)]
        NUM_NEIGHBORS = 10.0
        N_NODES, N_EDGES = (1250, 12500)

        def _dim(irreps):
            return sum((m * (2 * l + 1) for m, l, _ in irreps))

        def _slices(irreps):
            s, out = (0, [])
            for m, l, _ in irreps:
                d = m * (2 * l + 1)
                out.append((s, s + d))
                s += d
            return out

        def _instructions():
            ins = []
            for i1, (m1, l1, p1) in enumerate(IRREPS_IN):
                for i2, (m2, l2, p2) in enumerate(IRREPS_SH):
                    for io, (mo, lo, po) in enumerate(IRREPS_OUT):
                        if abs(l1 - l2) <= lo <= l1 + l2 and p1 * p2 == po:
                            ins.append((i1, i2, io))
            return ins
        _INSTR = _instructions()
        _SL_IN, _SL_SH, _SL_OUT = (_slices(IRREPS_IN), _slices(IRREPS_SH), _slices(IRREPS_OUT))
        _W3J = [jnp.asarray(wigner_3j(IRREPS_IN[i1][1], IRREPS_SH[i2][1], IRREPS_OUT[io][1]), dtype=jnp.float32) for i1, i2, io in _INSTR]
        _NORM = []
        for _i1, _i2, _io in _INSTR:
            _alpha = 2 * IRREPS_OUT[_io][1] + 1
            _x = sum((IRREPS_IN[j1][0] * IRREPS_SH[j2][0] for j1, j2, jo in _INSTR if jo == _io))
            _NORM.append(float(np.sqrt(_alpha / _x)))

        def _tensor_product(x1, x2, weights):
            E = x1.shape[0]
            out = jnp.zeros((E, _dim(IRREPS_OUT)), dtype=x1.dtype)
            for k, (i1, i2, io) in enumerate(_INSTR):
                m1, l1, _ = IRREPS_IN[i1]
                m2, l2, _ = IRREPS_SH[i2]
                mo, lo, _ = IRREPS_OUT[io]
                a, b = _SL_IN[i1]
                c, d = _SL_SH[i2]
                e, f = _SL_OUT[io]
                x1s = x1[:, a:b].reshape(E, m1, 2 * l1 + 1)
                x2s = x2[:, c:d].reshape(E, m2, 2 * l2 + 1)
                seg = jnp.einsum('uvw,ijk,eui,evj->ewk', weights[k], _W3J[k], x1s, x2s, optimize='optimal') * _NORM[k]
                out = out.at[:, e:f].add(seg.reshape(E, mo * (2 * lo + 1)))
            return out
        i, j = (edge_index[0], edge_index[1])
        summand = _tensor_product(x[i], edge_attr, [w0, w1, w2, w3, w4])
        out = jax.ops.segment_sum(summand, j, num_segments=x.shape[0])
        return out / float(np.sqrt(NUM_NEIGHBORS))
    edge_index = jnp.stack([src, dst])
    h = jnp.maximum(_layernorm(x, axis=-1), 0.0)
    x = x + _L0_gnn_ref(h, edge_weight, L0_gnn_Wq1, L0_gnn_bq1, L0_gnn_Wk1, L0_gnn_bk1, L0_gnn_Wv1, L0_gnn_bv1, L0_gnn_We1, L0_gnn_Ws1, L0_gnn_bs1, L0_gnn_Wq2, L0_gnn_bq2, L0_gnn_Wk2, L0_gnn_bk2, L0_gnn_Wv2, L0_gnn_bv2, L0_gnn_We2, L0_gnn_Ws2, L0_gnn_bs2, edge_index)
    h = jnp.maximum(_layernorm(x, axis=-1), 0.0)
    x = x + _L1_gnn_ref(h, edge_index, edge_attr_9, L1_gnn_w0, L1_gnn_w1, L1_gnn_w2, L1_gnn_w3, L1_gnn_w4)
    return x

_drawn_inputs = setup_inputs


def setup_inputs(seed=0):
    import zlib

    import numpy as np

    out = dict(_drawn_inputs(seed))
    spreads = {}
    factors = {'L0_gnn_Wq1': 5.799,
     'L0_gnn_bq1': 8.0,
     'L0_gnn_Wk1': 6.889,
     'L0_gnn_bk1': 8.0,
     'L0_gnn_Wq2': 5.497,
     'L0_gnn_bq2': 8.0,
     'L0_gnn_Wk2': 8.0,
     'L0_gnn_bk2': 8.0}
    for name, (base, spread) in spreads.items():
        noise = np.random.default_rng([zlib.crc32(name.encode()), seed]).standard_normal(out[name].shape)
        drawn = base * np.exp(spread * noise) if base else spread * noise
        out[name] = jnp.asarray(drawn.astype(out[name].dtype))
    for name, factor in factors.items():
        out[name] = (out[name] * factor).astype(out[name].dtype)
    return out
```

```python
from contextlib import ExitStack
from math import factorial

import numpy as np
import concourse.bass as bass
from concourse import mybir

ALU = mybir.AluOpType
ACT = mybir.ActivationFunctionType
AX = mybir.AxisListType
F32 = mybir.dt.float32
BF16 = mybir.dt.bfloat16
I32 = mybir.dt.int32

P = 128
D = 128
H = 4
CH = D // H
MUL = 32
T = 24
C = 3
NCH = T // C
QW = 136
OW = 136
MW = 352
NCOEF = 13
BIG = 1e38
KEY = 1e33
EPS = 1e-5
SCALE = float(1.0 / np.sqrt(np.float32(CH)))


def ceil_div(a, b):
    return (a + b - 1) // b


def sizes(n_nodes, n_edges):
    nb = ceil_div(n_nodes, P)
    nt = ceil_div(n_edges, P)
    groups = ceil_div(nt + nb - 1, T)
    groups += groups % 2
    return nb + nb % 2, nt, groups, ceil_div(groups * T, P)


def wigner_112():
    def ratio(a, b):
        return float(a) / float(b)

    def coeff(j1, m1, j2, m2, j3, m3):
        vmin = int(max(-j1 + j2 + m3, -j1 + m1, 0))
        vmax = int(min(j2 + j3 + m1, j3 - j1 + j2, j3 + m3))
        f = lambda n: factorial(round(n))
        c = ((2.0 * j3 + 1.0) * ratio(f(j3 + j1 - j2) * f(j3 - j1 + j2) * f(j1 + j2 - j3) * f(j3 + m3) * f(j3 - m3),
                                         f(j1 + j2 + j3 + 1) * f(j1 - m1) * f(j1 + m1) * f(j2 - m2) * f(j2 + m2))) ** 0.5
        s = 0
        for v in range(vmin, vmax + 1):
            s += (-1) ** (v + j2 + m2) * ratio(f(j2 + j3 + m1 - v) * f(j1 - m1 + v),
                                                  f(v) * f(j3 - j1 + j2 - v) * f(j3 + m3 - v) * f(v + j1 - j2 - m3))
        return float(c * s)

    def basis(l):
        q = np.zeros((2 * l + 1, 2 * l + 1), dtype=np.complex128)
        for m in range(-l, 0):
            q[l + m, l + abs(m)] = 1 / np.sqrt(2)
            q[l + m, l - abs(m)] = -1j / np.sqrt(2)
        q[l, l] = 1
        for m in range(1, l + 1):
            q[l + m, l + abs(m)] = (-1) ** m / np.sqrt(2)
            q[l + m, l - abs(m)] = 1j * (-1) ** m / np.sqrt(2)
        return (-1j) ** l * q

    c = np.zeros((3, 5, 3))
    for m1 in range(-1, 2):
        for m2 in range(-2, 3):
            if abs(m1 + m2) <= 1:
                c[1 + m1, 2 + m2, 1 + m1 + m2] = coeff(1, m1, 2, m2, 1, m1 + m2)
    r = np.real(np.einsum('ij,kl,mn,ikn->jlm', basis(1), basis(2), np.conj(basis(1).T), c.astype(np.complex128)))
    return r / np.linalg.norm(r)


def build(nc, x_p, src_t, dst_t, dlast, ew_t, attr_t, weights, out):
    n_rows = x_p.shape[0]
    n_nodes = weights["n_nodes"]
    n_edges = weights["n_edges"]
    NBE, NT, G, NBLK = sizes(n_nodes, n_edges)
    SP = NBLK * P
    assert n_rows == NBE * P and src_t.shape[0] == NT + 1 and G >= 6 and NBE >= 4

    def scratch(name, shape, dt):
        return nc.dram_tensor(name, shape, dt, kind="Internal").ap()

    idx_d = scratch("step_src", (P, SP), I32)
    dl_d = scratch("step_dloc", (P, SP), F32)
    ew_d = scratch("step_ew", (P, SP), F32)
    coef_d = scratch("step_coef", (P, SP, NCOEF), F32)
    brow_d = scratch("step_block", (3, SP), I32)
    kv_d = [scratch(f"kv{l}", (NBE * P, 2 * D), F32) for l in range(2)]
    skip_d = [scratch(f"skip{l}", (NBE * P, D), F32) for l in range(2)]
    h_d = scratch("h_planar", (NBE * P, D), F32)
    x1_d = scratch("x1", (NBE * P, D), F32)

    with ExitStack() as top:
        def sem(name):
            return top.enter_context(nc.semaphore(name))

        ident = top.enter_context(nc.sbuf_tensor("ident", [P, P], F32))
        ident_b = top.enter_context(nc.sbuf_tensor("ident_b", [P, P], BF16))
        iota_b = top.enter_context(nc.sbuf_tensor("iota_b", [P, P], BF16))
        iota_i = top.enter_context(nc.sbuf_tensor("iota_i", [P, P], I32))
        step_tables(nc, sem, locals())
        att = attention_sems(sem)
        with ExitStack() as mid:
            qtab = mid.enter_context(nc.sbuf_tensor("qtab", [P, NBE * QW], F32))
            otab = mid.enter_context(nc.sbuf_tensor("otab", [P, NBE * OW], F32))
            env = dict(locals())
            env["att"] = att
            node_phase(nc, sem, env, 0)
            attention_pass(nc, env, 0)
            node_phase(nc, sem, env, 1)
            attention_pass(nc, env, 1)
            node_phase(nc, sem, env, 2)
        with ExitStack() as mid:
            mtab = mid.enter_context(nc.sbuf_tensor("mtab", [P, NBE * MW], F32))
            env = dict(locals())
            message_pass(nc, sem, env)
            final_phase(nc, sem, env)



def step_tables(nc, sem, env):
    NT, NBLK, NBE, SP = env["NT"], env["NBLK"], env["NBE"], env["SP"]
    n_nodes = env["n_nodes"]
    nb = ceil_div(n_nodes, P)
    ident, ident_b, iota_b, iota_i = env["ident"], env["ident_b"], env["iota_b"], env["iota_i"]
    W3 = wigner_112()
    with ExitStack() as c:
        def sb(name, shape, dt=F32):
            return c.enter_context(nc.sbuf_tensor(name, shape, dt))

        last_i = sb("last_i", [P, NT], I32)
        tile_i = sb("tile_i", [P, NT], I32)
        step_i = sb("step_i", [P, NBLK], I32)
        last_m = sb("last_m", [P, NT], I32)
        last_b = sb("last_b", [P, NT], I32)
        last_f = sb("last_f", [P, NT])
        tile_f = sb("tile_f", [P, NT])
        end_f = sb("end_f", [P, NT])
        lt = sb("lt", [P, NT])
        step_f = sb("step_f", [P, NBLK])
        t_f = sb("t_f", [P, NBLK])
        t_i = sb("t_i", [P, NBLK], I32)
        b_f = sb("b_f", [P, NBLK])
        b_n = sb("b_n", [P, NBLK])
        b_s = sb("b_s", [P, 3, NBLK])
        b_rows = sb("b_rows", [NBLK, 3, P], I32)
        t_now = sb("t_now", [P, 1], I32)
        rows_s = sb("rows_s", [P, P], I32)
        rows_d = sb("rows_d", [P, P], I32)
        rows_w = sb("rows_w", [P, P])
        rows_a = sb("rows_a", [P, 9 * P])
        rows_sf = sb("rows_sf", [P, P])
        rows_df = sb("rows_df", [P, P])
        rows_dl = sb("rows_dl", [P, P])
        o_src = sb("o_src", [P, P], I32)
        o_dl = sb("o_dl", [P, P])
        o_w = sb("o_w", [P, P])
        o_at = sb("o_at", [P, 9, P])
        N_TWO = int(sum(np.sum(np.abs(W3[i, :, k]) > 1e-9) == 2 for i in range(3) for k in range(3)))
        second = sb("second", [P, N_TWO, P])
        tw = sem("pre_two")
        o_co = sb("o_co", [P, P, NCOEF])
        ps = [c.enter_context(nc.psum_tensor(f"pt{i}", [P, 4, P], F32)) for i in range(4)]

        consts = sem("pre_consts"); consts0 = sem("pre_consts0"); dl_in = sem("pre_last"); cd = sem("pre_calc")
        bt = sem("pre_bt"); br = sem("pre_br"); bout = sem("pre_bout"); tn = sem("pre_tnow")
        gat = sem("pre_gather"); rf = sem("pre_rowsf"); tr = sem("pre_tr"); ev = sem("pre_ev")
        atc = sem("pre_attr"); coz = sem("pre_coef"); st = sem("pre_store")
        block = c.enter_context(nc.Block())

        @block.gpsimd
        def _(pool):
            pool.memset(ident[:, :], 0.0).then_inc(consts0, 1)
            pool.iota(iota_i[:, :], pattern=[[1, P]], base=0, channel_multiplier=0).then_inc(consts, 1)
            pool.iota(tile_i[:, :], pattern=[[1, NT]], base=0, channel_multiplier=0).then_inc(consts, 1)
            pool.iota(step_i[:, :], pattern=[[P, NBLK]], base=0, channel_multiplier=1).then_inc(consts, 1)
            pool.wait_ge(consts0, 1)
            pool.affine_select(out=ident[:, :], in_=ident[:, :], compare_op=ALU.not_equal, fill=1.0, base=0,
                               pattern=[[-1, P]], channel_multiplier=1).then_inc(consts, 1)
            with pool.Fori(0, NBLK) as k:
                pool.wait_ge(tn, k + 1)
                pool.nop(nofuse=True)
                for buf, tab in ((rows_s, env["src_t"]), (rows_d, env["dst_t"]), (rows_w, env["ew_t"]),
                                 (rows_a, env["attr_t"])):
                    pool.indirect_dma_start(out=buf[:, :], out_offset=None, in_=tab,
                                            in_offset=bass.IndirectOffsetOnAxis(ap=t_now[:, 0:1], axis=0)).then_inc(gat, 16)

        @block.sync
        def _(sp):
            sp.dma_start(last_i[:, :], env["dlast"].partition_broadcast(P)).then_inc(dl_in, 16)
            sp.wait_ge(br, 3)
            sp.nop(nofuse=True)
            sp.dma_start(env["brow_d"].rearrange("w (k p) -> k w p", p=P), b_rows[:, :, :]).then_inc(bout, 16)
            with sp.Fori(0, NBLK) as k:
                sp.wait_ge(ev, 3 * k + 3)
                sp.nop(nofuse=True)
                cols = bass.ds(k * P, P)
                sp.dma_start(env["idx_d"][:, cols], o_src[:, :]).then_inc(st, 16)
                sp.dma_start(env["dl_d"][:, cols], o_dl[:, :]).then_inc(st, 16)
                sp.dma_start(env["ew_d"][:, cols], o_w[:, :]).then_inc(st, 16)
                sp.wait_ge(coz, NCOEF * (k + 1))
                sp.nop(nofuse=True)
                sp.dma_start(env["coef_d"][:, cols, :], o_co[:, :, :]).then_inc(st, 16)
            sp.wait_ge(bout, 16)
            sp.nop(nofuse=True)
            sp.wait_ge(st, 64 * NBLK)
            sp.nop(nofuse=True)

        @block.tensor
        def _(pe):
            pe.wait_ge(consts, 4)
            pe.wait_ge(cd, 14 + NBLK)
            for w in range(3):
                pe.transpose(ps[0][0:NBLK, w, :], b_s[:, w, :], ident[:, :]).then_inc(bt, 1)
            pe.wait_ge(br, 3)
            with pe.Fori(0, NBLK) as k:
                pe.wait_ge(rf, 3 * k + 3)
                pe.transpose(ps[0][:, 0, :], rows_sf[:, :], ident[:, :])
                pe.transpose(ps[0][:, 1, :], rows_dl[:, :], ident[:, :])
                pe.transpose(ps[0][:, 2, :], rows_w[:, :], ident[:, :])
                for a in range(9):
                    last = pe.transpose(ps[1 + a // 4][:, a % 4, :], rows_a[:, a * P:(a + 1) * P], ident[:, :])
                last.then_inc(tr, 1)

        @block.scalar
        def _(act):
            with act.Fori(0, NBLK) as k:
                act.wait_ge(tr, k + 1)
                act.activation(o_at[:, 0:4, :], ps[1][:, :, :], ACT.Copy).then_inc(atc, 1)
                act.activation(o_at[:, 4:8, :], ps[2][:, :, :], ACT.Copy).then_inc(atc, 1)
                act.activation(o_at[:, 8, :], ps[3][:, 0, :], ACT.Copy).then_inc(atc, 1)

        @block.vector
        def _(dve):
            n = [0]

            def link(ins):
                n[0] += 1
                ins.then_inc(cd, 1)
                dve.wait_ge(cd, n[0])

            dve.wait_ge(consts, 4)
            link(dve.tensor_copy(iota_b[:, :], iota_i[:, :]))
            link(dve.tensor_copy(ident_b[:, :], ident[:, :]))
            link(dve.tensor_copy(tile_f[:, :], tile_i[:, :]))
            link(dve.tensor_copy(step_f[:, :], step_i[:, :]))
            dve.wait_ge(dl_in, 16)
            link(dve.tensor_scalar(last_m[:, :], last_i[:, :], float(n_nodes - 1), None, ALU.min))
            link(dve.tensor_scalar(last_b[:, :], last_m[:, :], 7, None, ALU.arith_shift_right))
            link(dve.tensor_copy(last_f[:, :], last_b[:, :]))
            link(dve.tensor_tensor(end_f[:, :], last_f[:, :], tile_f[:, :], ALU.add))
            for k in range(NBLK):
                link(dve.tensor_scalar(lt[:, :], end_f[:, :], step_f[:, k:k + 1], 0.0, ALU.is_lt, ALU.add,
                                       accum_out=t_f[:, k:k + 1]))
            link(dve.tensor_copy(t_i[:, :], t_f[:, :]))
            link(dve.tensor_tensor(b_f[:, :], step_f[:, :], t_f[:, :], ALU.subtract))
            link(dve.tensor_scalar(b_n[:, :], b_f[:, :], float(nb - 1), None, ALU.min))
            for w, width in enumerate((QW, OW, MW)):
                link(dve.tensor_scalar(b_s[:, w, :], b_n[:, :], float(width), None, ALU.mult))
            dve.wait_ge(bt, 3)
            for w in range(3):
                dve.tensor_copy(b_rows[:, w, :], ps[0][0:NBLK, w, :]).then_inc(br, 1)

            with dve.Fori(0, NBLK) as k:
                dve.tensor_copy(t_now[:, :], t_i[:, bass.ds(k, 1)]).then_inc(tn, 1)
                dve.wait_ge(gat, 64 * k + 64)
                dve.tensor_copy(rows_sf[:, :], rows_s[:, :]).then_inc(rf, 1)
                dve.tensor_copy(rows_df[:, :], rows_d[:, :]).then_inc(rf, 1)
                dve.wait_ge(rf, 3 * k + 2)
                dve.scalar_tensor_tensor(out=rows_dl[:, :], in0=b_n[:, bass.ds(k, 1)].to_broadcast((P, P)), scalar=-float(P),
                                         in1=rows_df[:, :], op0=ALU.mult, op1=ALU.add).then_inc(rf, 1)
                dve.wait_ge(tr, k + 1)
                dve.tensor_copy(o_src[:, :], ps[0][:, 0, :]).then_inc(ev, 1)
                dve.tensor_copy(o_dl[:, :], ps[0][:, 1, :]).then_inc(ev, 1)
                dve.tensor_copy(o_w[:, :], ps[0][:, 2, :]).then_inc(ev, 1)
                dve.wait_ge(atc, 3 * k + 3)
                two = 0
                for kk in range(3):
                    for i in range(3):
                        terms = [(j, float(W3[i, j, kk])) for j in range(5) if abs(W3[i, j, kk]) > 1e-9]
                        at = o_co[:, :, 3 * kk + i]
                        j, w = terms[0]
                        if len(terms) == 1:
                            dve.tensor_scalar(at, o_at[:, 4 + j, :], w, None, ALU.mult).then_inc(coz, 1)
                        else:
                            (j2, w2), = terms[1:]
                            dve.tensor_scalar(second[:, two, :], o_at[:, 4 + j2, :], w2, None, ALU.mult).then_inc(tw, 1)
                            two += 1
                            dve.wait_ge(tw, N_TWO * k + two)
                            dve.scalar_tensor_tensor(out=at, in0=o_at[:, 4 + j, :], scalar=w, in1=second[:, two - 1, :],
                                                     op0=ALU.mult, op1=ALU.add).then_inc(coz, 1)
                for i in range(3):
                    dve.tensor_copy(o_co[:, :, 9 + i], o_at[:, 1 + i, :]).then_inc(coz, 1)
                dve.tensor_copy(o_co[:, :, 12], o_at[:, 0, :]).then_inc(coz, 1)
                dve.wait_ge(st, 64 * k + 64)



def node_phase(nc, sem, env, kind):
    NBE = env["NBE"]
    ident = env["ident"]
    qtab, otab = env["qtab"], env["otab"]
    W = env["weights"]
    name = f"n{kind}_"
    with ExitStack() as c:
        def sb(nm, shape, dt=F32):
            return c.enter_context(nc.sbuf_tensor(name + nm, shape, dt))

        w4 = sb("w4", [P, 4 * D])
        bias = sb("bias", [P, 4 * D])
        we_q = sb("we_q", [P, D])
        we_o = sb("we_o", [P, D])
        xin = sb("xin", [P, 2, D])
        sin = sb("sin", [P, 2, D])
        hin = sb("hin", [P, 2, D])
        x1 = sb("x1", [P, 2, D])
        den = sb("den", [P, 2, H])
        rec = sb("rec", [P, 2, H])
        pwr = sb("pwr", [P, 2, H])
        t1 = sb("t1", [P, 2, D])
        t2 = sb("t2", [P, 2, D])
        stat = sb("stat", [P, 2, 6])
        mv = sb("mv", [P, 2, 2])
        sd = sb("sd", [P, 2, 1])
        rs = sb("rs", [P, 2, 1])
        xn = sb("xn", [P, 2, D])
        hT = sb("hT", [P, 2, D])
        kvs = sb("kvs", [P, 2, 3 * D])
        qe = sb("qe", [P, 2, D])
        hp = sb("hp", [P, 2, D])
        eps = sb("eps", [P, 1])
        pT = c.enter_context(nc.psum_tensor(name + "pT", [P, 2, 512], F32))
        pp = c.enter_context(nc.psum_tensor(name + "pp", [P, 2, 512], F32))

        wl = sem(name + "weights"); xl = [sem(name + f"x{q}") for q in range(2)]
        ch = sem(name + "dve"); sq = sem(name + "sqrt"); xs = sem(name + "xn"); tt = sem(name + "tr")
        hs = sem(name + "hT"); mm = sem(name + "proj"); kd = sem(name + "kvs"); qd = sem(name + "q")
        st = [sem(name + f"st{q}") for q in range(2)]
        ez = sem(name + "eps")
        qq = sem(name + "qe")
        pre = {0: 0, 1: 6, 2: 8}[kind]
        nv = pre + 2
        per = {0: 3, 1: 6, 2: 11}[kind]

        loads = {0: 1, 1: 1, 2: 2}[kind]
        stores = {0: 2, 1: 2, 2: 2}[kind]
        block = c.enter_context(nc.Block())
        NP = NBE // 2

        def src_rows(ap, b):
            return ap[bass.ds(b * P, P), :]

        @block.sync
        def _(sp):
            nw = 0
            if kind < 2:
                l = kind + 1
                for i, k in enumerate(("q", "k", "v", "s")):
                    sp.dma_start(w4[:, i * D:(i + 1) * D], W[f"W{k}{l}"]).then_inc(wl, 16)
                    sp.dma_start(bias[:, i * D:(i + 1) * D],
                                 W[f"b{k}{l}"].rearrange("(a n) -> a n", a=1).partition_broadcast(P)).then_inc(wl, 16)
                    nw += 2
                sp.dma_start(we_q[:, :], W[f"We{l}"].partition_broadcast(P)).then_inc(wl, 16)
                nw += 1
            if kind > 0:
                sp.dma_start(we_o[:, :], W[f"We{kind}"].partition_broadcast(P)).then_inc(wl, 16)
                nw += 1

            def load(m, q, first):
                b = 2 * m + q
                if not first:
                    sp.wait_ge(xs, b - 1)
                    sp.nop(nofuse=True)
                if kind == 0:
                    sp.dma_start(xin[:, q, :], src_rows(env["x_p"], b)).then_inc(xl[q], 16)
                else:
                    sp.dma_start(sin[:, q, :], src_rows(env["skip_d"][kind - 1], b)).then_inc(xl[q], 16)
                if kind == 2:
                    sp.dma_start(xin[:, q, :], src_rows(env["x_p"], b)).then_inc(xl[q], 16)

            for q in range(2):
                load(0, q, True)
            with sp.Fori(1, NP) as m:
                for q in range(2):
                    load(m, q, False)

        @block.tensor
        def _(pe):
            if kind == 2:
                return

            def body(m, q, first):
                b = 2 * m + q
                pe.wait_ge(xs, b + 1)
                if not first:
                    pe.wait_ge(hs, b - 1)
                pe.transpose(pT[:, q, 0:D], xn[:, q, :] if kind == 0 else hin[:, q, :], ident[:, :]).then_inc(tt, 1)
                pe.wait_ge(hs, b + 1)
                if not first:
                    pe.wait_ge(qd, b - 1)
                pe.matmul(pp[:, q, :], hT[:, q, :], w4[:, :], start=True, stop=True).then_inc(mm, 1)

            pe.wait_ge(wl, 16 * (10 if kind else 9))
            body(0, 0, True)
            body(0, 1, True)
            with pe.Fori(1, NP) as m:
                body(m, 0, False)
                body(m, 1, False)

        @block.scalar
        def _(act):
            act.wait_ge(ez, 1)

            def body(m, q, first):
                b = 2 * m + q
                if kind != 1:
                    act.wait_ge(ch, per * b + nv)
                    act.activation(sd[:, q, :], mv[:, q, 1:2], ACT.Sqrt, bias=eps[:, 0:1]).then_inc(sq, 1)
                if kind < 2:
                    act.wait_ge(tt, b + 1)
                    if not first:
                        act.wait_ge(mm, b - 1)
                    act.activation(hT[:, q, :], pT[:, q, 0:D], ACT.Relu if kind == 0 else ACT.Copy).then_inc(hs, 1)

            body(0, 0, True)
            body(0, 1, True)
            with act.Fori(1, NP) as m:
                body(m, 0, False)
                body(m, 1, False)

        @block.gpsimd
        def _(pool):
            def body(m, q):
                b = 2 * m + q
                pool.wait_ge(kd, b + 1)
                pool.nop(nofuse=True)
                if kind < 2:
                    pool.dma_start(src_rows(env["kv_d"][kind], b), kvs[:, q, 0:2 * D]).then_inc(st[q], 16)
                    pool.dma_start(src_rows(env["skip_d"][kind], b), kvs[:, q, 2 * D:3 * D]).then_inc(st[q], 16)
                else:
                    pool.dma_start(src_rows(env["h_d"], b), hp[:, q, :]).then_inc(st[q], 16)
                    pool.dma_start(src_rows(env["x1_d"], b), x1[:, q, :]).then_inc(st[q], 16)

            with pool.Fori(0, NP) as m:
                body(m, 0)
                body(m, 1)
            for q in range(2):
                pool.wait_ge(st[q], 32 * NP)

        @block.vector
        def _(dve):
            dve.memset(eps[:, :], EPS).then_inc(ez, 1)
            dve.wait_ge(wl, 16 * {0: 9, 1: 10, 2: 1}[kind])

            def body(m, q, first):
                b = 2 * m + q
                n = [0]

                def link(ins):
                    n[0] += 1
                    ins.then_inc(ch, 1)
                    dve.wait_ge(ch, per * b + n[0])

                dve.wait_ge(xl[q], 16 * loads * (m + 1))
                x = xin[:, q, :]
                if kind > 0:
                    ob = otab[:, bass.ds(b * OW, OW)]
                    link(dve.tensor_scalar(den[:, q, :], otab[:, bass.ds(b * OW + D, H)], 1e-30, None, ALU.max))
                    link(dve.reciprocal(rec[:, q, :], den[:, q, :]))
                    link(dve.tensor_tensor(pwr[:, q, :], otab[:, bass.ds(b * OW + D + H, H)], rec[:, q, :], ALU.mult))
                    r4 = rec[:, q, :].unsqueeze(2).to_broadcast((P, H, CH))
                    p4 = pwr[:, q, :].unsqueeze(2).to_broadcast((P, H, CH))
                    link(dve.tensor_tensor(t1[:, q, :].rearrange("p (h c) -> p h c", h=H),
                                           otab[:, bass.ds(b * OW, D)].rearrange("p (h c) -> p h c", h=H), r4, ALU.mult))
                    link(dve.tensor_tensor(t2[:, q, :].rearrange("p (h c) -> p h c", h=H),
                                           we_o[:, :].rearrange("p (h c) -> p h c", h=H), p4, ALU.mult))
                    link(dve.tensor_tensor(t1[:, q, :], t1[:, q, :], t2[:, q, :], ALU.add))
                    if kind == 1:
                        if not first:
                            dve.wait_ge(tt, b - 1)
                        dve.tensor_tensor(hin[:, q, :], t1[:, q, :], sin[:, q, :], ALU.add).then_inc(xs, 1)
                    else:
                        if not first:
                            dve.wait_ge(st[q], 32 * m)
                        link(dve.tensor_tensor(t1[:, q, :], t1[:, q, :], sin[:, q, :], ALU.add))
                        link(dve.tensor_tensor(x1[:, q, :], t1[:, q, :], xin[:, q, :], ALU.add))
                        x = x1[:, q, :]
                if kind != 1:
                    link(dve.bn_stats(stat[:, q, :], x))
                    dve.nop(nofuse=True)
                    link(dve.bn_aggr(mv[:, q, :], stat[:, q, :]))
                    dve.wait_ge(sq, b + 1)
                    link(dve.reciprocal(rs[:, q, :], sd[:, q, :]))
                    if kind == 0 and not first:
                        dve.wait_ge(tt, b - 1)
                    dve.tensor_scalar(xn[:, q, :], x, mv[:, q, 0:1], rs[:, q, 0:1], ALU.subtract, ALU.mult).then_inc(xs, 1)
                if kind == 2:
                    dve.wait_ge(xs, b + 1)
                    dve.tensor_scalar(hp[:, q, 0:MUL], xn[:, q, 0:MUL], 0.0, None, ALU.max)
                    dve.tensor_scalar(hp[:, q, MUL:D].rearrange("p (i u) -> p i u", i=3),
                                      xn[:, q, MUL:D].rearrange("p (u i) -> p i u", i=3), 0.0, None,
                                      ALU.max).then_inc(kd, 1)
                else:
                    dve.wait_ge(mm, b + 1)
                    if not first:
                        dve.wait_ge(st[q], 32 * m)
                    dve.tensor_tensor(kvs[:, q, :], pp[:, q, D:4 * D], bias[:, D:4 * D], ALU.add).then_inc(kd, 1)
                    qb = qtab[:, bass.ds(b * QW, D)]
                    dve.tensor_tensor(qb, pp[:, q, 0:D], bias[:, 0:D], ALU.add).then_inc(qd, 1)
                    dve.wait_ge(qd, b + 1)
                    dve.tensor_tensor(qe[:, q, :], qb, we_q[:, :], ALU.mult).then_inc(qq, 1)
                    dve.wait_ge(qq, b + 1)
                    dve.tensor_reduce(qtab[:, bass.ds(b * QW + D, H)],
                                      qe[:, q, :].rearrange("p (h c) -> p h c", h=H), AX.X, ALU.add)
            body(0, 0, True)
            body(0, 1, True)
            with dve.Fori(1, NP) as m:
                body(m, 0, False)
                body(m, 1, False)
            if kind < 2:
                dve.memset(otab[:, :], 0.0)



def attention_sems(sem):
    names = ("oh", "ohT", "ohTc", "qmm", "prod", "qwe", "red", "al1", "alpha", "d4", "aT", "dTs", "pen", "scan1",
             "rowsT", "rw", "rowv", "cr", "fe", "fac", "cols", "cin", "scan2", "mx", "mT", "da", "p", "pp", "pw",
             "ohf", "vp", "vals", "agg", "oadd", "facps", "facn", "resc", "init")
    s = {k: sem("a_" + k) for k in names}
    for k in ("idx", "dl", "bA", "w", "bB"):
        s["ld_" + k] = [sem(f"a_ld_{k}{q}") for q in range(2)]
    s["kv"] = [[sem(f"a_kv{q}_{c}") for c in range(NCH)] for q in range(2)]
    return s


def attention_pass(nc, env, L):
    G, SP = env["G"], env["SP"]
    ident, ident_b, iota_b = env["ident"], env["ident_b"], env["iota_b"]
    qtab, otab = env["qtab"], env["otab"]
    S = env["att"]
    kv_d = env["kv_d"][L]
    name = f"e{L}_"
    R4 = H * T
    NR = 9
    with ExitStack() as c:
        def sb(nm, shape, dt=F32):
            return c.enter_context(nc.sbuf_tensor(name + nm, shape, dt))

        def psum(nm, shape, dt=F32):
            return c.enter_context(nc.psum_tensor(name + nm, shape, dt))

        kv = sb("kv", [P, 2 * T, 2 * D])
        idx = sb("idx", [P, 2 * T], I32)
        dl = sb("dl", [P, 2, T])
        wq = sb("wq", [P, 2, T])
        bA = sb("bA", [1, 2 * T], I32)
        bB = sb("bB", [1, 2 * T], I32)
        oh = sb("oh", [P, 2 * T, P], BF16)
        ohT = sb("ohT", [P, 2, C, P])
        ohf = sb("ohf", [P, 2, C, P])
        vals = sb("vals", [P, 2, C, OW])
        prod = sb("prod", [P, C, D])
        alpha = sb("alpha", [P, 2, H, T])
        qw = sb("qw", [P, 2, H, T])
        tmp = sb("tmp", [P, H, T])
        d4 = sb("d4", [P, H, T])
        pp = sb("pp", [P, 2, T, 2 * H])
        dTs = sb("dTs", [R4, P])
        pen = sb("pen", [R4, P + 1])
        f1 = sb("f1", [R4, P])
        b1 = sb("b1", [R4, P])
        cin = sb("cin", [R4, 2])
        mx = sb("mx", [R4, P])
        rw = sb("rw", [1, 4, H, T])
        fx = sb("fx", [1, H, T + 1])
        lx = sb("lx", [1, H, T + 1])
        dlx = sb("dlx", [1, T + 1])
        pc = sb("pc", [1, T])
        ne = sb("ne", [1, T])
        pw = sb("pw", [1, T])
        pwx = sb("pwx", [1, H, T + 1])
        qbx = sb("qbx", [1, H, T])
        bf = sb("bf", [1, H, T])
        cr = sb("cr", [1, 2, H, T])
        dm = sb("dm", [1, H])
        cf = sb("cf", [1, 1])
        fe = sb("fe", [1, H])
        fac = sb("fac", [1, H])
        facn = sb("facn", [P, H])
        one = sb("one", [1, 1])

        ohT_ps = psum("ohT_ps", [P, 2, 1024], BF16)
        q_ps = psum("q_ps", [P, 2, 512])
        agg = psum("agg", [P, 2, 512])
        turn = psum("turn", [P, 512])
        small = psum("small", [P, 512])
        p2 = small[:, 0:R4].rearrange("p (h t) -> p h t", h=H)
        fac_ps = small[:, R4:R4 + H]
        col_ps = small[0:R4, R4 + H:R4 + H + 2]
        row_ps = small[0:1, R4 + H + 2:R4 + H + 2 + 4 * R4]
        aT_ps = turn[0:R4, 0:P]
        dT_ps = turn[0:R4, P:2 * P]
        mT_ps = turn[:, 2 * P:2 * P + R4]

        def done(m, q, per, k):
            return (2 * m + q) * per + (L * G * per + k)

        def nth(m, n):
            return m * n + (L * (G // 2) * n + n)

        def prev(m, q, by=1):
            return (m, q - by) if q - by >= 0 else (m - 1, q - by + 2)

        block = c.enter_context(nc.Block())

        def drive(a_part, b_part, order):
            order(0, 0, True, False, 0)
            order(0, 1, True, True, 1)

        def schedule(eng, iteration):
            iteration(0, 0, True, False, 0)
            iteration(0, 1, True, True, 1)
            with eng.Fori(1, G // 2) as m:
                iteration(m, 0, True, True, 2)
                iteration(m, 1, True, True, 2)
            iteration(G // 2, 0, False, True, 2)

        @block.sync
        def _(sp):
            def load(which, dst, src, m, q):
                sp.dma_start(dst, src).then_inc(S["ld_" + which][q], 16)

            def cols(m, q):
                return bass.ds((2 * m + q) * T, T)

            def first_loads(m, q):
                load("idx", idx[:, q * T:(q + 1) * T], env["idx_d"][:, cols(m, q)], m, q)
                load("dl", dl[:, q, :], env["dl_d"][:, cols(m, q)], m, q)
                load("bA", bA[:, q * T:(q + 1) * T], env["brow_d"][0:1, cols(m, q)], m, q)

            first_loads(0, 0)
            first_loads(0, 1)

            def iteration(m, q, a, b, n):
                if not a:
                    return
                if n >= 1:
                    pm, pq = prev(m, q)
                    nm, nq = (m, 1) if q == 0 else (m + 1, 0)
                    sp.wait_ge(S["prod"], done(pm, pq, NCH, NCH))
                    sp.nop(nofuse=True)
                    sp.wait_ge(S["d4"], done(pm, pq, 1, 1))
                    sp.nop(nofuse=True)
                    first_loads(nm, nq)
                if n == 2:
                    pm, pq = prev(m, q, 2)
                    sp.wait_ge(S["pw"], done(pm, pq, 1, 1))
                    sp.nop(nofuse=True)
                    sp.wait_ge(S["oadd"], done(pm, pq, T, T))
                    sp.nop(nofuse=True)
                load("w", wq[:, q, :], env["ew_d"][:, cols(m, q)], m, q)
                load("bB", bB[:, q * T:(q + 1) * T], env["brow_d"][1:2, cols(m, q)], m, q)

            iteration(0, 0, True, False, 0)
            iteration(0, 1, True, True, 1)
            with sp.Fori(1, G // 2 - 1) as m:
                iteration(m, 0, True, True, 2)
                iteration(m, 1, True, True, 2)
            m = G // 2 - 1
            iteration(m, 0, True, True, 2)
            pm, pq = prev(m, 1, 2)
            sp.wait_ge(S["pw"], done(pm, pq, 1, 1))
            sp.nop(nofuse=True)
            sp.wait_ge(S["oadd"], done(pm, pq, T, T))
            sp.nop(nofuse=True)
            load("w", wq[:, 1, :], env["ew_d"][:, cols(m, 1)], m, 1)
            load("bB", bB[:, T:2 * T], env["brow_d"][1:2, cols(m, 1)], m, 1)

        @block.gpsimd
        def _(pool):
            def gathers(m, q, first):
                for ch in range(NCH):
                    if not first:
                        pm, pq = prev(m, q, 2)
                        pool.wait_ge(S["vals"], done(pm, pq, NCH, ch + 1))
                    if ch == 0:
                        pool.wait_ge(S["ld_idx"][q], nth(m, 16))
                    pool.nop(nofuse=True)
                    for r in range(C):
                        s = q * T + ch * C + r
                        pool.indirect_dma_start(
                            out=kv[:, s, :], out_offset=None, in_=kv_d,
                            in_offset=bass.IndirectOffsetOnAxis(ap=idx[:, s:s + 1], axis=0)).then_inc(S["kv"][q][ch], 16)

            gathers(0, 0, True)
            gathers(0, 1, True)
            with pool.Fori(1, G // 2) as m:
                gathers(m, 0, False)
                gathers(m, 1, False)

        @block.tensor
        def _(pe):
            def turn_onehot(m, q, ch):
                pe.wait_ge(S["oh"], done(m, q, NCH, ch + 1))
                cm, cq = (m, q) if ch >= 2 else prev(m, q)
                if not (isinstance(m, int) and m == 0 and q == 0 and ch < 2):
                    pe.wait_ge(S["ohTc"], done(cm, cq, NCH, (ch - 2) % NCH + 1))
                for r in range(C):
                    last = pe.transpose(ohT_ps[:, ch % 2, r * P:(r + 1) * P], oh[:, q * T + ch * C + r, :], ident_b[:, :])
                last.then_inc(S["ohT"], 1)

            def q_rows(m, q, ch):
                if ch == 0:
                    pe.wait_ge(S["ld_bA"][q], nth(m, 16))
                    pe.nop(nofuse=True)
                colr = [pe.value_load(bA[0:1, q * T + s:q * T + s + 1], min_val=0, max_val=(env["NBE"] - 1) * QW)
                        for s in range(ch * C, ch * C + C)]
                cm, cq = (m, q) if ch >= 2 else prev(m, q)
                pe.wait_ge(S["ohTc"], done(m, q, NCH, ch + 1))
                if not (isinstance(m, int) and m == 0 and q == 0 and ch < 2):
                    pe.wait_ge(S["prod"], done(cm, cq, NCH, (ch - 2) % NCH + 1))
                    pe.wait_ge(S["qwe"], done(cm, cq, NCH, (ch - 2) % NCH + 1))
                for r in range(C):
                    s = ch * C + r
                    col = colr[r]
                    last = pe.matmul(q_ps[:, ch % 2, r * QW:r * QW + D + H], ohT[:, ch % 2, r, :],
                                     qtab[:, bass.ds(col, D + H)], start=True, stop=True)
                last.then_inc(S["qmm"], 1)

            def sums(m, q, ch):
                cm, cq = (m, q) if ch >= 2 else prev(m, q)
                pe.wait_ge(S["ohf"], done(m, q, NCH, ch + 1))
                pe.wait_ge(S["vp"], done(m, q, NCH, ch + 1))
                pe.wait_ge(S["vals"], done(m, q, NCH, ch + 1))
                if not (isinstance(m, int) and m == 0 and q == 0 and ch < 2):
                    pe.wait_ge(S["oadd"], done(cm, cq, T, ((ch - 2) % NCH + 1) * C))
                for r in range(C):
                    last = pe.matmul(agg[:, ch % 2, r * OW:(r + 1) * OW], ohf[:, ch % 2, r, :],
                                     vals[:, ch % 2, r, :], start=True, stop=True)
                last.then_inc(S["agg"], 1)

            def iteration(m, q, a, b, n):
                hm, hq = prev(m, q)
                if n == 0:
                    turn_onehot(m, q, 0)
                for ch in range(NCH):
                    if b and ch == 0:
                        pe.wait_ge(S["alpha"], done(hm, hq, 1, 1))
                        pe.wait_ge(S["d4"], done(hm, hq, 1, 1))
                        pe.transpose(aT_ps, alpha[:, hq, :, :].rearrange("p h t -> p (h t)"), ident[:, :])
                        pe.transpose(dT_ps, d4[:, :, :].rearrange("p h t -> p (h t)"), ident[:, :]).then_inc(S["aT"], 1)
                    if b and ch == 1:
                        pe.wait_ge(S["scan1"], done(hm, hq, 2, 2))
                        for j, col in enumerate((f1[:, P - 1:P], b1[:, 0:1], dTs[:, 0:1], dTs[:, P - 1:P])):
                            last = pe.transpose(row_ps[0:1, j * R4:(j + 1) * R4], col, ident[0:R4, 0:R4])
                        last.then_inc(S["rowsT"], 1)
                    if b and ch == 2:
                        pe.wait_ge(S["cr"], done(hm, hq, 2, 2))
                        for j in range(2):
                            last = pe.matmul(col_ps[:, j:j + 1], cr[0:1, j, :, :].rearrange("p h t -> p (h t)"), one[0:1, 0:1],
                                             start=True, stop=True)
                        last.then_inc(S["cols"], 1)
                    if b and ch == 3:
                        pe.wait_ge(S["mx"], done(hm, hq, 1, 1))
                        pe.transpose(mT_ps, mx[:, :], ident[0:R4, 0:R4]).then_inc(S["mT"], 1)
                    if a and ch + 1 < NCH:
                        turn_onehot(m, q, ch + 1)
                    elif a:
                        nm, nq = (m, 1) if q == 0 else (m + 1, 0)
                        last_group = isinstance(m, int) and 2 * m + q == G - 1
                        if not last_group:
                            turn_onehot(nm, nq, 0)
                    if a:
                        q_rows(m, q, ch)
                    if b and ch >= 4:
                        u = 2 * (ch - 4)
                        if u == 0:
                            pe.wait_ge(S["ohf"], done(hm, hq, NCH, 1))
                            pe.wait_ge(S["fac"], done(hm, hq, 1, 1))
                            pe.wait_ge(S["p"], done(hm, hq, 1, 1))
                            pe.matmul(fac_ps, ohf[0:1, 0, 0, :], fac[0:1, :], start=True, stop=True).then_inc(S["facps"], 1)
                        sums(hm, hq, u)
                        sums(hm, hq, u + 1)

            iteration(0, 0, True, False, 0)
            iteration(0, 1, True, True, 1)
            with pe.Fori(1, G // 2 - 1) as m:
                iteration(m, 0, True, True, 2)
                iteration(m, 1, True, True, 2)
            iteration(G // 2 - 1, 0, True, True, 2)
            iteration(G // 2 - 1, 1, True, True, 2)
            iteration(G // 2, 0, False, True, 2)

        @block.scalar
        def _(act):
            def copy_ohT(m, q, ch):
                cm, cq = (m, q) if ch >= 2 else prev(m, q)
                act.wait_ge(S["ohT"], done(m, q, NCH, ch + 1))
                if not (isinstance(m, int) and m == 0 and q == 0 and ch < 2):
                    act.wait_ge(S["qmm"], done(cm, cq, NCH, (ch - 2) % NCH + 1))
                act.activation(ohT[:, ch % 2, :, :].rearrange("p r n -> p (r n)"), ohT_ps[:, ch % 2, 0:C * P],
                               ACT.Copy).then_inc(S["ohTc"], 1)

            def iteration(m, q, a, b, n):
                hm, hq = prev(m, q)
                if n == 0:
                    copy_ohT(m, q, 0)
                for ch in range(NCH):
                    if b and ch == 0:
                        act.wait_ge(S["aT"], done(hm, hq, 1, 1))
                        act.activation(dTs[:, :], dT_ps, ACT.Copy, scale=KEY).then_inc(S["dTs"], 1)
                    if b and ch == 1:
                        act.wait_ge(S["rowsT"], done(hm, hq, 1, 1))
                        act.activation(rw[0:1, :, :, :].rearrange("p k h t -> p (k h t)"), row_ps[0:1, 0:4 * R4],
                                       ACT.Copy).then_inc(S["rw"], 1)
                    if b and ch == 2:
                        act.wait_ge(S["cols"], done(hm, hq, 1, 1))
                        act.activation(cin[:, :], col_ps, ACT.Copy).then_inc(S["cin"], 1)
                        act.wait_ge(S["rowv"], done(hm, hq, NR, 8))
                        act.activation(fe[0:1, :], dm[0:1, :], ACT.Exp, scale=SCALE).then_inc(S["fe"], 1)
                    if a and ch + 1 < NCH:
                        copy_ohT(m, q, ch + 1)
                    elif a:
                        nm, nq = (m, 1) if q == 0 else (m + 1, 0)
                        if not (isinstance(m, int) and 2 * m + q == G - 1):
                            copy_ohT(nm, nq, 0)
                    if a:
                        if ch == 0 and n == 2:
                            pm, pq = prev(m, q, 2)
                            act.wait_ge(S["alpha"], done(pm, pq, 1, 1))
                        act.wait_ge(S["prod"], done(m, q, NCH, ch + 1))
                        act.activation(qw[:, q, :, ch * C:(ch + 1) * C].rearrange("p h r -> p r h"),
                                       q_ps[:, ch % 2, 0:C * QW].rearrange("p (r w) -> p r w", w=QW)[:, :, D:D + H],
                                       ACT.Copy).then_inc(S["qwe"], 1)
                    if b and ch == 3:
                        act.wait_ge(S["da"], done(hm, hq, 1, 1))
                        act.activation(p2, tmp[:, :, :], ACT.Exp, scale=SCALE).then_inc(S["p"], 1)
                        act.activation(pp[:, hq, :, 0:H].rearrange("p t h -> p h t"), tmp[:, :, :], ACT.Exp,
                                       scale=SCALE).then_inc(S["pp"], 1)
                    if b and ch >= 4:
                        for u in (2 * (ch - 4), 2 * (ch - 4) + 1):
                            cm, cq = (hm, hq) if u >= 2 else prev(hm, hq)
                            first = (n == 1) and u < 2
                            if not first:
                                act.wait_ge(S["agg"], done(cm, cq, NCH, (u - 2) % NCH + 1))
                            act.activation(ohf[:, u % 2, :, :], oh[:, hq * T + u * C:hq * T + (u + 1) * C, :],
                                           ACT.Copy).then_inc(S["ohf"], 1)
                            if u == 0:
                                act.wait_ge(S["pw"], done(hm, hq, 1, 1))
                            act.activation(vals[:, u % 2, :, D:OW], pp[:, hq, u * C:(u + 1) * C, :],
                                           ACT.Copy).then_inc(S["vp"], 1)

            iteration(0, 0, True, False, 0)
            iteration(0, 1, True, True, 1)
            with act.Fori(1, G // 2 - 1) as m:
                iteration(m, 0, True, True, 2)
                iteration(m, 1, True, True, 2)
            iteration(G // 2 - 1, 0, True, True, 2)
            iteration(G // 2 - 1, 1, True, True, 2)
            iteration(G // 2, 0, False, True, 2)

        @block.vector
        def _(dve):
            def onehots(m, q, ch, n):
                if ch == 0:
                    dve.wait_ge(S["ld_dl"][q], nth(m, 16))
                if n == 2:
                    pm, pq = prev(m, q, 2)
                    dve.wait_ge(S["ohf"], done(pm, pq, NCH, ch + 1))
                for r in range(C):
                    s = ch * C + r
                    last = dve.tensor_scalar(oh[:, q * T + s, :], iota_b[:, :], dl[:, q, s:s + 1], None, ALU.is_equal)
                last.then_inc(S["oh"], 1)

            def onehots_ahead(m, q, ch, n):
                if ch + 2 < NCH:
                    onehots(m, q, ch + 2, n)
                elif not (isinstance(m, int) and 2 * m + q == G - 1):
                    nm, nq = (m, 1) if q == 0 else (m + 1, 0)
                    onehots(nm, nq, ch + 2 - NCH, 2 if n >= 1 else n)

            def products(m, q, ch):
                if not (isinstance(m, int) and m == 0 and q == 0 and ch == 0):
                    cm, cq = (m, q) if ch else prev(m, q)
                    dve.wait_ge(S["red"], done(cm, cq, NCH, (ch - 1) % NCH + 1))
                dve.wait_ge(S["kv"][q][ch], nth(m, 16 * C))
                dve.wait_ge(S["qmm"], done(m, q, NCH, ch + 1))
                s = q * T + ch * C
                dve.tensor_tensor(prod[:, :, :], kv[:, s:s + C, 0:D],
                                  q_ps[:, ch % 2, 0:C * QW].rearrange("p (r w) -> p r w", w=QW)[:, :, 0:D],
                                  ALU.mult).then_inc(S["prod"], 1)

            def reduces(m, q, ch):
                dve.wait_ge(S["prod"], done(m, q, NCH, ch + 1))
                dve.tensor_reduce(alpha[:, q, :, ch * C:(ch + 1) * C].rearrange("p h r -> p r h"),
                                  prod[:, :, :].rearrange("p r (h c) -> p r h c", h=H), AX.X, ALU.add).then_inc(S["red"], 1)

            def weighted(m, q, ch):
                cm, cq = (m, q) if ch >= 2 else prev(m, q)
                if not (isinstance(m, int) and m == 0 and q == 0 and ch < 2):
                    dve.wait_ge(S["agg"], done(cm, cq, NCH, (ch - 2) % NCH + 1))
                s = q * T + ch * C
                pb = p2[:, :, ch * C:(ch + 1) * C].rearrange("p h r -> p r h").unsqueeze(3).to_broadcast((P, C, H, CH))
                dve.tensor_tensor(vals[:, ch % 2, :, 0:D].rearrange("p r (h c) -> p r h c", h=H),
                                  kv[:, s:s + C, D:2 * D].rearrange("p r (h c) -> p r h c", h=H), pb,
                                  ALU.mult).then_inc(S["vals"], 1)

            def add_sums(m, q, ch):
                colr = [dve.value_load(bB[0:1, q * T + s:q * T + s + 1], min_val=0, max_val=(env["NBE"] - 1) * OW)
                        for s in range(ch * C, ch * C + C)]
                dve.wait_ge(S["agg"], done(m, q, NCH, ch + 1))
                for r in range(C):
                    s = ch * C + r
                    col = colr[r]
                    if s:
                        dve.wait_ge(S["oadd"], done(m, q, T, s))
                    else:
                        dve.wait_ge(S["resc"], done(m, q, 2, 2))
                    ob = otab[:, bass.ds(col, OW)]
                    dve.tensor_tensor(ob, agg[:, ch % 2, r * OW:(r + 1) * OW], ob, ALU.add).then_inc(S["oadd"], 1)

            def scores(m, q):
                dve.wait_ge(S["ld_w"][q], nth(m, 16))
                dve.wait_ge(S["qwe"], done(m, q, NCH, NCH))
                wb = wq[:, q, :].unsqueeze(1).to_broadcast((P, H, T))
                dve.tensor_tensor(tmp[:, :, :], qw[:, q, :, :], wb, ALU.mult).then_inc(S["al1"], 1)
                dve.wait_ge(S["al1"], done(m, q, 1, 1))
                dve.wait_ge(S["red"], done(m, q, NCH, NCH))
                dve.tensor_tensor(alpha[:, q, :, :], alpha[:, q, :, :], tmp[:, :, :], ALU.add).then_inc(S["alpha"], 1)
                dve.tensor_copy(d4[:, :, :], dl[:, q, :].unsqueeze(1).to_broadcast((P, H, T))).then_inc(S["d4"], 1)

            def row_scans(m, q):
                dve.wait_ge(S["dTs"], done(m, q, 1, 1))
                dve.tensor_tensor(pen[:, 1:P], dTs[:, 0:P - 1], dTs[:, 1:P], ALU.subtract).then_inc(S["pen"], 1)
                dve.wait_ge(S["pen"], done(m, q, 1, 1))
                dve.tensor_tensor_scan(f1[:, :], pen[:, 0:P], aT_ps, -BIG, ALU.add, ALU.max).then_inc(S["scan1"], 1)
                dve.tensor_tensor_scan(b1[:, ::-1], pen[:, P:0:-1], aT_ps[:, ::-1], -BIG, ALU.add,
                                       ALU.max).then_inc(S["scan1"], 1)

            def carries(m, q):
                k = [0]

                def link(ins):
                    k[0] += 1
                    ins.then_inc(S["rowv"], 1)
                    dve.wait_ge(S["rowv"], done(m, q, NR, k[0]))

                dve.wait_ge(S["rw"], done(m, q, 1, 1))
                d_first, d_last = rw[0:1, 2, 0, :], rw[0:1, 3, 0, :]
                dve.tensor_copy(fx[0:1, :, 1:T + 1], rw[0:1, 0, :, :])
                link(dve.tensor_copy(dlx[0:1, 1:T + 1], d_last))
                dve.tensor_tensor(pw[0:1, :], d_first, d_last, ALU.subtract)
                link(dve.tensor_tensor(ne[0:1, :], dlx[0:1, 0:T], d_first, ALU.not_equal))
                dve.tensor_scalar(cf[0:1, :], ne[0:1, 0:1], -1.0, 1.0, ALU.mult, ALU.add)
                link(dve.tensor_scalar(pc[0:1, :], ne[0:1, :], -BIG, None, ALU.mult))

                def wide(ap, n):
                    return ap.unsqueeze(1).to_broadcast((1, H, n))

                dve.tensor_tensor(qbx[0:1, :, 0:T - 1], wide(pw[0:1, 0:T - 1], T - 1), wide(pc[0:1, 1:T], T - 1), ALU.add)
                link(dve.tensor_tensor(pwx[0:1, :, 1:T + 1], wide(pw[0:1, :], T), wide(pc[0:1, :], T), ALU.add))
                flat = lambda ap: ap.rearrange("p h t -> p (h t)")
                link(dve.tensor_tensor_scan(flat(bf[0:1, :, :])[:, ::-1], flat(qbx[0:1, :, :])[:, ::-1],
                                            rw[0:1, 1, :, :].rearrange("p h t -> p (h t)")[:, ::-1], -BIG, ALU.add, ALU.max))
                link(dve.tensor_tensor_scan(flat(lx[0:1, :, :]), flat(pwx[0:1, :, :]), flat(fx[0:1, :, :]), 0.0,
                                            ALU.add, ALU.max))
                dve.tensor_tensor(cr[0:1, 1, :, 0:T - 1], bf[0:1, :, 1:T], wide(pc[0:1, 1:T], T - 1), ALU.add).then_inc(S["cr"], 1)
                dve.tensor_tensor(cr[0:1, 0, :, :], lx[0:1, :, 0:T], wide(pc[0:1, :], T), ALU.add).then_inc(S["cr"], 1)
                link(dve.tensor_tensor(dm[0:1, :], fx[0:1, :, 0], bf[0:1, :, 0], ALU.subtract))
                link(dve.tensor_scalar(dm[0:1, :], dm[0:1, :], 0.0, cf[0:1, 0:1], ALU.min, ALU.mult))
                dve.tensor_copy(fx[0:1, :, 0], lx[0:1, :, T])
                link(dve.tensor_copy(dlx[0:1, 0:1], dlx[0:1, T:T + 1]))
                assert k[0] == NR

            def maxima(m, q):
                dve.wait_ge(S["cin"], done(m, q, 1, 1))
                dve.tensor_tensor_scan(f1[:, :], pen[:, 0:P], aT_ps, cin[:, 0:1], ALU.add, ALU.max).then_inc(S["scan2"], 1)
                dve.tensor_tensor_scan(b1[:, ::-1], pen[:, P:0:-1], aT_ps[:, ::-1], cin[:, 1:2], ALU.add,
                                       ALU.max).then_inc(S["scan2"], 1)
                dve.wait_ge(S["scan2"], done(m, q, 2, 2))
                dve.tensor_tensor(mx[:, :], f1[:, :], b1[:, :], ALU.max).then_inc(S["mx"], 1)
                dve.wait_ge(S["fe"], done(m, q, 1, 1))
                dve.tensor_scalar(fac[0:1, :], fe[0:1, :], -1.0, None, ALU.add).then_inc(S["fac"], 1)

            def below_max(m, q):
                dve.wait_ge(S["mT"], done(m, q, 1, 1))
                dve.tensor_tensor(tmp[:, :, :].rearrange("p h t -> p (h t)"), alpha[:, q, :, :].rearrange("p h t -> p (h t)"),
                                  mT_ps, ALU.subtract).then_inc(S["da"], 1)

            def times_weight(m, q):
                dve.wait_ge(S["pp"], done(m, q, 1, 1))
                wb = wq[:, q, :].unsqueeze(2).to_broadcast((P, T, H))
                dve.tensor_tensor(pp[:, q, :, H:2 * H], pp[:, q, :, 0:H], wb, ALU.mult).then_inc(S["pw"], 1)

            def rescale(m, q):
                col = dve.value_load(bB[0:1, q * T:q * T + 1], min_val=0, max_val=(env["NBE"] - 1) * OW)
                dve.wait_ge(S["facps"], done(m, q, 1, 1))
                dve.tensor_scalar(facn[:, :], fac_ps, 1.0, None, ALU.add).then_inc(S["facn"], 1)
                dve.wait_ge(S["facn"], done(m, q, 1, 1))
                ov = otab[:, bass.ds(col, D)].rearrange("p (h c) -> p h c", h=H)
                op = otab[:, bass.ds(col + D, 2 * H)].rearrange("p (k h) -> p k h", h=H)
                dve.tensor_tensor(ov, ov, facn[:, :].unsqueeze(2).to_broadcast((P, H, CH)), ALU.mult).then_inc(S["resc"], 1)
                dve.tensor_tensor(op, op, facn[:, :].unsqueeze(1).to_broadcast((P, 2, H)), ALU.mult).then_inc(S["resc"], 1)

            def iteration(m, q, a, b, n):
                hm, hq = prev(m, q)
                if n == 0:
                    onehots(m, q, 0, 0)
                    onehots(m, q, 1, 0)
                for ch in range(NCH):
                    if b and ch == 0:
                        scores(hm, hq)
                    if b and ch == 1:
                        row_scans(hm, hq)
                    if b and ch == 2:
                        carries(hm, hq)
                    if b and ch == 3:
                        maxima(hm, hq)
                    if a:
                        onehots_ahead(m, q, ch, n)
                        products(m, q, ch)
                    u = 2 * (ch - 4)
                    if b and ch == 3:
                        below_max(hm, hq)
                    if b and u >= 0:
                        if u == 0:
                            rescale(hm, hq)
                            dve.wait_ge(S["p"], done(hm, hq, 1, 1))
                        weighted(hm, hq, u)
                        if u:
                            add_sums(hm, hq, u - 1)
                    if a:
                        reduces(m, q, ch)
                    if b and u >= 0:
                        weighted(hm, hq, u + 1)
                        add_sums(hm, hq, u)
                    if b and ch == 3:
                        dve.wait_ge(S["ld_bB"][hq], nth(hm, 16))
                        times_weight(hm, hq)
                if b:
                    add_sums(hm, hq, NCH - 1)

            dve.memset(pen[:, :], 0.0)
            dve.memset(fx[0:1, :, :], 0.0)
            dve.memset(dlx[0:1, :], -BIG)
            dve.memset(pwx[0:1, :, :], -BIG)
            dve.memset(qbx[0:1, :, :], -BIG)
            dve.memset(cr[0:1, :, :, :], -BIG)
            dve.memset(one[0:1, :], 1.0).then_inc(S["init"], 1)
            dve.wait_ge(S["init"], L + 1)
            iteration(0, 0, True, False, 0)
            iteration(0, 1, True, True, 1)
            with dve.Fori(1, G // 2 - 1) as m:
                iteration(m, 0, True, True, 2)
                iteration(m, 1, True, True, 2)
            iteration(G // 2 - 1, 0, True, True, 2)
            iteration(G // 2 - 1, 1, True, True, 2)
            iteration(G // 2, 0, False, True, 2)



def message_pass(nc, sem, env):
    G, NBE = env["G"], env["NBE"]
    iota_b = env["iota_b"]
    mtab = env["mtab"]
    with ExitStack() as c:
        def sb(nm, shape, dt=F32):
            return c.enter_context(nc.sbuf_tensor("m_" + nm, shape, dt))

        hv = sb("hv", [P, 2 * T, D])
        idx = sb("idx", [P, 2 * T], I32)
        dl = sb("dl", [P, 2, T])
        co = sb("co", [P, 2, T, NCOEF])
        bB = sb("bB", [1, 2 * T], I32)
        oh = sb("oh", [P, 2, C, P])
        vals = sb("vals", [P, 2, C, MW])
        prod = sb("prod", [P, 2, 4, MUL, 3])
        co_ps = c.enter_context(nc.psum_tensor("m_co_ps", [P, 2, 512], F32))
        agg = c.enter_context(nc.psum_tensor("m_agg", [P, 2 * C, 512], F32))
        cp = co_ps[:, :, 0:T * NCOEF].rearrange("p q (t k) -> p q t k", k=NCOEF)

        ld = [sem(f"m_ld{q}") for q in range(2)]
        li = [sem(f"m_li{q}") for q in range(2)]
        hs = env["att"]["kv"]
        before = 2 * (G // 2) * 16 * C
        cs = sem("m_coef"); os_ = sem("m_onehot"); a0 = sem("m_a0"); a1 = sem("m_a1"); pr = sem("m_prod")
        rd = sem("m_red"); ag = sem("m_agg_s"); ad = sem("m_add"); z = sem("m_zero")

        def done(m, q, per, k):
            return (2 * m + q) * per + k

        def prev(m, q, by=1):
            return (m, q - by) if q - by >= 0 else (m - 1, q - by + 2)

        block = c.enter_context(nc.Block())

        def whole(eng, group):
            group(0, 0, 0)
            group(0, 1, 1)
            with eng.Fori(1, G // 2) as m:
                group(m, 0, 2)
                group(m, 1, 2)

        def back(m, q, ch):
            return (m, q, ch - 1) if ch >= 2 else (*prev(m, q), NCH + ch - 1)

        @block.sync
        def _(sp):
            def group(m, q, n):
                cols = bass.ds((2 * m + q) * T, T)
                if n == 2:
                    pm, pq = prev(m, q, 2)
                    sp.wait_ge(a1, done(pm, pq, NCH, NCH))
                    sp.nop(nofuse=True)
                sp.dma_start(idx[:, q * T:(q + 1) * T], env["idx_d"][:, cols]).then_inc(li[q], 16)
                if n == 2:
                    sp.wait_ge(ad, done(pm, pq, T, T))
                    sp.nop(nofuse=True)
                    sp.wait_ge(a0, done(pm, pq, NCH, NCH))
                    sp.nop(nofuse=True)
                    sp.wait_ge(cs, done(pm, pq, 1, 1))
                    sp.nop(nofuse=True)
                sp.dma_start(dl[:, q, :], env["dl_d"][:, cols]).then_inc(ld[q], 16)
                sp.dma_start(co[:, q, :, :], env["coef_d"][:, cols, :]).then_inc(ld[q], 16)
                sp.dma_start(bB[:, q * T:(q + 1) * T], env["brow_d"][2:3, cols]).then_inc(ld[q], 16)
            whole(sp, group)

        @block.gpsimd
        def _(pool):
            def group(m, q, n):
                for ch in range(NCH):
                    if n == 2:
                        pm, pq = prev(m, q, 2)
                        pool.wait_ge(rd, done(pm, pq, T, C * (ch + 1)))
                        pool.wait_ge(a0, done(pm, pq, NCH, ch + 1))
                    if ch == 0:
                        pool.wait_ge(li[q], m * 16 + 16)
                    pool.nop(nofuse=True)
                    for r in range(C):
                        s = q * T + ch * C + r
                        pool.indirect_dma_start(
                            out=hv[:, s, :], out_offset=None, in_=env["h_d"],
                            in_offset=bass.IndirectOffsetOnAxis(ap=idx[:, s:s + 1], axis=0)).then_inc(hs[q][ch], 16)
            whole(pool, group)

        @block.scalar
        def _(act):
            def group(m, q, n):
                act.wait_ge(ld[q], m * 48 + 48)
                if n == 2:
                    pm, pq = prev(m, q, 2)
                    act.wait_ge(rd, done(pm, pq, T, T))
                act.activation(co_ps[:, q, 0:T * NCOEF], co[:, q, :, :].rearrange("p t k -> p (t k)"),
                               ACT.Copy).then_inc(cs, 1)
                for ch in range(NCH):
                    if n or ch >= 2:
                        act.wait_ge(ag, done(*back(m, q, ch)[:2], NCH, back(m, q, ch)[2]))
                    act.wait_ge(hs[q][ch], m * 48 + (48 + before))
                    for r in range(C):
                        s = ch * C + r
                        last = act.activation(vals[:, ch % 2, r, 0:D], hv[:, q * T + s, :], ACT.Copy,
                                              scale=co[:, q, s, 12:13])
                    last.then_inc(a0, 1)
            whole(act, group)

        @block.tensor
        def _(pe):
            pe.wait_ge(z, 1)

            def group(m, q, n):
                for ch in range(NCH):
                    pe.wait_ge(a0, done(m, q, NCH, ch + 1))
                    pe.wait_ge(rd, done(m, q, T, C * (ch + 1)))
                    if n or ch >= 2:
                        bm, bq, bc = back(m, q, ch)
                        pe.wait_ge(ad, done(bm, bq, T, bc * C))
                    for r in range(C):
                        last = pe.matmul(agg[:, (ch % 2) * C + r, 0:MW], oh[:, ch % 2, r, :], vals[:, ch % 2, r, :],
                                         start=True, stop=True)
                    last.then_inc(ag, 1)
            whole(pe, group)

        @block.vector
        def _(dve):
            dve.memset(mtab[:, :], 0.0).then_inc(z, 1)
            dve.wait_ge(z, 1)

            def add_sums(m, q, ch):
                colr = [dve.value_load(bB[0:1, q * T + s:q * T + s + 1], min_val=0, max_val=(NBE - 1) * MW)
                        for s in range(ch * C, ch * C + C)]
                dve.wait_ge(ag, done(m, q, NCH, ch + 1))
                for r in range(C):
                    s = ch * C + r
                    col = colr[r]
                    if not (isinstance(m, int) and m == 0 and q == 0 and s == 0):
                        dve.wait_ge(ad, done(m, q, T, s))
                    mb = mtab[:, bass.ds(col, MW)]
                    dve.tensor_tensor(mb, agg[:, (ch % 2) * C + r, 0:MW], mb, ALU.add).then_inc(ad, 1)

            def group(m, q, n):
                dve.wait_ge(ld[q], m * 48 + 48)
                dve.wait_ge(cs, done(m, q, 1, 1))
                for ch in range(NCH):
                    if n or ch >= 2:
                        bm, bq, bc = back(m, q, ch)
                        dve.wait_ge(ag, done(bm, bq, NCH, bc))
                    for r in range(C):
                        s = ch * C + r
                        last = dve.tensor_scalar(oh[:, ch % 2, r, :], iota_b[:, :], dl[:, q, s:s + 1], None, ALU.is_equal)
                    last.then_inc(os_, 1)
                    dve.wait_ge(hs[q][ch], m * 48 + (48 + before))
                    s0 = ch * C
                    dve.tensor_tensor(vals[:, ch % 2, :, D:D + 96].rearrange("p r (k u) -> p r k u", k=3),
                                      hv[:, q * T + s0:q * T + s0 + C, 0:MUL].unsqueeze(2).to_broadcast((P, C, 3, MUL)),
                                      cp[:, q, s0:s0 + C, 9:12].unsqueeze(3).to_broadcast((P, C, 3, MUL)),
                                      ALU.mult).then_inc(a1, 1)
                    for r in range(C):
                        s = s0 + r
                        if not (isinstance(m, int) and m == 0 and q == 0 and s < 2):
                            pm, pq = (m, q) if s >= 2 else prev(m, q)
                            dve.wait_ge(rd, done(pm, pq, T, (s - 2) % T + 1))
                        dve.tensor_tensor(prod[:, s % 2, :, :, :],
                                          hv[:, q * T + s, MUL:D].rearrange("p (i u) -> p u i", i=3).unsqueeze(1)
                                          .to_broadcast((P, 4, MUL, 3)),
                                          cp[:, q, s, 0:12].rearrange("p (k i) -> p k i", i=3).unsqueeze(2)
                                          .to_broadcast((P, 4, MUL, 3)), ALU.mult).then_inc(pr, 1)
                        dve.wait_ge(pr, done(m, q, T, s + 1))
                        dve.tensor_reduce(vals[:, ch % 2, r, D + 96:MW].rearrange("p (k u) -> p k u", k=4),
                                          prod[:, s % 2, :, :, :], AX.X, ALU.add).then_inc(rd, 1)
                    if ch:
                        add_sums(m, q, ch - 1)
                    elif n:
                        add_sums(*prev(m, q), NCH - 1)

            whole(dve, group)
            add_sums(G // 2 - 1, 1, NCH - 1)



def final_phase(nc, sem, env):
    NBE = env["NBE"]
    ident, mtab = env["ident"], env["mtab"]
    W = env["weights"]
    r10 = 1.0 / float(np.sqrt(10.0))
    n0 = float(np.sqrt(1.0 / 64)) * r10
    n1 = float(np.sqrt(3.0 / 96)) * r10
    r3 = 1.0 / float(np.sqrt(3.0))
    cst = [n0, n1 * r3, n1 * r3, n0 * r3, n1]
    rows = ([(0, 0, 0, 1)] + [(32 + 32 * k, 2, 32 + k, 3) for k in range(3)] + [(128 + 32 * k, 1, 32 + k, 3) for k in range(3)]
            + [(224 + 32 * k, 4, 32 + k, 3) for k in range(3)] + [(320, 3, 0, 1)])
    with ExitStack() as c:
        def sb(nm, shape, dt=F32):
            return c.enter_context(nc.sbuf_tensor("f_" + nm, shape, dt))

        wraw = sb("wraw", [P, 3, MUL])
        wbig = sb("wbig", [P, 3, D])
        mT = sb("mT", [P, 2, 3, P])
        rows_now = sb("rows_now", [P, 2, MW])
        x1 = sb("x1", [P, 2, D])
        y = sb("y", [P, 2, D])
        pT = c.enter_context(nc.psum_tensor("f_pT", [P, 2, 512], F32))
        po = c.enter_context(nc.psum_tensor("f_po", [P, 2, 512], F32))
        wl = sem("f_wl"); wz = sem("f_wz"); wb = sem("f_wb"); xl = [sem(f"f_x{q}") for q in range(2)]
        rn = sem("f_rows"); tt = sem("f_tr"); mc = sem("f_mT"); mm = sem("f_mm"); ys = sem("f_y"); st = [sem(f"f_st{q}") for q in range(2)]
        block = c.enter_context(nc.Block())
        NP = NBE // 2
        KS = (128, 128, 96)

        def loop(eng, body):
            body(0, 0, True)
            body(0, 1, True)
            with eng.Fori(1, NP) as m:
                body(m, 0, False)
                body(m, 1, False)

        @block.sync
        def _(sp):
            for r, k, _, _ in rows:
                sp.dma_start(wraw[r % P:r % P + MUL, r // P, :], W[f"w{k}"]).then_inc(wl, 16)

            def body(m, q, first):
                b = 2 * m + q
                if not first:
                    sp.wait_ge(ys, b - 1)
                    sp.nop(nofuse=True)
                sp.dma_start(x1[:, q, :], env["x1_d"][bass.ds(b * P, P), :]).then_inc(xl[q], 16)
            loop(sp, body)

        @block.gpsimd
        def _(pool):
            def body(m, q, first):
                b = 2 * m + q
                pool.wait_ge(ys, b + 1)
                pool.nop(nofuse=True)
                pool.dma_start(env["out"][bass.ds(b * P, P), :], y[:, q, :]).then_inc(st[q], 16)
            loop(pool, body)
            for q in range(2):
                pool.wait_ge(st[q], 16 * NP)

        @block.tensor
        def _(pe):
            pe.wait_ge(wb, len(rows))

            def body(m, q, first):
                b = 2 * m + q
                pe.wait_ge(rn, b + 1)
                if not first:
                    pe.wait_ge(mc, b - 1)
                for j, k in enumerate(KS):
                    last = pe.transpose(pT[0:k, q, j * P:(j + 1) * P], rows_now[:, q, j * P:j * P + k], ident[:, :])
                last.then_inc(tt, 1)
                pe.wait_ge(mc, b + 1)
                if not first:
                    pe.wait_ge(ys, b - 1)
                for j, k in enumerate(KS):
                    last = pe.matmul(po[:, q, 0:D], mT[0:k, q, j, :], wbig[0:k, j, :], start=(j == 0), stop=(j == 2))
                last.then_inc(mm, 1)
            loop(pe, body)

        @block.scalar
        def _(act):
            def body(m, q, first):
                b = 2 * m + q
                act.wait_ge(tt, b + 1)
                if not first:
                    act.wait_ge(mm, b - 1)
                act.activation(mT[:, q, 0:2, :].rearrange("p j n -> p (j n)"), pT[:, q, 0:2 * P], ACT.Copy)
                act.activation(mT[0:96, q, 2, :], pT[0:96, q, 2 * P:3 * P], ACT.Copy).then_inc(mc, 1)
            loop(act, body)

        @block.vector
        def _(dve):
            dve.memset(wbig[:, :, :], 0.0).then_inc(wz, 1)
            dve.wait_ge(wz, 1)
            dve.wait_ge(wl, 16 * len(rows))
            for r, k, col, step in rows:
                o = wbig[r % P:r % P + MUL, r // P, col:col + step * (MUL - 1) + 1:step]
                dve.tensor_scalar(o, wraw[r % P:r % P + MUL, r // P, :], cst[k], None, ALU.mult).then_inc(wb, 1)

            def body(m, q, first):
                b = 2 * m + q
                if not first:
                    dve.wait_ge(tt, b - 1)
                dve.tensor_copy(rows_now[:, q, :], mtab[:, bass.ds(b * MW, MW)]).then_inc(rn, 1)
                dve.wait_ge(mm, b + 1)
                dve.wait_ge(xl[q], 16 * m + 16)
                if not first:
                    dve.wait_ge(st[q], 16 * m)
                dve.tensor_tensor(y[:, q, :], po[:, q, 0:D], x1[:, q, :], ALU.add).then_inc(ys, 1)
            loop(dve, body)



def kernel(**inputs):
    import numpy as _np
    import concourse.bacc as _bacc
    from concourse import mybir as _mybir
    from concourse.bass_utils import run_bass_kernel_spmd as _run

    x = _np.asarray(inputs["x"])
    n_nodes, n_edges = x.shape[0], inputs["src"].shape[0]
    NBE, NT, _, _ = sizes(n_nodes, n_edges)

    def tiles(a, fill):
        a = _np.asarray(a)
        out = _np.full(((NT + 1) * P,) + a.shape[1:], fill, a.dtype)
        out[:n_edges] = a
        return out.reshape((NT + 1, P) + a.shape[1:])

    x_p = _np.zeros((NBE * P, D), x.dtype)
    x_p[:n_nodes] = x
    dst_t = tiles(inputs["dst"], (NBE + 1) * P)
    arrays = {
        "x_p": x_p,
        "src_t": tiles(inputs["src"], 0),
        "dst_t": dst_t,
        "dlast": _np.ascontiguousarray(dst_t[:NT, P - 1][None, :]),
        "ew_t": tiles(inputs["edge_weight"], 0),
        "attr_t": _np.ascontiguousarray(tiles(inputs["edge_attr_9"], 0).transpose(0, 2, 1)).reshape(NT + 1, 9 * P),
    }
    wnames = {}
    for l in (1, 2):
        for k in ("Wq", "bq", "Wk", "bk", "Wv", "bv", "We", "Ws", "bs"):
            wnames[f"{k}{l}"] = f"L0_gnn_{k}{l}"
    for k in range(5):
        wnames[f"w{k}"] = f"L1_gnn_w{k}"
    for short, full in wnames.items():
        a = _np.ascontiguousarray(inputs[full])
        arrays["in_" + short] = a.reshape(MUL, MUL) if full.startswith("L1") else a

    nc = _bacc.Bacc("TRN2", target_bir_lowering=False, num_devices=1)
    aps = {n: nc.dram_tensor(n, a.shape, _mybir.dt.from_np(a.dtype), kind="ExternalInput").ap() for n, a in arrays.items()}
    out = nc.dram_tensor("out", (NBE * P, D), F32, kind="ExternalOutput").ap()
    weights = {short: aps["in_" + short] for short in wnames}
    weights["n_nodes"], weights["n_edges"] = n_nodes, n_edges
    build(nc, aps["x_p"], aps["src_t"], aps["dst_t"], aps["dlast"], aps["ew_t"], aps["attr_t"], weights, out)
    r = _run(nc, [arrays], core_ids=[0])
    return r.results[0]["out"][:n_nodes]
```

```python
from contextlib import ExitStack
from math import factorial

import numpy as np
import concourse.bass as bass
from concourse import mybir

ALU = mybir.AluOpType
ACT = mybir.ActivationFunctionType
AX = mybir.AxisListType
F32 = mybir.dt.float32
BF16 = mybir.dt.bfloat16
I32 = mybir.dt.int32

P = 128
D = 128
H = 4
CH = D // H
MUL = 32
T = 24
C = 3
NCH = T // C
QW = 136
OW = 136
MW = 352
NCOEF = 13
BIG = 1e38
KEY = 1e33
EPS = 1e-5
SCALE = float(1.0 / np.sqrt(np.float32(CH)))


CLAMPED = "the block numbers are clamped to 0 .. blocks - 1 where they are made"


def ceil_div(a, b):
    return (a + b - 1) // b


def sizes(n_nodes, n_edges):
    nb = ceil_div(n_nodes, P)
    nt = ceil_div(n_edges, C * P)
    groups = ceil_div(nt + nb - 1, NCH)
    groups += groups % 2
    return nb + nb % 2, nt, groups, ceil_div(groups * NCH, P)


def wigner_112():
    def ratio(a, b):
        return float(a) / float(b)

    def coeff(j1, m1, j2, m2, j3, m3):
        vmin = int(max(-j1 + j2 + m3, -j1 + m1, 0))
        vmax = int(min(j2 + j3 + m1, j3 - j1 + j2, j3 + m3))
        f = lambda n: factorial(round(n))
        c = ((2.0 * j3 + 1.0) * ratio(f(j3 + j1 - j2) * f(j3 - j1 + j2) * f(j1 + j2 - j3) * f(j3 + m3) * f(j3 - m3),
                                         f(j1 + j2 + j3 + 1) * f(j1 - m1) * f(j1 + m1) * f(j2 - m2) * f(j2 + m2))) ** 0.5
        s = 0
        for v in range(vmin, vmax + 1):
            s += (-1) ** (v + j2 + m2) * ratio(f(j2 + j3 + m1 - v) * f(j1 - m1 + v),
                                                  f(v) * f(j3 - j1 + j2 - v) * f(j3 + m3 - v) * f(v + j1 - j2 - m3))
        return float(c * s)

    def basis(l):
        q = np.zeros((2 * l + 1, 2 * l + 1), dtype=np.complex128)
        for m in range(-l, 0):
            q[l + m, l + abs(m)] = 1 / np.sqrt(2)
            q[l + m, l - abs(m)] = -1j / np.sqrt(2)
        q[l, l] = 1
        for m in range(1, l + 1):
            q[l + m, l + abs(m)] = (-1) ** m / np.sqrt(2)
            q[l + m, l - abs(m)] = 1j * (-1) ** m / np.sqrt(2)
        return (-1j) ** l * q

    c = np.zeros((3, 5, 3))
    for m1 in range(-1, 2):
        for m2 in range(-2, 3):
            if abs(m1 + m2) <= 1:
                c[1 + m1, 2 + m2, 1 + m1 + m2] = coeff(1, m1, 2, m2, 1, m1 + m2)
    r = np.real(np.einsum('ij,kl,mn,ikn->jlm', basis(1), basis(2), np.conj(basis(1).T), c.astype(np.complex128)))
    return r / np.linalg.norm(r)


def build(nc, x_p, src_t, dst_t, dlast, ew_t, attr_t, weights, out):
    n_rows = x_p.shape[0]
    n_nodes = weights["n_nodes"]
    n_edges = weights["n_edges"]
    NBE, NT, G, NBLK = sizes(n_nodes, n_edges)
    SP = NBLK * P * C
    assert n_rows == NBE * P and src_t.shape[0] == NT + 1 and G >= 6 and NBE >= 4

    def scratch(name, shape, dt):
        return nc.dram_tensor(name, shape, dt, kind="Internal").ap()

    idx_d = scratch("slot_src", (P, SP), I32)
    dl_d = scratch("slot_dloc", (P, SP), F32)
    ew_d = scratch("slot_ew", (P, SP), F32)
    coef_d = scratch("slot_coef", (P, SP, NCOEF), F32)
    brow_d = scratch("chunk_block", (3, NBLK * P), I32)
    kv_d = [scratch(f"kv{l}", (NBE * P, 2 * D), F32) for l in range(2)]
    skip_d = [scratch(f"skip{l}", (NBE * P, D), F32) for l in range(2)]
    h_d = scratch("h_planar", (NBE * P, D), F32)
    x1_d = scratch("x1", (NBE * P, D), F32)

    with ExitStack() as top:
        def sem(name):
            return top.enter_context(nc.semaphore(name))

        ident = top.enter_context(nc.sbuf_tensor("ident", [P, P], F32))
        ident_b = top.enter_context(nc.sbuf_tensor("ident_b", [P, P], BF16))
        iota_b = top.enter_context(nc.sbuf_tensor("iota_b", [P, P], BF16))
        iota_i = top.enter_context(nc.sbuf_tensor("iota_i", [P, P], I32))
        step_tables(nc, sem, locals())
        att = attention_sems(sem)
        with ExitStack() as mid:
            qtab = mid.enter_context(nc.sbuf_tensor("qtab", [P, NBE * QW], F32))
            otab = mid.enter_context(nc.sbuf_tensor("otab", [P, NBE * OW], F32))
            env = dict(locals())
            env["att"] = att
            node_phase(nc, sem, env, 0)
            attention_pass(nc, env, 0)
            node_phase(nc, sem, env, 1)
            attention_pass(nc, env, 1)
            node_phase(nc, sem, env, 2)
        with ExitStack() as mid:
            mtab = mid.enter_context(nc.sbuf_tensor("mtab", [P, NBE * MW], F32))
            env = dict(locals())
            message_pass(nc, sem, env)
            final_phase(nc, sem, env)



def step_tables(nc, sem, env):
    NT, NBLK = env["NT"], env["NBLK"]
    n_nodes = env["n_nodes"]
    nb = ceil_div(n_nodes, P)
    ident, ident_b, iota_b, iota_i = env["ident"], env["ident_b"], env["iota_b"], env["iota_i"]
    W3 = wigner_112()
    terms = {(i, k): [(j, float(W3[i, j, k])) for j in range(5) if abs(W3[i, j, k]) > 1e-9]
             for i in range(3) for k in range(3)}
    N_TWO = sum(len(t) == 2 for t in terms.values())
    R = C * P
    with ExitStack() as c:
        def sb(name, shape, dt=F32):
            return c.enter_context(nc.sbuf_tensor(name, shape, dt))

        last_i = sb("last_i", [P, NT], I32)
        tile_i = sb("tile_i", [P, NT], I32)
        step_i = sb("step_i", [P, NBLK], I32)
        last_m = sb("last_m", [P, NT], I32)
        last_b = sb("last_b", [P, NT], I32)
        last_f = sb("last_f", [P, NT])
        tile_f = sb("tile_f", [P, NT])
        end_f = sb("end_f", [P, NT])
        lt = sb("lt", [P, NT])
        step_f = sb("step_f", [P, NBLK])
        t_f = sb("t_f", [P, NBLK])
        t_i = sb("t_i", [P, NBLK], I32)
        b_f = sb("b_f", [P, NBLK])
        b_n = sb("b_n", [P, NBLK])
        b_s = sb("b_s", [P, 3, NBLK])
        b_rows = sb("b_rows", [NBLK, 3, P], I32)
        rows_s = sb("rows_s", [P, 2, R], I32)
        rows_d = sb("rows_d", [P, 2, R], I32)
        rows_w = sb("rows_w", [P, 2, R])
        rows_a = sb("rows_a", [P, 2, 9 * R])
        rows_sf = sb("rows_sf", [P, R])
        rows_df = sb("rows_df", [P, R])
        rows_dl = sb("rows_dl", [P, R])
        o_src = sb("o_src", [P, 2, P, C], I32)
        o_dl = sb("o_dl", [P, 2, P, C])
        o_w = sb("o_w", [P, 2, P, C])
        o_at = sb("o_at", [P, 9, P, C])
        second = sb("second", [P, N_TWO, R])
        o_co = sb("o_co", [P, 2, P * C, NCOEF])
        ps = [c.enter_context(nc.psum_tensor(f"pt{i}", [P, 4, P], F32)) for i in range(3)]
        pa = [c.enter_context(nc.psum_tensor(f"pa{i}", [P, 4, P], F32)) for i in range(4)]

        consts = sem("pre_consts"); consts0 = sem("pre_consts0"); dl_in = sem("pre_last"); cd = sem("pre_calc")
        bt = sem("pre_bt"); br = sem("pre_br"); bout = sem("pre_bout")
        gat = [sem(f"pre_gather{q}") for q in range(2)]
        rf = sem("pre_rowsf"); tr = sem("pre_tr"); ev = sem("pre_ev")
        atc = sem("pre_attr"); coz = sem("pre_coef"); tw = sem("pre_two")
        st = [sem(f"pre_store{q}") for q in range(2)]
        block = c.enter_context(nc.Block())
        T_READY = 10 + NBLK
        B_READY = 14 + NBLK

        @block.gpsimd
        def _(pool):
            pool.memset(ident[:, :], 0.0).then_inc(consts0, 1)
            pool.iota(iota_i[:, :], pattern=[[1, P]], base=0, channel_multiplier=0).then_inc(consts, 1)
            pool.iota(tile_i[:, :], pattern=[[1, NT]], base=0, channel_multiplier=0).then_inc(consts, 1)
            pool.iota(step_i[:, :], pattern=[[P, NBLK]], base=0, channel_multiplier=1).then_inc(consts, 1)
            pool.wait_ge(consts0, 1)
            pool.affine_select(out=ident[:, :], in_=ident[:, :], compare_op=ALU.not_equal, fill=1.0, base=0,
                               pattern=[[-1, P]], channel_multiplier=1).then_inc(consts, 1)
            pool.wait_ge(cd, T_READY)
            for k in range(NBLK):
                if k >= 2:
                    pool.wait_ge(tr, C * (k - 1))
                for buf, tab in ((rows_s, "src_t"), (rows_d, "dst_t"), (rows_w, "ew_t"), (rows_a, "attr_t")):
                    pool.indirect_dma_start(out=buf[:, k % 2, :], out_offset=None, in_=env[tab],
                                            in_offset=bass.IndirectOffsetOnAxis(ap=t_i[:, k:k + 1], axis=0))\
                        .then_inc(gat[k % 2], 16)

        @block.sync
        def _(sp):
            sp.dma_start(last_i[:, :], env["dlast"].partition_broadcast(P)).then_inc(dl_in, 16)
            sp.wait_ge(br, 3)
            sp.dma_start(env["brow_d"].rearrange("w (k p) -> k w p", p=P), b_rows[:, :, :]).then_inc(bout, 16)
            for k in range(NBLK):
                q = k % 2
                sp.wait_ge(ev, 3 * C * (k + 1))
                cols = slice(k * R, (k + 1) * R)
                for ap, buf in ((env["idx_d"], o_src), (env["dl_d"], o_dl), (env["ew_d"], o_w)):
                    sp.dma_start(ap[:, cols], buf[:, q, :, :].rearrange("p n r -> p (n r)")).then_inc(st[q], 16)
                sp.wait_ge(coz, NCOEF * (k + 1))
                sp.dma_start(env["coef_d"][:, cols, :], o_co[:, q, :, :]).then_inc(st[q], 16)
            sp.wait_ge(bout, 16)
            for q in range(2):
                sp.wait_ge(st[q], 64 * ((NBLK + 1 - q) // 2))

        @block.tensor
        def _(pe):
            pe.wait_ge(consts, 4)
            pe.wait_ge(cd, B_READY)
            for w in range(3):
                pe.transpose(ps[0][0:NBLK, w, :], b_s[:, w, :], ident[:, :]).then_inc(bt, 1)
            pe.wait_ge(br, 3)
            for k in range(NBLK):
                q = k % 2
                pe.wait_ge(rf, 3 * (k + 1))
                for r in range(C):
                    n = k * C + r
                    if n >= C:
                        pe.wait_ge(ev, 3 * (n - C + 1))
                    if n >= 2:
                        pe.wait_ge(atc, 3 * (n - 1))
                    e = slice(r * P, (r + 1) * P)
                    pe.transpose(ps[r][:, 0, :], rows_sf[:, e], ident[:, :])
                    pe.transpose(ps[r][:, 1, :], rows_dl[:, e], ident[:, :])
                    pe.transpose(ps[r][:, 2, :], rows_w[:, q, e], ident[:, :])
                    for a in range(9):
                        dst = ps[r][:, 3, :] if a == 8 else pa[2 * (n % 2) + a // 4][:, a % 4, :]
                        last = pe.transpose(dst, rows_a[:, q, a * R + r * P:a * R + (r + 1) * P], ident[:, :])
                    last.then_inc(tr, 1)

        @block.scalar
        def _(act):
            for n in range(NBLK * C):
                k, r = n // C, n % C
                act.wait_ge(tr, n + 1)
                if k and r == 0:
                    act.wait_ge(coz, NCOEF * k)
                for h in range(2):
                    act.activation(o_at[:, 4 * h:4 * h + 4, :, r], pa[2 * (n % 2) + h][:, :, :], ACT.Copy).then_inc(atc, 1)
                act.wait_ge(ev, 3 * (n + 1))
                act.activation(o_at[:, 8, :, r], ps[r][:, 3, :], ACT.Copy).then_inc(atc, 1)

        @block.vector
        def _(dve):
            n = [0]

            def link(ins):
                n[0] += 1
                ins.then_inc(cd, 1)
                dve.wait_ge(cd, n[0])

            dve.wait_ge(consts, 4)
            link(dve.tensor_copy(iota_b[:, :], iota_i[:, :]))
            link(dve.tensor_copy(ident_b[:, :], ident[:, :]))
            link(dve.tensor_copy(tile_f[:, :], tile_i[:, :]))
            link(dve.tensor_copy(step_f[:, :], step_i[:, :]))
            dve.wait_ge(dl_in, 16)
            link(dve.tensor_scalar(last_m[:, :], last_i[:, :], float(n_nodes - 1), None, ALU.min))
            link(dve.tensor_scalar(last_b[:, :], last_m[:, :], 7, None, ALU.arith_shift_right))
            link(dve.tensor_copy(last_f[:, :], last_b[:, :]))
            link(dve.tensor_tensor(end_f[:, :], last_f[:, :], tile_f[:, :], ALU.add))
            for k in range(NBLK):
                link(dve.tensor_scalar(lt[:, :], end_f[:, :], step_f[:, k:k + 1], 0.0, ALU.is_lt, ALU.add,
                                       accum_out=t_f[:, k:k + 1]))
            link(dve.tensor_copy(t_i[:, :], t_f[:, :]))
            link(dve.tensor_tensor(b_f[:, :], step_f[:, :], t_f[:, :], ALU.subtract))
            assert n[0] == T_READY
            link(dve.tensor_scalar(b_n[:, :], b_f[:, :], float(nb - 1), None, ALU.min))
            for w, width in enumerate((QW, OW, MW)):
                link(dve.tensor_scalar(b_s[:, w, :], b_n[:, :], float(width), None, ALU.mult))
            assert n[0] == B_READY
            dve.wait_ge(bt, 3)
            for w in range(3):
                dve.tensor_copy(b_rows[:, w, :], ps[0][0:NBLK, w, :]).then_inc(br, 1)

            two = 0
            for k in range(NBLK):
                q = k % 2
                dve.wait_ge(gat[q], 64 * (k // 2 + 1))
                if k:
                    dve.wait_ge(tr, C * k)
                dve.tensor_copy(rows_sf[:, :], rows_s[:, q, :]).then_inc(rf, 1)
                dve.tensor_copy(rows_df[:, :], rows_d[:, q, :]).then_inc(rf, 1)
                dve.wait_ge(rf, 3 * k + 2)
                dve.scalar_tensor_tensor(out=rows_dl[:, :], in0=b_n[:, k:k + 1].to_broadcast((P, R)), scalar=-float(P),
                                         in1=rows_df[:, :], op0=ALU.mult, op1=ALU.add).then_inc(rf, 1)
                if k >= 2:
                    dve.wait_ge(st[q], 64 * (k // 2))
                for r in range(C):
                    dve.wait_ge(tr, C * k + r + 1)
                    dve.tensor_copy(o_src[:, q, :, r], ps[r][:, 0, :]).then_inc(ev, 1)
                    dve.tensor_copy(o_dl[:, q, :, r], ps[r][:, 1, :]).then_inc(ev, 1)
                    dve.tensor_copy(o_w[:, q, :, r], ps[r][:, 2, :]).then_inc(ev, 1)
                dve.wait_ge(atc, 3 * C * (k + 1))
                at = lambda a: o_at[:, a, :, :].rearrange("p n r -> p (n r)")
                for kk in range(3):
                    for i in range(3):
                        o = o_co[:, q, :, 3 * kk + i]
                        j, w = terms[i, kk][0]
                        if len(terms[i, kk]) == 1:
                            dve.tensor_scalar(o, at(4 + j), w, None, ALU.mult).then_inc(coz, 1)
                        else:
                            j2, w2 = terms[i, kk][1]
                            buf = second[:, two % N_TWO, :]
                            dve.tensor_scalar(buf, at(4 + j2), w2, None, ALU.mult).then_inc(tw, 1)
                            two += 1
                            dve.wait_ge(tw, two)
                            dve.scalar_tensor_tensor(out=o, in0=at(4 + j), scalar=w, in1=buf,
                                                     op0=ALU.mult, op1=ALU.add).then_inc(coz, 1)
                for i in range(3):
                    dve.tensor_copy(o_co[:, q, :, 9 + i], at(1 + i)).then_inc(coz, 1)
                dve.tensor_copy(o_co[:, q, :, 12], at(0)).then_inc(coz, 1)



def node_phase(nc, sem, env, kind):
    NBE = env["NBE"]
    ident = env["ident"]
    qtab, otab = env["qtab"], env["otab"]
    W = env["weights"]
    name = f"n{kind}_"
    with ExitStack() as c:
        def sb(nm, shape, dt=F32):
            return c.enter_context(nc.sbuf_tensor(name + nm, shape, dt))

        w4 = sb("w4", [P, 4 * D])
        bias = sb("bias", [P, 4 * D])
        we_q = sb("we_q", [P, D])
        we_o = sb("we_o", [P, D])
        xin = sb("xin", [P, 2, D])
        sin = sb("sin", [P, 2, D])
        hin = sb("hin", [P, 2, D])
        x1 = sb("x1", [P, 2, D])
        den = sb("den", [P, 2, H])
        rec = sb("rec", [P, 2, H])
        pwr = sb("pwr", [P, 2, H])
        t1 = sb("t1", [P, 2, D])
        t2 = sb("t2", [P, 2, D])
        stat = sb("stat", [P, 2, 6])
        mv = sb("mv", [P, 2, 2])
        sd = sb("sd", [P, 2, 1])
        rs = sb("rs", [P, 2, 1])
        xn = sb("xn", [P, 2, D])
        hT = sb("hT", [P, 2, D])
        kvs = sb("kvs", [P, 2, 3 * D])
        qe = sb("qe", [P, 2, D])
        hp = sb("hp", [P, 2, D])
        eps = sb("eps", [P, 1])
        pT = c.enter_context(nc.psum_tensor(name + "pT", [P, 2, 512], F32))
        pp = c.enter_context(nc.psum_tensor(name + "pp", [P, 2, 512], F32))

        wl = sem(name + "weights"); xl = [sem(name + f"x{q}") for q in range(2)]
        ch = sem(name + "dve"); sq = sem(name + "sqrt"); xs = sem(name + "xn"); tt = sem(name + "tr")
        hs = sem(name + "hT"); mm = sem(name + "proj"); kd = sem(name + "kvs"); qd = sem(name + "q")
        st = [sem(name + f"st{q}") for q in range(2)]
        ez = sem(name + "eps")
        qq = sem(name + "qe")
        pre = {0: 0, 1: 6, 2: 8}[kind]
        nv = pre + 2
        per = {0: 3, 1: 6, 2: 11}[kind]

        loads = {0: 1, 1: 1, 2: 2}[kind]
        stores = {0: 2, 1: 2, 2: 2}[kind]
        block = c.enter_context(nc.Block())
        NP = NBE // 2

        def src_rows(ap, b):
            return ap[bass.ds(b * P, P), :]

        @block.sync
        def _(sp):
            nw = 0
            if kind < 2:
                l = kind + 1
                for i, k in enumerate(("q", "k", "v", "s")):
                    sp.dma_start(w4[:, i * D:(i + 1) * D], W[f"W{k}{l}"]).then_inc(wl, 16)
                    sp.dma_start(bias[:, i * D:(i + 1) * D],
                                 W[f"b{k}{l}"].rearrange("(a n) -> a n", a=1).partition_broadcast(P)).then_inc(wl, 16)
                    nw += 2
                sp.dma_start(we_q[:, :], W[f"We{l}"].partition_broadcast(P)).then_inc(wl, 16)
                nw += 1
            if kind > 0:
                sp.dma_start(we_o[:, :], W[f"We{kind}"].partition_broadcast(P)).then_inc(wl, 16)
                nw += 1

            def load(m, q, first):
                b = 2 * m + q
                if not first:
                    sp.wait_ge(xs, b - 1)
                    sp.nop(nofuse=True)
                if kind == 0:
                    sp.dma_start(xin[:, q, :], src_rows(env["x_p"], b)).then_inc(xl[q], 16)
                else:
                    sp.dma_start(sin[:, q, :], src_rows(env["skip_d"][kind - 1], b)).then_inc(xl[q], 16)
                if kind == 2:
                    sp.dma_start(xin[:, q, :], src_rows(env["x_p"], b)).then_inc(xl[q], 16)

            for q in range(2):
                load(0, q, True)
            with sp.Fori(1, NP) as m:
                for q in range(2):
                    load(m, q, False)

        @block.tensor
        def _(pe):
            if kind == 2:
                return

            def body(m, q, first):
                b = 2 * m + q
                pe.wait_ge(xs, b + 1)
                if not first:
                    pe.wait_ge(hs, b - 1)
                pe.transpose(pT[:, q, 0:D], xn[:, q, :] if kind == 0 else hin[:, q, :], ident[:, :]).then_inc(tt, 1)
                pe.wait_ge(hs, b + 1)
                if not first:
                    pe.wait_ge(qd, b - 1)
                pe.matmul(pp[:, q, :], hT[:, q, :], w4[:, :], start=True, stop=True).then_inc(mm, 1)

            pe.wait_ge(wl, 16 * (10 if kind else 9))
            body(0, 0, True)
            body(0, 1, True)
            with pe.Fori(1, NP) as m:
                body(m, 0, False)
                body(m, 1, False)

        @block.scalar
        def _(act):
            act.wait_ge(ez, 1)

            def body(m, q, first):
                b = 2 * m + q
                if kind != 1:
                    act.wait_ge(ch, per * b + nv)
                    act.activation(sd[:, q, :], mv[:, q, 1:2], ACT.Sqrt, bias=eps[:, 0:1]).then_inc(sq, 1)
                if kind < 2:
                    act.wait_ge(tt, b + 1)
                    if not first:
                        act.wait_ge(mm, b - 1)
                    act.activation(hT[:, q, :], pT[:, q, 0:D], ACT.Relu if kind == 0 else ACT.Copy).then_inc(hs, 1)

            body(0, 0, True)
            body(0, 1, True)
            with act.Fori(1, NP) as m:
                body(m, 0, False)
                body(m, 1, False)

        @block.gpsimd
        def _(pool):
            def body(m, q):
                b = 2 * m + q
                pool.wait_ge(kd, b + 1)
                pool.nop(nofuse=True)
                if kind < 2:
                    pool.dma_start(src_rows(env["kv_d"][kind], b), kvs[:, q, 0:2 * D]).then_inc(st[q], 16)
                    pool.dma_start(src_rows(env["skip_d"][kind], b), kvs[:, q, 2 * D:3 * D]).then_inc(st[q], 16)
                else:
                    pool.dma_start(src_rows(env["h_d"], b), hp[:, q, :]).then_inc(st[q], 16)
                    pool.dma_start(src_rows(env["x1_d"], b), x1[:, q, :]).then_inc(st[q], 16)

            with pool.Fori(0, NP) as m:
                body(m, 0)
                body(m, 1)
            for q in range(2):
                pool.wait_ge(st[q], 32 * NP)

        @block.vector
        def _(dve):
            dve.memset(eps[:, :], EPS).then_inc(ez, 1)
            dve.wait_ge(wl, 16 * {0: 9, 1: 10, 2: 1}[kind])

            def body(m, q, first):
                b = 2 * m + q
                n = [0]

                def link(ins):
                    n[0] += 1
                    ins.then_inc(ch, 1)
                    dve.wait_ge(ch, per * b + n[0])

                dve.wait_ge(xl[q], 16 * loads * (m + 1))
                x = xin[:, q, :]
                if kind > 0:
                    ob = otab[:, bass.ds(b * OW, OW)]
                    link(dve.tensor_scalar(den[:, q, :], otab[:, bass.ds(b * OW + D, H)], 1e-30, None, ALU.max))
                    link(dve.reciprocal(rec[:, q, :], den[:, q, :]))
                    link(dve.tensor_tensor(pwr[:, q, :], otab[:, bass.ds(b * OW + D + H, H)], rec[:, q, :], ALU.mult))
                    r4 = rec[:, q, :].unsqueeze(2).to_broadcast((P, H, CH))
                    p4 = pwr[:, q, :].unsqueeze(2).to_broadcast((P, H, CH))
                    link(dve.tensor_tensor(t1[:, q, :].rearrange("p (h c) -> p h c", h=H),
                                           otab[:, bass.ds(b * OW, D)].rearrange("p (h c) -> p h c", h=H), r4, ALU.mult))
                    link(dve.tensor_tensor(t2[:, q, :].rearrange("p (h c) -> p h c", h=H),
                                           we_o[:, :].rearrange("p (h c) -> p h c", h=H), p4, ALU.mult))
                    link(dve.tensor_tensor(t1[:, q, :], t1[:, q, :], t2[:, q, :], ALU.add))
                    if kind == 1:
                        if not first:
                            dve.wait_ge(tt, b - 1)
                        dve.tensor_tensor(hin[:, q, :], t1[:, q, :], sin[:, q, :], ALU.add).then_inc(xs, 1)
                    else:
                        if not first:
                            dve.wait_ge(st[q], 32 * m)
                        link(dve.tensor_tensor(t1[:, q, :], t1[:, q, :], sin[:, q, :], ALU.add))
                        link(dve.tensor_tensor(x1[:, q, :], t1[:, q, :], xin[:, q, :], ALU.add))
                        x = x1[:, q, :]
                if kind != 1:
                    link(dve.bn_stats(stat[:, q, :], x))
                    dve.nop(nofuse=True)
                    link(dve.bn_aggr(mv[:, q, :], stat[:, q, :]))
                    dve.wait_ge(sq, b + 1)
                    link(dve.reciprocal(rs[:, q, :], sd[:, q, :]))
                    if kind == 0 and not first:
                        dve.wait_ge(tt, b - 1)
                    dve.tensor_scalar(xn[:, q, :], x, mv[:, q, 0:1], rs[:, q, 0:1], ALU.subtract, ALU.mult).then_inc(xs, 1)
                if kind == 2:
                    dve.wait_ge(xs, b + 1)
                    dve.tensor_scalar(hp[:, q, 0:MUL], xn[:, q, 0:MUL], 0.0, None, ALU.max)
                    dve.tensor_scalar(hp[:, q, MUL:D].rearrange("p (i u) -> p i u", i=3),
                                      xn[:, q, MUL:D].rearrange("p (u i) -> p i u", i=3), 0.0, None,
                                      ALU.max).then_inc(kd, 1)
                else:
                    dve.wait_ge(mm, b + 1)
                    if not first:
                        dve.wait_ge(st[q], 32 * m)
                    dve.tensor_tensor(kvs[:, q, :], pp[:, q, D:4 * D], bias[:, D:4 * D], ALU.add).then_inc(kd, 1)
                    qb = qtab[:, bass.ds(b * QW, D)]
                    dve.tensor_tensor(qb, pp[:, q, 0:D], bias[:, 0:D], ALU.add).then_inc(qd, 1)
                    dve.wait_ge(qd, b + 1)
                    dve.tensor_tensor(qe[:, q, :], qb, we_q[:, :], ALU.mult).then_inc(qq, 1)
                    dve.wait_ge(qq, b + 1)
                    dve.tensor_reduce(qtab[:, bass.ds(b * QW + D, H)],
                                      qe[:, q, :].rearrange("p (h c) -> p h c", h=H), AX.X, ALU.add)
            body(0, 0, True)
            body(0, 1, True)
            with dve.Fori(1, NP) as m:
                body(m, 0, False)
                body(m, 1, False)
            if kind < 2:
                dve.memset(otab[:, :], 0.0)



def attention_sems(sem):
    names = ("oh", "ohT", "ohTc", "qmm", "prod", "qwe", "red", "al1", "alpha", "d4", "aT", "dTs", "pen", "scan1",
             "rowsT", "rw", "rowv", "cr", "fe", "fac", "cols", "cin", "scan2", "mx", "mT", "da", "p", "pp", "pw",
             "ohf", "vp", "vals", "agg", "oadd", "facps", "facn", "resc", "init")
    s = {k: sem("a_" + k) for k in names}
    for k in ("idx", "dl", "bA", "w", "bB"):
        s["ld_" + k] = [sem(f"a_ld_{k}{q}") for q in range(2)]
    s["kv"] = [[sem(f"a_kv{q}_{c}") for c in range(NCH)] for q in range(2)]
    return s


def attention_pass(nc, env, L):
    G, SP = env["G"], env["SP"]
    ident, ident_b, iota_b = env["ident"], env["ident_b"], env["iota_b"]
    qtab, otab = env["qtab"], env["otab"]
    S = env["att"]
    kv_d = env["kv_d"][L]
    name = f"e{L}_"
    R4 = H * T
    NR = 9
    with ExitStack() as c:
        def sb(nm, shape, dt=F32):
            return c.enter_context(nc.sbuf_tensor(name + nm, shape, dt))

        def psum(nm, shape, dt=F32):
            return c.enter_context(nc.psum_tensor(name + nm, shape, dt))

        kv = sb("kv", [P, 2 * T, 2 * D])
        idx = sb("idx", [P, 2 * T], I32)
        dl = sb("dl", [P, 2, T])
        wq = sb("wq", [P, 2, T])
        bA = sb("bA", [1, 2 * NCH], I32)
        bB = sb("bB", [1, 2 * NCH], I32)
        oh = sb("oh", [P, 2 * T, P], BF16)
        ohT = sb("ohT", [P, 2, C, P])
        ohf = sb("ohf", [P, 2, C, P])
        vals = sb("vals", [P, 2, C, OW])
        prod = sb("prod", [P, C, D])
        alpha = sb("alpha", [P, 2, H, T])
        qw = sb("qw", [P, 2, H, T])
        tmp = sb("tmp", [P, H, T])
        d4 = sb("d4", [P, H, T])
        pp = sb("pp", [P, 2, T, 2 * H])
        dTs = sb("dTs", [R4, P])
        pen = sb("pen", [R4, P + 1])
        f1 = sb("f1", [R4, P])
        b1 = sb("b1", [R4, P])
        cin = sb("cin", [R4, 2])
        mx = sb("mx", [R4, P])
        rw = sb("rw", [1, 4, H, T])
        fx = sb("fx", [1, H, T + 1])
        lx = sb("lx", [1, H, T + 1])
        dlx = sb("dlx", [1, T + 1])
        pc = sb("pc", [1, T])
        ne = sb("ne", [1, T])
        pw = sb("pw", [1, T])
        pwx = sb("pwx", [1, H, T + 1])
        qbx = sb("qbx", [1, H, T])
        bf = sb("bf", [1, H, T])
        cr = sb("cr", [1, 2, H, T])
        dm = sb("dm", [1, H])
        cf = sb("cf", [1, 1])
        fe = sb("fe", [1, H])
        fac = sb("fac", [1, H])
        facn = sb("facn", [P, H])
        one = sb("one", [1, 1])

        ohT_ps = psum("ohT_ps", [P, 2, 1024], BF16)
        q_ps = psum("q_ps", [P, 2, 512])
        agg = psum("agg", [P, 2, 512])
        turn = psum("turn", [P, 512])
        small = psum("small", [P, 512])
        p2 = small[:, 0:R4].rearrange("p (h t) -> p h t", h=H)
        fac_ps = small[:, R4:R4 + H]
        col_ps = small[0:R4, R4 + H:R4 + H + 2]
        row_ps = small[0:1, R4 + H + 2:R4 + H + 2 + 4 * R4]
        aT_ps = turn[0:R4, 0:P]
        dT_ps = turn[0:R4, P:2 * P]
        mT_ps = turn[:, 2 * P:2 * P + R4]

        def done(m, q, per, k):
            return (2 * m + q) * per + (L * G * per + k)

        def nth(m, n):
            return m * n + (L * (G // 2) * n + n)

        def prev(m, q, by=1):
            return (m, q - by) if q - by >= 0 else (m - 1, q - by + 2)

        block = c.enter_context(nc.Block())

        def drive(a_part, b_part, order):
            order(0, 0, True, False, 0)
            order(0, 1, True, True, 1)

        def schedule(eng, iteration):
            iteration(0, 0, True, False, 0)
            iteration(0, 1, True, True, 1)
            with eng.Fori(1, G // 2) as m:
                iteration(m, 0, True, True, 2)
                iteration(m, 1, True, True, 2)
            iteration(G // 2, 0, False, True, 2)

        @block.sync
        def _(sp):
            def load(which, dst, src, m, q):
                sp.dma_start(dst, src).then_inc(S["ld_" + which][q], 16)

            def cols(m, q, n=T):
                return bass.ds((2 * m + q) * n, n)

            def first_loads(m, q):
                load("idx", idx[:, q * T:(q + 1) * T], env["idx_d"][:, cols(m, q)], m, q)
                load("dl", dl[:, q, :], env["dl_d"][:, cols(m, q)], m, q)
                load("bA", bA[:, q * NCH:(q + 1) * NCH], env["brow_d"][0:1, cols(m, q, NCH)], m, q)

            first_loads(0, 0)
            first_loads(0, 1)

            def iteration(m, q, a, b, n):
                if not a:
                    return
                if n >= 1:
                    pm, pq = prev(m, q)
                    nm, nq = (m, 1) if q == 0 else (m + 1, 0)
                    sp.wait_ge(S["prod"], done(pm, pq, NCH, NCH))
                    sp.nop(nofuse=True)
                    sp.wait_ge(S["d4"], done(pm, pq, 1, 1))
                    sp.nop(nofuse=True)
                    first_loads(nm, nq)
                if n == 2:
                    pm, pq = prev(m, q, 2)
                    sp.wait_ge(S["pw"], done(pm, pq, 1, 1))
                    sp.nop(nofuse=True)
                    sp.wait_ge(S["oadd"], done(pm, pq, NCH, NCH))
                    sp.nop(nofuse=True)
                load("w", wq[:, q, :], env["ew_d"][:, cols(m, q)], m, q)
                load("bB", bB[:, q * NCH:(q + 1) * NCH], env["brow_d"][1:2, cols(m, q, NCH)], m, q)

            iteration(0, 0, True, False, 0)
            iteration(0, 1, True, True, 1)
            with sp.Fori(1, G // 2 - 1) as m:
                iteration(m, 0, True, True, 2)
                iteration(m, 1, True, True, 2)
            m = G // 2 - 1
            iteration(m, 0, True, True, 2)
            pm, pq = prev(m, 1, 2)
            sp.wait_ge(S["pw"], done(pm, pq, 1, 1))
            sp.nop(nofuse=True)
            sp.wait_ge(S["oadd"], done(pm, pq, NCH, NCH))
            sp.nop(nofuse=True)
            load("w", wq[:, 1, :], env["ew_d"][:, cols(m, 1)], m, 1)
            load("bB", bB[:, NCH:2 * NCH], env["brow_d"][1:2, cols(m, 1, NCH)], m, 1)

        @block.gpsimd
        def _(pool):
            def gathers(m, q, first):
                for ch in range(NCH):
                    if not first:
                        pm, pq = prev(m, q, 2)
                        pool.wait_ge(S["vals"], done(pm, pq, NCH, ch + 1))
                    if ch == 0:
                        pool.wait_ge(S["ld_idx"][q], nth(m, 16))
                    pool.nop(nofuse=True)
                    for r in range(C):
                        s = q * T + ch * C + r
                        pool.indirect_dma_start(
                            out=kv[:, s, :], out_offset=None, in_=kv_d,
                            in_offset=bass.IndirectOffsetOnAxis(ap=idx[:, s:s + 1], axis=0)).then_inc(S["kv"][q][ch], 16)

            gathers(0, 0, True)
            gathers(0, 1, True)
            with pool.Fori(1, G // 2) as m:
                gathers(m, 0, False)
                gathers(m, 1, False)

        @block.tensor
        def _(pe):
            def turn_onehot(m, q, ch):
                pe.wait_ge(S["oh"], done(m, q, NCH, ch + 1))
                for r in range(C):
                    last = pe.transpose(ohT_ps[:, ch % 2, r * P:(r + 1) * P], oh[:, q * T + ch * C + r, :], ident_b[:, :])
                last.then_inc(S["ohT"], 1)

            def q_rows(m, q, ch):
                if ch == 0:
                    pe.wait_ge(S["ld_bA"][q], nth(m, 16))
                    pe.nop(nofuse=True)
                col = nc.values_load(bA[0:1, q * NCH + ch:q * NCH + ch + 1], engines=(mybir.EngineType.PE,), min_val=0,
                                     max_val=(env["NBE"] - 1) * QW, skip_runtime_bounds_check_because=CLAMPED)
                pe.wait_ge(S["ohTc"], done(m, q, NCH, ch + 1))
                for r in range(C):
                    last = pe.matmul(q_ps[:, ch % 2, r * QW:r * QW + D + H], ohT[:, ch % 2, r, :],
                                     qtab[:, bass.ds(col, D + H)], start=True, stop=True)
                last.then_inc(S["qmm"], 1)

            def sums(m, q, ch):
                pe.wait_ge(S["vp"], done(m, q, NCH, ch + 1))
                pe.wait_ge(S["vals"], done(m, q, NCH, ch + 1))
                for r in range(C):
                    last = pe.matmul(agg[:, ch % 2, 0:OW], ohf[:, ch % 2, r, :], vals[:, ch % 2, r, :],
                                     start=(r == 0), stop=(r == C - 1))
                last.then_inc(S["agg"], 1)

            def iteration(m, q, a, b, n):
                hm, hq = prev(m, q)
                if n == 0:
                    turn_onehot(m, q, 0)
                for ch in range(NCH):
                    if a and ch + 1 < NCH:
                        turn_onehot(m, q, ch + 1)
                    elif a:
                        nm, nq = (m, 1) if q == 0 else (m + 1, 0)
                        last_group = isinstance(m, int) and 2 * m + q == G - 1
                        if not last_group:
                            turn_onehot(nm, nq, 0)
                    if a:
                        q_rows(m, q, ch)
                    if b and ch == 0:
                        pe.wait_ge(S["alpha"], done(hm, hq, 1, 1))
                        pe.wait_ge(S["d4"], done(hm, hq, 1, 1))
                        pe.transpose(aT_ps, alpha[:, hq, :, :].rearrange("p h t -> p (h t)"), ident[:, :])
                        pe.transpose(dT_ps, d4[:, :, :].rearrange("p h t -> p (h t)"), ident[:, :]).then_inc(S["aT"], 1)
                    if b and ch == 1:
                        pe.wait_ge(S["scan1"], done(hm, hq, 2, 2))
                        for j, col in enumerate((f1[:, P - 1:P], b1[:, 0:1], dTs[:, 0:1], dTs[:, P - 1:P])):
                            last = pe.transpose(row_ps[0:1, j * R4:(j + 1) * R4], col, ident[0:R4, 0:R4])
                        last.then_inc(S["rowsT"], 1)
                    if b and ch == 2:
                        pe.wait_ge(S["cr"], done(hm, hq, 2, 2))
                        for j in range(2):
                            last = pe.matmul(col_ps[:, j:j + 1], cr[0:1, j, :, :].rearrange("p h t -> p (h t)"), one[0:1, 0:1],
                                             start=True, stop=True)
                        last.then_inc(S["cols"], 1)
                    if b and ch == 3:
                        pe.wait_ge(S["mx"], done(hm, hq, 1, 1))
                        pe.transpose(mT_ps, mx[:, :], ident[0:R4, 0:R4]).then_inc(S["mT"], 1)
                    if b and ch >= 4:
                        u = 2 * (ch - 4)
                        if u == 0:
                            pe.wait_ge(S["ohf"], done(hm, hq, NCH, 1))
                            pe.wait_ge(S["fac"], done(hm, hq, 1, 1))
                            pe.matmul(fac_ps, ohf[0:1, 0, 0, :], fac[0:1, :], start=True, stop=True).then_inc(S["facps"], 1)
                        sums(hm, hq, u)
                        sums(hm, hq, u + 1)

            iteration(0, 0, True, False, 0)
            iteration(0, 1, True, True, 1)
            with pe.Fori(1, G // 2 - 1) as m:
                iteration(m, 0, True, True, 2)
                iteration(m, 1, True, True, 2)
            iteration(G // 2 - 1, 0, True, True, 2)
            iteration(G // 2 - 1, 1, True, True, 2)
            iteration(G // 2, 0, False, True, 2)

        @block.scalar
        def _(act):
            def copy_ohT(m, q, ch):
                cm, cq = (m, q) if ch >= 2 else prev(m, q)
                act.wait_ge(S["ohT"], done(m, q, NCH, ch + 1))
                if not (isinstance(m, int) and m == 0 and q == 0 and ch < 2):
                    act.wait_ge(S["qmm"], done(cm, cq, NCH, (ch - 2) % NCH + 1))
                act.activation(ohT[:, ch % 2, :, :].rearrange("p r n -> p (r n)"), ohT_ps[:, ch % 2, 0:C * P],
                               ACT.Copy).then_inc(S["ohTc"], 1)

            def iteration(m, q, a, b, n):
                hm, hq = prev(m, q)
                if n == 0:
                    copy_ohT(m, q, 0)
                for ch in range(NCH):
                    if a and ch + 1 < NCH:
                        copy_ohT(m, q, ch + 1)
                    elif a:
                        nm, nq = (m, 1) if q == 0 else (m + 1, 0)
                        if not (isinstance(m, int) and 2 * m + q == G - 1):
                            copy_ohT(nm, nq, 0)
                    if b and ch >= 4:
                        for u in (2 * (ch - 4), 2 * (ch - 4) + 1):
                            cm, cq = (hm, hq) if u >= 2 else prev(hm, hq)
                            first = (n == 1) and u < 2
                            if not first:
                                act.wait_ge(S["agg"], done(cm, cq, NCH, (u - 2) % NCH + 1))
                            act.activation(ohf[:, u % 2, :, :], oh[:, hq * T + u * C:hq * T + (u + 1) * C, :],
                                           ACT.Copy).then_inc(S["ohf"], 1)
                            if u == 0:
                                act.wait_ge(S["pw"], done(hm, hq, 1, 1))
                            act.activation(vals[:, u % 2, :, D:OW], pp[:, hq, u * C:(u + 1) * C, :],
                                           ACT.Copy).then_inc(S["vp"], 1)
                    if a:
                        if ch == 0 and n == 2:
                            pm, pq = prev(m, q, 2)
                            act.wait_ge(S["alpha"], done(pm, pq, 1, 1))
                        act.wait_ge(S["prod"], done(m, q, NCH, ch + 1))
                        act.activation(qw[:, q, :, ch * C:(ch + 1) * C].rearrange("p h r -> p r h"),
                                       q_ps[:, ch % 2, 0:C * QW].rearrange("p (r w) -> p r w", w=QW)[:, :, D:D + H],
                                       ACT.Copy).then_inc(S["qwe"], 1)
                    if b and ch == 0:
                        act.wait_ge(S["aT"], done(hm, hq, 1, 1))
                        act.activation(dTs[:, :], dT_ps, ACT.Copy, scale=KEY).then_inc(S["dTs"], 1)
                    if b and ch == 1:
                        act.wait_ge(S["rowsT"], done(hm, hq, 1, 1))
                        act.activation(rw[0:1, :, :, :].rearrange("p k h t -> p (k h t)"), row_ps[0:1, 0:4 * R4],
                                       ACT.Copy).then_inc(S["rw"], 1)
                    if b and ch == 2:
                        act.wait_ge(S["cols"], done(hm, hq, 1, 1))
                        act.activation(cin[:, :], col_ps, ACT.Copy).then_inc(S["cin"], 1)
                        act.wait_ge(S["rowv"], done(hm, hq, NR, 8))
                        act.activation(fe[0:1, :], dm[0:1, :], ACT.Exp, scale=SCALE).then_inc(S["fe"], 1)
                    if b and ch == 3:
                        act.wait_ge(S["da"], done(hm, hq, 1, 1))
                        act.activation(p2, tmp[:, :, :], ACT.Exp, scale=SCALE).then_inc(S["p"], 1)
                        act.activation(pp[:, hq, :, 0:H].rearrange("p t h -> p h t"), tmp[:, :, :], ACT.Exp,
                                       scale=SCALE).then_inc(S["pp"], 1)

            iteration(0, 0, True, False, 0)
            iteration(0, 1, True, True, 1)
            with act.Fori(1, G // 2 - 1) as m:
                iteration(m, 0, True, True, 2)
                iteration(m, 1, True, True, 2)
            iteration(G // 2 - 1, 0, True, True, 2)
            iteration(G // 2 - 1, 1, True, True, 2)
            iteration(G // 2, 0, False, True, 2)

        @block.vector
        def _(dve):
            def onehots(m, q, ch, n):
                if ch == 0:
                    dve.wait_ge(S["ld_dl"][q], nth(m, 16))
                if n == 2:
                    pm, pq = prev(m, q, 2)
                    dve.wait_ge(S["ohf"], done(pm, pq, NCH, ch + 1))
                for r in range(C):
                    s = ch * C + r
                    last = dve.tensor_scalar(oh[:, q * T + s, :], iota_b[:, :], dl[:, q, s:s + 1], None, ALU.is_equal)
                last.then_inc(S["oh"], 1)

            def onehots_ahead(m, q, ch, n):
                if ch + 2 < NCH:
                    onehots(m, q, ch + 2, n)
                elif not (isinstance(m, int) and 2 * m + q == G - 1):
                    nm, nq = (m, 1) if q == 0 else (m + 1, 0)
                    onehots(nm, nq, ch + 2 - NCH, 2 if n >= 1 else n)

            def products(m, q, ch):
                if not (isinstance(m, int) and m == 0 and q == 0 and ch == 0):
                    cm, cq = (m, q) if ch else prev(m, q)
                    dve.wait_ge(S["red"], done(cm, cq, NCH, (ch - 1) % NCH + 1))
                dve.wait_ge(S["kv"][q][ch], nth(m, 16 * C))
                dve.wait_ge(S["qmm"], done(m, q, NCH, ch + 1))
                s = q * T + ch * C
                dve.tensor_tensor(prod[:, :, :], kv[:, s:s + C, 0:D],
                                  q_ps[:, ch % 2, 0:C * QW].rearrange("p (r w) -> p r w", w=QW)[:, :, 0:D],
                                  ALU.mult).then_inc(S["prod"], 1)

            def reduces(m, q, ch):
                dve.wait_ge(S["prod"], done(m, q, NCH, ch + 1))
                dve.tensor_reduce(alpha[:, q, :, ch * C:(ch + 1) * C].rearrange("p h r -> p r h"),
                                  prod[:, :, :].rearrange("p r (h c) -> p r h c", h=H), AX.X, ALU.add).then_inc(S["red"], 1)

            def weighted(m, q, ch):
                cm, cq = (m, q) if ch >= 2 else prev(m, q)
                if not (isinstance(m, int) and m == 0 and q == 0 and ch < 2):
                    dve.wait_ge(S["agg"], done(cm, cq, NCH, (ch - 2) % NCH + 1))
                s = q * T + ch * C
                pb = p2[:, :, ch * C:(ch + 1) * C].rearrange("p h r -> p r h").unsqueeze(3).to_broadcast((P, C, H, CH))
                dve.tensor_tensor(vals[:, ch % 2, :, 0:D].rearrange("p r (h c) -> p r h c", h=H),
                                  kv[:, s:s + C, D:2 * D].rearrange("p r (h c) -> p r h c", h=H), pb,
                                  ALU.mult).then_inc(S["vals"], 1)

            def block_column(m, q, ch):
                return nc.values_load(bB[0:1, q * NCH + ch:q * NCH + ch + 1], engines=(mybir.EngineType.DVE,), min_val=0,
                                      max_val=(env["NBE"] - 1) * OW, skip_runtime_bounds_check_because=CLAMPED)

            def add_sums(m, q, ch, col):
                dve.wait_ge(S["agg"], done(m, q, NCH, ch + 1))
                if ch:
                    dve.wait_ge(S["oadd"], done(m, q, NCH, ch))
                else:
                    dve.wait_ge(S["resc"], done(m, q, 2, 2))
                ob = otab[:, bass.ds(col, OW)]
                dve.tensor_tensor(ob, agg[:, ch % 2, 0:OW], ob, ALU.add).then_inc(S["oadd"], 1)

            def scores(m, q):
                dve.wait_ge(S["ld_w"][q], nth(m, 16))
                dve.wait_ge(S["qwe"], done(m, q, NCH, NCH))
                wb = wq[:, q, :].unsqueeze(1).to_broadcast((P, H, T))
                dve.tensor_tensor(tmp[:, :, :], qw[:, q, :, :], wb, ALU.mult).then_inc(S["al1"], 1)
                dve.wait_ge(S["al1"], done(m, q, 1, 1))
                dve.wait_ge(S["red"], done(m, q, NCH, NCH))
                dve.tensor_tensor(alpha[:, q, :, :], alpha[:, q, :, :], tmp[:, :, :], ALU.add).then_inc(S["alpha"], 1)
                dve.tensor_copy(d4[:, :, :], dl[:, q, :].unsqueeze(1).to_broadcast((P, H, T))).then_inc(S["d4"], 1)

            def row_scans(m, q):
                dve.wait_ge(S["dTs"], done(m, q, 1, 1))
                dve.tensor_tensor(pen[:, 1:P], dTs[:, 0:P - 1], dTs[:, 1:P], ALU.subtract).then_inc(S["pen"], 1)
                dve.wait_ge(S["pen"], done(m, q, 1, 1))
                dve.tensor_tensor_scan(f1[:, :], pen[:, 0:P], aT_ps, -BIG, ALU.add, ALU.max).then_inc(S["scan1"], 1)
                dve.tensor_tensor_scan(b1[:, ::-1], pen[:, P:0:-1], aT_ps[:, ::-1], -BIG, ALU.add,
                                       ALU.max).then_inc(S["scan1"], 1)

            def carries(m, q):
                k = [0]

                def link(ins):
                    k[0] += 1
                    ins.then_inc(S["rowv"], 1)
                    dve.wait_ge(S["rowv"], done(m, q, NR, k[0]))

                dve.wait_ge(S["rw"], done(m, q, 1, 1))
                d_first, d_last = rw[0:1, 2, 0, :], rw[0:1, 3, 0, :]
                dve.tensor_copy(fx[0:1, :, 1:T + 1], rw[0:1, 0, :, :])
                link(dve.tensor_copy(dlx[0:1, 1:T + 1], d_last))
                dve.tensor_tensor(pw[0:1, :], d_first, d_last, ALU.subtract)
                link(dve.tensor_tensor(ne[0:1, :], dlx[0:1, 0:T], d_first, ALU.not_equal))
                dve.tensor_scalar(cf[0:1, :], ne[0:1, 0:1], -1.0, 1.0, ALU.mult, ALU.add)
                link(dve.tensor_scalar(pc[0:1, :], ne[0:1, :], -BIG, None, ALU.mult))

                def wide(ap, n):
                    return ap.unsqueeze(1).to_broadcast((1, H, n))

                dve.tensor_tensor(qbx[0:1, :, 0:T - 1], wide(pw[0:1, 0:T - 1], T - 1), wide(pc[0:1, 1:T], T - 1), ALU.add)
                link(dve.tensor_tensor(pwx[0:1, :, 1:T + 1], wide(pw[0:1, :], T), wide(pc[0:1, :], T), ALU.add))
                flat = lambda ap: ap.rearrange("p h t -> p (h t)")
                link(dve.tensor_tensor_scan(flat(bf[0:1, :, :])[:, ::-1], flat(qbx[0:1, :, :])[:, ::-1],
                                            rw[0:1, 1, :, :].rearrange("p h t -> p (h t)")[:, ::-1], -BIG, ALU.add, ALU.max))
                link(dve.tensor_tensor_scan(flat(lx[0:1, :, :]), flat(pwx[0:1, :, :]), flat(fx[0:1, :, :]), 0.0,
                                            ALU.add, ALU.max))
                dve.tensor_tensor(cr[0:1, 1, :, 0:T - 1], bf[0:1, :, 1:T], wide(pc[0:1, 1:T], T - 1), ALU.add).then_inc(S["cr"], 1)
                dve.tensor_tensor(cr[0:1, 0, :, :], lx[0:1, :, 0:T], wide(pc[0:1, :], T), ALU.add).then_inc(S["cr"], 1)
                link(dve.tensor_tensor(dm[0:1, :], fx[0:1, :, 0], bf[0:1, :, 0], ALU.subtract))
                link(dve.tensor_scalar(dm[0:1, :], dm[0:1, :], 0.0, cf[0:1, 0:1], ALU.min, ALU.mult))
                dve.tensor_copy(fx[0:1, :, 0], lx[0:1, :, T])
                link(dve.tensor_copy(dlx[0:1, 0:1], dlx[0:1, T:T + 1]))
                assert k[0] == NR

            def maxima(m, q):
                dve.wait_ge(S["cin"], done(m, q, 1, 1))
                dve.tensor_tensor_scan(f1[:, :], pen[:, 0:P], aT_ps, cin[:, 0:1], ALU.add, ALU.max).then_inc(S["scan2"], 1)
                dve.tensor_tensor_scan(b1[:, ::-1], pen[:, P:0:-1], aT_ps[:, ::-1], cin[:, 1:2], ALU.add,
                                       ALU.max).then_inc(S["scan2"], 1)
                dve.wait_ge(S["scan2"], done(m, q, 2, 2))
                dve.tensor_tensor(mx[:, :], f1[:, :], b1[:, :], ALU.max).then_inc(S["mx"], 1)
                dve.wait_ge(S["fe"], done(m, q, 1, 1))
                dve.tensor_scalar(fac[0:1, :], fe[0:1, :], -1.0, None, ALU.add).then_inc(S["fac"], 1)

            def below_max(m, q):
                dve.wait_ge(S["mT"], done(m, q, 1, 1))
                dve.tensor_tensor(tmp[:, :, :].rearrange("p h t -> p (h t)"), alpha[:, q, :, :].rearrange("p h t -> p (h t)"),
                                  mT_ps, ALU.subtract).then_inc(S["da"], 1)

            def times_weight(m, q):
                dve.wait_ge(S["pp"], done(m, q, 1, 1))
                wb = wq[:, q, :].unsqueeze(2).to_broadcast((P, T, H))
                dve.tensor_tensor(pp[:, q, :, H:2 * H], pp[:, q, :, 0:H], wb, ALU.mult).then_inc(S["pw"], 1)

            def rescale(m, q):
                col = block_column(m, q, 0)
                dve.wait_ge(S["facps"], done(m, q, 1, 1))
                dve.tensor_scalar(facn[:, :], fac_ps, 1.0, None, ALU.add).then_inc(S["facn"], 1)
                dve.wait_ge(S["facn"], done(m, q, 1, 1))
                ov = otab[:, bass.ds(col, D)].rearrange("p (h c) -> p h c", h=H)
                op = otab[:, bass.ds(col + D, 2 * H)].rearrange("p (k h) -> p k h", h=H)
                dve.tensor_tensor(ov, ov, facn[:, :].unsqueeze(2).to_broadcast((P, H, CH)), ALU.mult).then_inc(S["resc"], 1)
                dve.tensor_tensor(op, op, facn[:, :].unsqueeze(1).to_broadcast((P, 2, H)), ALU.mult).then_inc(S["resc"], 1)

            def iteration(m, q, a, b, n):
                hm, hq = prev(m, q)
                if n == 0:
                    onehots(m, q, 0, 0)
                    onehots(m, q, 1, 0)
                for ch in range(NCH):
                    u = 2 * (ch - 4)
                    if b and u >= 0:
                        if u == 0:
                            rescale(hm, hq)
                            dve.wait_ge(S["p"], done(hm, hq, 1, 1))
                        weighted(hm, hq, u)
                    before = prev(hm, hq) + (NCH - 1,) if ch == 0 and n == 2 else (hm, hq, u - 1) if b and u > 0 else None
                    if before:
                        col = block_column(*before)
                    if a:
                        products(m, q, ch)
                        onehots_ahead(m, q, ch, n)
                    if before:
                        add_sums(*before, col)
                    if b and ch == 3:
                        below_max(hm, hq)
                    if b and u >= 0:
                        weighted(hm, hq, u + 1)
                        col = block_column(hm, hq, u)
                    if a:
                        reduces(m, q, ch)
                    if b and u >= 0:
                        add_sums(hm, hq, u, col)
                    if b and ch == 0:
                        row_scans(hm, hq)
                    if b and ch == 1:
                        carries(hm, hq)
                    if b and ch == 2:
                        maxima(hm, hq)
                    if b and ch == 3:
                        dve.wait_ge(S["ld_bB"][hq], nth(hm, 16))
                        times_weight(hm, hq)
                if a:
                    scores(m, q)

            dve.memset(pen[:, :], 0.0)
            dve.memset(fx[0:1, :, :], 0.0)
            dve.memset(dlx[0:1, :], -BIG)
            dve.memset(pwx[0:1, :, :], -BIG)
            dve.memset(qbx[0:1, :, :], -BIG)
            dve.memset(cr[0:1, :, :, :], -BIG)
            dve.memset(one[0:1, :], 1.0).then_inc(S["init"], 1)
            dve.wait_ge(S["init"], L + 1)
            iteration(0, 0, True, False, 0)
            iteration(0, 1, True, True, 1)
            with dve.Fori(1, G // 2 - 1) as m:
                iteration(m, 0, True, True, 2)
                iteration(m, 1, True, True, 2)
            iteration(G // 2 - 1, 0, True, True, 2)
            iteration(G // 2 - 1, 1, True, True, 2)
            iteration(G // 2, 0, False, True, 2)
            col = block_column(G // 2 - 1, 1, NCH - 1)
            add_sums(G // 2 - 1, 1, NCH - 1, col)



def message_pass(nc, sem, env):
    G, NBE = env["G"], env["NBE"]
    iota_b = env["iota_b"]
    mtab = env["mtab"]
    with ExitStack() as c:
        def sb(nm, shape, dt=F32):
            return c.enter_context(nc.sbuf_tensor("m_" + nm, shape, dt))

        hv = sb("hv", [P, 2 * T, D])
        idx = sb("idx", [P, 2 * T], I32)
        dl = sb("dl", [P, 2, T])
        co = sb("co", [P, 2, T, NCOEF])
        bB = sb("bB", [1, 2 * NCH], I32)
        oh = sb("oh", [P, 2, C, P])
        vals = sb("vals", [P, 2, C, MW])
        prod = sb("prod", [P, C, 4, MUL, 3])
        co_ps = c.enter_context(nc.psum_tensor("m_co_ps", [P, 2, 512], F32))
        agg = c.enter_context(nc.psum_tensor("m_agg", [P, 2, 512], F32))
        cp = co_ps[:, :, 0:T * NCOEF].rearrange("p q (t k) -> p q t k", k=NCOEF)

        ld = [sem(f"m_ld{q}") for q in range(2)]
        li = [sem(f"m_li{q}") for q in range(2)]
        hs = env["att"]["kv"]
        earlier = 2 * (G // 2) * 16 * C
        cs = sem("m_coef"); os_ = sem("m_onehot"); a0 = sem("m_a0"); a1 = sem("m_a1"); pr = sem("m_prod")
        rd = sem("m_red"); ag = sem("m_agg_s"); ad = sem("m_add"); z = sem("m_zero")

        def done(m, q, per, k):
            return (2 * m + q) * per + k

        def prev(m, q, by=1):
            return (m, q - by) if q - by >= 0 else (m - 1, q - by + 2)

        block = c.enter_context(nc.Block())

        def whole(eng, group):
            group(0, 0, 0)
            group(0, 1, 1)
            with eng.Fori(1, G // 2) as m:
                group(m, 0, 2)
                group(m, 1, 2)

        def back(m, q, ch):
            return (m, q, ch - 1) if ch >= 2 else (*prev(m, q), NCH + ch - 1)

        @block.sync
        def _(sp):
            def group(m, q, n):
                cols = bass.ds((2 * m + q) * T, T)
                if n == 2:
                    pm, pq = prev(m, q, 2)
                    sp.wait_ge(a1, done(pm, pq, NCH, NCH))
                    sp.nop(nofuse=True)
                sp.dma_start(idx[:, q * T:(q + 1) * T], env["idx_d"][:, cols]).then_inc(li[q], 16)
                if n == 2:
                    sp.wait_ge(ad, done(pm, pq, NCH, NCH))
                    sp.nop(nofuse=True)
                    sp.wait_ge(a0, done(pm, pq, NCH, NCH))
                    sp.nop(nofuse=True)
                    sp.wait_ge(cs, done(pm, pq, 1, 1))
                    sp.nop(nofuse=True)
                sp.dma_start(dl[:, q, :], env["dl_d"][:, cols]).then_inc(ld[q], 16)
                sp.dma_start(co[:, q, :, :], env["coef_d"][:, cols, :]).then_inc(ld[q], 16)
                sp.dma_start(bB[:, q * NCH:(q + 1) * NCH], env["brow_d"][2:3, bass.ds((2 * m + q) * NCH, NCH)]).then_inc(ld[q], 16)
            whole(sp, group)

        @block.gpsimd
        def _(pool):
            def group(m, q, n):
                for ch in range(NCH):
                    if n == 2:
                        pm, pq = prev(m, q, 2)
                        pool.wait_ge(rd, done(pm, pq, T, C * (ch + 1)))
                        pool.wait_ge(a0, done(pm, pq, NCH, ch + 1))
                    if ch == 0:
                        pool.wait_ge(li[q], m * 16 + 16)
                    pool.nop(nofuse=True)
                    for r in range(C):
                        s = q * T + ch * C + r
                        pool.indirect_dma_start(
                            out=hv[:, s, :], out_offset=None, in_=env["h_d"],
                            in_offset=bass.IndirectOffsetOnAxis(ap=idx[:, s:s + 1], axis=0)).then_inc(hs[q][ch], 16)
            whole(pool, group)

        @block.scalar
        def _(act):
            def group(m, q, n):
                act.wait_ge(ld[q], m * 48 + 48)
                if n == 2:
                    pm, pq = prev(m, q, 2)
                    act.wait_ge(rd, done(pm, pq, T, T))
                act.activation(co_ps[:, q, 0:T * NCOEF], co[:, q, :, :].rearrange("p t k -> p (t k)"),
                               ACT.Copy).then_inc(cs, 1)
                for ch in range(NCH):
                    if n or ch >= 2:
                        act.wait_ge(ag, done(*back(m, q, ch)[:2], NCH, back(m, q, ch)[2]))
                    act.wait_ge(hs[q][ch], m * 48 + (48 + earlier))
                    for r in range(C):
                        s = ch * C + r
                        last = act.activation(vals[:, ch % 2, r, 0:D], hv[:, q * T + s, :], ACT.Copy,
                                              scale=co[:, q, s, 12:13])
                    last.then_inc(a0, 1)
            whole(act, group)

        @block.tensor
        def _(pe):
            pe.wait_ge(z, 1)

            def group(m, q, n):
                for ch in range(NCH):
                    pe.wait_ge(a0, done(m, q, NCH, ch + 1))
                    pe.wait_ge(rd, done(m, q, T, C * (ch + 1)))
                    if n or ch >= 2:
                        bm, bq, bc = back(m, q, ch)
                        pe.wait_ge(ad, done(bm, bq, NCH, bc))
                    for r in range(C):
                        last = pe.matmul(agg[:, ch % 2, 0:MW], oh[:, ch % 2, r, :], vals[:, ch % 2, r, :],
                                         start=(r == 0), stop=(r == C - 1))
                    last.then_inc(ag, 1)
            whole(pe, group)

        @block.vector
        def _(dve):
            dve.memset(mtab[:, :], 0.0).then_inc(z, 1)
            dve.wait_ge(z, 1)

            def block_column(m, q, ch):
                return nc.values_load(bB[0:1, q * NCH + ch:q * NCH + ch + 1], engines=(mybir.EngineType.DVE,), min_val=0,
                                      max_val=(NBE - 1) * MW, skip_runtime_bounds_check_because=CLAMPED)

            def add_sums(m, q, ch, col):
                dve.wait_ge(ag, done(m, q, NCH, ch + 1))
                if not (isinstance(m, int) and m == 0 and q == 0 and ch == 0):
                    dve.wait_ge(ad, done(m, q, NCH, ch))
                mb = mtab[:, bass.ds(col, MW)]
                dve.tensor_tensor(mb, agg[:, ch % 2, 0:MW], mb, ALU.add).then_inc(ad, 1)

            def group(m, q, n):
                dve.wait_ge(ld[q], m * 48 + 48)
                dve.wait_ge(cs, done(m, q, 1, 1))
                for ch in range(NCH):
                    if n or ch >= 2:
                        bm, bq, bc = back(m, q, ch)
                        dve.wait_ge(ag, done(bm, bq, NCH, bc))
                    for r in range(C):
                        s = ch * C + r
                        last = dve.tensor_scalar(oh[:, ch % 2, r, :], iota_b[:, :], dl[:, q, s:s + 1], None, ALU.is_equal)
                    last.then_inc(os_, 1)
                    dve.wait_ge(hs[q][ch], m * 48 + (48 + earlier))
                    s0 = ch * C
                    dve.tensor_tensor(vals[:, ch % 2, :, D:D + 96].rearrange("p r (k u) -> p r k u", k=3),
                                      hv[:, q * T + s0:q * T + s0 + C, 0:MUL].unsqueeze(2).to_broadcast((P, C, 3, MUL)),
                                      cp[:, q, s0:s0 + C, 9:12].unsqueeze(3).to_broadcast((P, C, 3, MUL)),
                                      ALU.mult).then_inc(a1, 1)
                    if n or ch:
                        dve.wait_ge(rd, done(m, q, T, s0))
                    for r in range(C):
                        dve.tensor_tensor(prod[:, r, :, :, :],
                                          hv[:, q * T + s0 + r, MUL:D].rearrange("p (i u) -> p u i", i=3).unsqueeze(1)
                                          .to_broadcast((P, 4, MUL, 3)),
                                          cp[:, q, s0 + r, 0:12].rearrange("p (k i) -> p k i", i=3).unsqueeze(2)
                                          .to_broadcast((P, 4, MUL, 3)), ALU.mult).then_inc(pr, 1)
                    before = (m, q, ch - 1) if ch else (*prev(m, q), NCH - 1) if n else None
                    if before:
                        col = block_column(*before)
                        add_sums(*before, col)
                    for r in range(C):
                        dve.wait_ge(pr, done(m, q, T, s0 + r + 1))
                        dve.tensor_reduce(vals[:, ch % 2, r, D + 96:MW].rearrange("p (k u) -> p k u", k=4),
                                          prod[:, r, :, :, :], AX.X, ALU.add).then_inc(rd, 1)

            whole(dve, group)
            col = block_column(G // 2 - 1, 1, NCH - 1)
            add_sums(G // 2 - 1, 1, NCH - 1, col)



def final_phase(nc, sem, env):
    NBE = env["NBE"]
    ident, mtab = env["ident"], env["mtab"]
    W = env["weights"]
    r10 = 1.0 / float(np.sqrt(10.0))
    n0 = float(np.sqrt(1.0 / 64)) * r10
    n1 = float(np.sqrt(3.0 / 96)) * r10
    r3 = 1.0 / float(np.sqrt(3.0))
    cst = [n0, n1 * r3, n1 * r3, n0 * r3, n1]
    rows = ([(0, 0, 0, 1)] + [(32 + 32 * k, 2, 32 + k, 3) for k in range(3)] + [(128 + 32 * k, 1, 32 + k, 3) for k in range(3)]
            + [(224 + 32 * k, 4, 32 + k, 3) for k in range(3)] + [(320, 3, 0, 1)])
    with ExitStack() as c:
        def sb(nm, shape, dt=F32):
            return c.enter_context(nc.sbuf_tensor("f_" + nm, shape, dt))

        wraw = sb("wraw", [P, 3, MUL])
        wbig = sb("wbig", [P, 3, D])
        mT = sb("mT", [P, 2, 3, P])
        rows_now = sb("rows_now", [P, 2, MW])
        x1 = sb("x1", [P, 2, D])
        y = sb("y", [P, 2, D])
        pT = c.enter_context(nc.psum_tensor("f_pT", [P, 2, 512], F32))
        po = c.enter_context(nc.psum_tensor("f_po", [P, 2, 512], F32))
        wl = sem("f_wl"); wz = sem("f_wz"); wb = sem("f_wb"); xl = [sem(f"f_x{q}") for q in range(2)]
        rn = sem("f_rows"); tt = sem("f_tr"); mc = sem("f_mT"); mm = sem("f_mm"); ys = sem("f_y"); st = [sem(f"f_st{q}") for q in range(2)]
        block = c.enter_context(nc.Block())
        NP = NBE // 2
        KS = (128, 128, 96)

        def loop(eng, body):
            body(0, 0, True)
            body(0, 1, True)
            with eng.Fori(1, NP) as m:
                body(m, 0, False)
                body(m, 1, False)

        @block.sync
        def _(sp):
            for r, k, _, _ in rows:
                sp.dma_start(wraw[r % P:r % P + MUL, r // P, :], W[f"w{k}"]).then_inc(wl, 16)

            def body(m, q, first):
                b = 2 * m + q
                if not first:
                    sp.wait_ge(ys, b - 1)
                    sp.nop(nofuse=True)
                sp.dma_start(x1[:, q, :], env["x1_d"][bass.ds(b * P, P), :]).then_inc(xl[q], 16)
            loop(sp, body)

        @block.gpsimd
        def _(pool):
            def body(m, q, first):
                b = 2 * m + q
                pool.wait_ge(ys, b + 1)
                pool.nop(nofuse=True)
                pool.dma_start(env["out"][bass.ds(b * P, P), :], y[:, q, :]).then_inc(st[q], 16)
            loop(pool, body)
            for q in range(2):
                pool.wait_ge(st[q], 16 * NP)

        @block.tensor
        def _(pe):
            pe.wait_ge(wb, len(rows))

            def body(m, q, first):
                b = 2 * m + q
                pe.wait_ge(rn, b + 1)
                if not first:
                    pe.wait_ge(mc, b - 1)
                for j, k in enumerate(KS):
                    last = pe.transpose(pT[0:k, q, j * P:(j + 1) * P], rows_now[:, q, j * P:j * P + k], ident[:, :])
                last.then_inc(tt, 1)
                pe.wait_ge(mc, b + 1)
                if not first:
                    pe.wait_ge(ys, b - 1)
                for j, k in enumerate(KS):
                    last = pe.matmul(po[:, q, 0:D], mT[0:k, q, j, :], wbig[0:k, j, :], start=(j == 0), stop=(j == 2))
                last.then_inc(mm, 1)
            loop(pe, body)

        @block.scalar
        def _(act):
            def body(m, q, first):
                b = 2 * m + q
                act.wait_ge(tt, b + 1)
                if not first:
                    act.wait_ge(mm, b - 1)
                act.activation(mT[:, q, 0:2, :].rearrange("p j n -> p (j n)"), pT[:, q, 0:2 * P], ACT.Copy)
                act.activation(mT[0:96, q, 2, :], pT[0:96, q, 2 * P:3 * P], ACT.Copy).then_inc(mc, 1)
            loop(act, body)

        @block.vector
        def _(dve):
            dve.memset(wbig[:, :, :], 0.0).then_inc(wz, 1)
            dve.wait_ge(wz, 1)
            dve.wait_ge(wl, 16 * len(rows))
            for r, k, col, step in rows:
                o = wbig[r % P:r % P + MUL, r // P, col:col + step * (MUL - 1) + 1:step]
                dve.tensor_scalar(o, wraw[r % P:r % P + MUL, r // P, :], cst[k], None, ALU.mult).then_inc(wb, 1)

            def body(m, q, first):
                b = 2 * m + q
                if not first:
                    dve.wait_ge(tt, b - 1)
                dve.tensor_copy(rows_now[:, q, :], mtab[:, bass.ds(b * MW, MW)]).then_inc(rn, 1)
                dve.wait_ge(mm, b + 1)
                dve.wait_ge(xl[q], 16 * m + 16)
                if not first:
                    dve.wait_ge(st[q], 16 * m)
                dve.tensor_tensor(y[:, q, :], po[:, q, 0:D], x1[:, q, :], ALU.add).then_inc(ys, 1)
            loop(dve, body)



def kernel(**inputs):
    import numpy as _np
    import concourse.bacc as _bacc
    from concourse import mybir as _mybir
    from concourse.bass_utils import run_bass_kernel_spmd as _run

    x = _np.asarray(inputs["x"])
    n_nodes, n_edges = x.shape[0], inputs["src"].shape[0]
    NBE, NT, _, _ = sizes(n_nodes, n_edges)

    def triples(a, fill):
        a = _np.asarray(a)
        out = _np.full(((NT + 1) * C * P,) + a.shape[1:], fill, a.dtype)
        out[:n_edges] = a
        return out.reshape((NT + 1, C * P) + a.shape[1:])

    x_p = _np.zeros((NBE * P, D), x.dtype)
    x_p[:n_nodes] = x
    dst_t = triples(inputs["dst"], (NBE + 1) * P)
    arrays = {
        "x_p": x_p,
        "src_t": triples(inputs["src"], 0),
        "dst_t": dst_t,
        "dlast": _np.ascontiguousarray(dst_t[:NT, -1][None, :]),
        "ew_t": triples(inputs["edge_weight"], 0),
        "attr_t": _np.ascontiguousarray(triples(inputs["edge_attr_9"], 0).transpose(0, 2, 1)).reshape(NT + 1, 9 * C * P),
    }
    wnames = {}
    for l in (1, 2):
        for k in ("Wq", "bq", "Wk", "bk", "Wv", "bv", "We", "Ws", "bs"):
            wnames[f"{k}{l}"] = f"L0_gnn_{k}{l}"
    for k in range(5):
        wnames[f"w{k}"] = f"L1_gnn_w{k}"
    for short, full in wnames.items():
        a = _np.ascontiguousarray(inputs[full])
        arrays["in_" + short] = a.reshape(MUL, MUL) if full.startswith("L1") else a

    nc = _bacc.Bacc("TRN2", target_bir_lowering=False, num_devices=1)
    aps = {n: nc.dram_tensor(n, a.shape, _mybir.dt.from_np(a.dtype), kind="ExternalInput").ap() for n, a in arrays.items()}
    out = nc.dram_tensor("out", (NBE * P, D), F32, kind="ExternalOutput").ap()
    weights = {short: aps["in_" + short] for short in wnames}
    weights["n_nodes"], weights["n_edges"] = n_nodes, n_edges
    build(nc, aps["x_p"], aps["src_t"], aps["dst_t"], aps["dlast"], aps["ew_t"], aps["attr_t"], weights, out)
    r = _run(nc, [arrays], core_ids=[0])
    return r.results[0]["out"][:n_nodes]
```

```python
from contextlib import ExitStack
from math import factorial

import numpy as np
import concourse.bass as bass
from concourse import mybir

ALU = mybir.AluOpType
ACT = mybir.ActivationFunctionType
AX = mybir.AxisListType
F32 = mybir.dt.float32
BF16 = mybir.dt.bfloat16
I32 = mybir.dt.int32

P = 128
D = 128
H = 4
CH = D // H
MUL = 32
T = 24
C = 3
NCH = T // C
QW = 136
OW = 136
MW = 352
NCOEF = 13
BIG = 1e38
KEY = 1e33
EPS = 1e-5
SCALE = float(1.0 / np.sqrt(np.float32(CH)))


CLAMPED = "the block numbers are clamped to 0 .. blocks - 1 where they are made"


def ceil_div(a, b):
    return (a + b - 1) // b


def sizes(n_nodes, n_edges):
    nb = ceil_div(n_nodes, P)
    nt = ceil_div(n_edges, C * P)
    groups = ceil_div(nt + nb - 1, NCH)
    groups += groups % 2
    return nb + nb % 2, nt, groups, ceil_div(groups * NCH, P)


def blocks_per_batch(nbe):
    return max(k for k in range(1, 8) if nbe % (2 * k) == 0 and nbe // k >= 6)


def wigner_112():
    def ratio(a, b):
        return float(a) / float(b)

    def coeff(j1, m1, j2, m2, j3, m3):
        vmin = int(max(-j1 + j2 + m3, -j1 + m1, 0))
        vmax = int(min(j2 + j3 + m1, j3 - j1 + j2, j3 + m3))
        f = lambda n: factorial(round(n))
        c = ((2.0 * j3 + 1.0) * ratio(f(j3 + j1 - j2) * f(j3 - j1 + j2) * f(j1 + j2 - j3) * f(j3 + m3) * f(j3 - m3),
                                         f(j1 + j2 + j3 + 1) * f(j1 - m1) * f(j1 + m1) * f(j2 - m2) * f(j2 + m2))) ** 0.5
        s = 0
        for v in range(vmin, vmax + 1):
            s += (-1) ** (v + j2 + m2) * ratio(f(j2 + j3 + m1 - v) * f(j1 - m1 + v),
                                                  f(v) * f(j3 - j1 + j2 - v) * f(j3 + m3 - v) * f(v + j1 - j2 - m3))
        return float(c * s)

    def basis(l):
        q = np.zeros((2 * l + 1, 2 * l + 1), dtype=np.complex128)
        for m in range(-l, 0):
            q[l + m, l + abs(m)] = 1 / np.sqrt(2)
            q[l + m, l - abs(m)] = -1j / np.sqrt(2)
        q[l, l] = 1
        for m in range(1, l + 1):
            q[l + m, l + abs(m)] = (-1) ** m / np.sqrt(2)
            q[l + m, l - abs(m)] = 1j * (-1) ** m / np.sqrt(2)
        return (-1j) ** l * q

    c = np.zeros((3, 5, 3))
    for m1 in range(-1, 2):
        for m2 in range(-2, 3):
            if abs(m1 + m2) <= 1:
                c[1 + m1, 2 + m2, 1 + m1 + m2] = coeff(1, m1, 2, m2, 1, m1 + m2)
    r = np.real(np.einsum('ij,kl,mn,ikn->jlm', basis(1), basis(2), np.conj(basis(1).T), c.astype(np.complex128)))
    return r / np.linalg.norm(r)


def build(nc, x_p, src_t, dst_t, dlast, ew_t, attr_t, weights, out):
    n_rows = x_p.shape[0]
    n_nodes = weights["n_nodes"]
    n_edges = weights["n_edges"]
    NBE, NT, G, NBLK = sizes(n_nodes, n_edges)
    SP = NBLK * P * C
    assert n_rows == NBE * P and src_t.shape[0] == NT + 1 and G >= 6 and NBE >= 4

    def scratch(name, shape, dt):
        return nc.dram_tensor(name, shape, dt, kind="Internal").ap()

    idx_d = scratch("slot_src", (P, SP), I32)
    dl_d = scratch("slot_dloc", (P, SP), F32)
    ew_d = scratch("slot_ew", (P, SP), F32)
    coef_d = scratch("slot_coef", (P, SP, NCOEF), F32)
    brow_d = scratch("chunk_block", (3, NBLK * P), I32)
    kv_d = [scratch(f"kv{l}", (NBE * P, 2 * D), F32) for l in range(2)]
    skip_d = [scratch(f"skip{l}", (NBE * P, D), F32) for l in range(2)]
    h_d = scratch("h_planar", (NBE * P, D), F32)
    x1_d = scratch("x1", (NBE * P, D), F32)

    with ExitStack() as top:
        def sem(name):
            return top.enter_context(nc.semaphore(name))

        ident = top.enter_context(nc.sbuf_tensor("ident", [P, P], F32))
        ident_b = top.enter_context(nc.sbuf_tensor("ident_b", [P, P], BF16))
        iota_b = top.enter_context(nc.sbuf_tensor("iota_b", [P, P], BF16))
        iota_i = top.enter_context(nc.sbuf_tensor("iota_i", [P, P], I32))
        step_tables(nc, sem, locals())
        att = attention_sems(sem)
        with ExitStack() as mid:
            qtab = mid.enter_context(nc.sbuf_tensor("qtab", [P, NBE * QW], F32))
            otab = mid.enter_context(nc.sbuf_tensor("otab", [P, NBE * OW], F32))
            env = dict(locals())
            env["att"] = att
            node_phase(nc, sem, env, 0)
            attention_pass(nc, env, 0)
            node_phase(nc, sem, env, 1)
            attention_pass(nc, env, 1)
            node_phase(nc, sem, env, 2)
        with ExitStack() as mid:
            mtab = mid.enter_context(nc.sbuf_tensor("mtab", [P, NBE * MW], F32))
            env = dict(locals())
            message_pass(nc, sem, env)
            final_phase(nc, sem, env)



def step_tables(nc, sem, env):
    NT, NBLK = env["NT"], env["NBLK"]
    n_nodes = env["n_nodes"]
    nb = ceil_div(n_nodes, P)
    ident, ident_b, iota_b, iota_i = env["ident"], env["ident_b"], env["iota_b"], env["iota_i"]
    W3 = wigner_112()
    terms = {(i, k): [(j, float(W3[i, j, k])) for j in range(5) if abs(W3[i, j, k]) > 1e-9]
             for i in range(3) for k in range(3)}
    N_TWO = sum(len(t) == 2 for t in terms.values())
    R = C * P
    with ExitStack() as c:
        def sb(name, shape, dt=F32):
            return c.enter_context(nc.sbuf_tensor(name, shape, dt))

        last_i = sb("last_i", [P, NT], I32)
        tile_i = sb("tile_i", [P, NT], I32)
        step_i = sb("step_i", [P, NBLK], I32)
        last_m = sb("last_m", [P, NT], I32)
        last_b = sb("last_b", [P, NT], I32)
        last_f = sb("last_f", [P, NT])
        tile_f = sb("tile_f", [P, NT])
        end_f = sb("end_f", [P, NT])
        lt = sb("lt", [P, NT])
        step_f = sb("step_f", [P, NBLK])
        t_f = sb("t_f", [P, NBLK])
        t_i = sb("t_i", [P, NBLK], I32)
        b_f = sb("b_f", [P, NBLK])
        b_n = sb("b_n", [P, NBLK])
        b_s = sb("b_s", [P, 3, NBLK])
        b_rows = sb("b_rows", [NBLK, 3, P], I32)
        rows_s = sb("rows_s", [P, 2, R], I32)
        rows_d = sb("rows_d", [P, 2, R], I32)
        rows_w = sb("rows_w", [P, 2, R])
        rows_a = sb("rows_a", [P, 2, 9 * R])
        rows_sf = sb("rows_sf", [P, R])
        rows_df = sb("rows_df", [P, R])
        rows_dl = sb("rows_dl", [P, R])
        o_src = sb("o_src", [P, 2, P, C], I32)
        o_dl = sb("o_dl", [P, 2, P, C])
        o_w = sb("o_w", [P, 2, P, C])
        o_at = sb("o_at", [P, 9, P, C])
        second = sb("second", [P, N_TWO, R])
        o_co = sb("o_co", [P, 2, P * C, NCOEF])
        ps = [c.enter_context(nc.psum_tensor(f"pt{i}", [P, 4, P], F32)) for i in range(3)]
        pa = [c.enter_context(nc.psum_tensor(f"pa{i}", [P, 4, P], F32)) for i in range(4)]

        consts = sem("pre_consts"); consts0 = sem("pre_consts0"); dl_in = sem("pre_last"); cd = sem("pre_calc")
        bt = sem("pre_bt"); br = sem("pre_br"); bout = sem("pre_bout")
        gat = [sem(f"pre_gather{q}") for q in range(2)]
        rf = sem("pre_rowsf"); tr = sem("pre_tr"); ev = sem("pre_ev")
        atc = sem("pre_attr"); coz = sem("pre_coef"); tw = sem("pre_two")
        st = [sem(f"pre_store{q}") for q in range(2)]
        block = c.enter_context(nc.Block())
        T_READY = 10 + NBLK
        B_READY = 14 + NBLK

        single = [(3 * kk + i, 4 + terms[i, kk][0][0], terms[i, kk][0][1]) for kk in range(3) for i in range(3)
                  if len(terms[i, kk]) == 1] + [(9 + i, 1 + i, 1.0) for i in range(3)] + [(12, 0, 1.0)]

        def at(a):
            return o_at[:, a, :, :].rearrange("p n r -> p (n r)")

        @block.gpsimd
        def _(pool):
            pool.memset(ident[:, :], 0.0).then_inc(consts0, 1)
            pool.iota(iota_i[:, :], pattern=[[1, P]], base=0, channel_multiplier=0).then_inc(consts, 1)
            pool.iota(tile_i[:, :], pattern=[[1, NT]], base=0, channel_multiplier=0).then_inc(consts, 1)
            pool.iota(step_i[:, :], pattern=[[P, NBLK]], base=0, channel_multiplier=1).then_inc(consts, 1)
            pool.wait_ge(consts0, 1)
            pool.affine_select(out=ident[:, :], in_=ident[:, :], compare_op=ALU.not_equal, fill=1.0, base=0,
                               pattern=[[-1, P]], channel_multiplier=1).then_inc(consts, 1)
            pool.wait_ge(cd, T_READY)
            for k in range(NBLK):
                if k >= 2:
                    pool.wait_ge(tr, C * (k - 1))
                for buf, tab in ((rows_s, "src_t"), (rows_d, "dst_t"), (rows_w, "ew_t"), (rows_a, "attr_t")):
                    pool.indirect_dma_start(out=buf[:, k % 2, :], out_offset=None, in_=env[tab],
                                            in_offset=bass.IndirectOffsetOnAxis(ap=t_i[:, k:k + 1], axis=0))\
                        .then_inc(gat[k % 2], 16)

        @block.sync
        def _(sp):
            sp.dma_start(last_i[:, :], env["dlast"].partition_broadcast(P)).then_inc(dl_in, 16)
            sp.wait_ge(br, 3)
            sp.dma_start(env["brow_d"].rearrange("w (k p) -> k w p", p=P), b_rows[:, :, :]).then_inc(bout, 16)
            for k in range(NBLK):
                q = k % 2
                sp.wait_ge(ev, 3 * C * (k + 1))
                cols = slice(k * R, (k + 1) * R)
                for ap, buf in ((env["idx_d"], o_src), (env["dl_d"], o_dl), (env["ew_d"], o_w)):
                    sp.dma_start(ap[:, cols], buf[:, q, :, :].rearrange("p n r -> p (n r)")).then_inc(st[q], 16)
                sp.wait_ge(coz, NCOEF * (k + 1))
                sp.dma_start(env["coef_d"][:, cols, :], o_co[:, q, :, :]).then_inc(st[q], 16)
            sp.wait_ge(bout, 16)
            for q in range(2):
                sp.wait_ge(st[q], 64 * ((NBLK + 1 - q) // 2))

        @block.tensor
        def _(pe):
            pe.wait_ge(consts, 4)
            pe.wait_ge(cd, B_READY)
            for w in range(3):
                pe.transpose(ps[0][0:NBLK, w, :], b_s[:, w, :], ident[:, :]).then_inc(bt, 1)
            pe.wait_ge(br, 3)
            for k in range(NBLK):
                q = k % 2
                pe.wait_ge(rf, 3 * (k + 1))
                for r in range(C):
                    n = k * C + r
                    if n >= C:
                        pe.wait_ge(ev, 3 * (n - C + 1))
                    if n >= 2:
                        pe.wait_ge(atc, 3 * (n - 1))
                    e = slice(r * P, (r + 1) * P)
                    pe.transpose(ps[r][:, 0, :], rows_sf[:, e], ident[:, :])
                    pe.transpose(ps[r][:, 1, :], rows_dl[:, e], ident[:, :])
                    pe.transpose(ps[r][:, 2, :], rows_w[:, q, e], ident[:, :])
                    for a in range(9):
                        dst = ps[r][:, 3, :] if a == 8 else pa[2 * (n % 2) + a // 4][:, a % 4, :]
                        last = pe.transpose(dst, rows_a[:, q, a * R + r * P:a * R + (r + 1) * P], ident[:, :])
                    last.then_inc(tr, 1)

        @block.scalar
        def _(act):
            for n in range(NBLK * C):
                k, r = n // C, n % C
                act.wait_ge(tr, n + 1)
                if k and r == 0:
                    act.wait_ge(coz, NCOEF * k)
                for h in range(2):
                    act.activation(o_at[:, 4 * h:4 * h + 4, :, r], pa[2 * (n % 2) + h][:, :, :], ACT.Copy).then_inc(atc, 1)
                act.wait_ge(ev, 3 * (n + 1))
                act.activation(o_at[:, 8, :, r], ps[r][:, 3, :], ACT.Copy).then_inc(atc, 1)
                if r == C - 1:
                    act.wait_ge(atc, 3 * (n + 1))
                    if k >= 2:
                        act.wait_ge(st[k % 2], 64 * (k // 2))
                    for col, a, w in single:
                        act.activation(o_co[:, k % 2, :, col], at(a), ACT.Copy, scale=w).then_inc(coz, 1)

        @block.vector
        def _(dve):
            n = [0]

            def link(ins):
                n[0] += 1
                ins.then_inc(cd, 1)
                dve.wait_ge(cd, n[0])

            dve.wait_ge(consts, 4)
            link(dve.tensor_copy(iota_b[:, :], iota_i[:, :]))
            link(dve.tensor_copy(ident_b[:, :], ident[:, :]))
            link(dve.tensor_copy(tile_f[:, :], tile_i[:, :]))
            link(dve.tensor_copy(step_f[:, :], step_i[:, :]))
            dve.wait_ge(dl_in, 16)
            link(dve.tensor_scalar(last_m[:, :], last_i[:, :], float(n_nodes - 1), None, ALU.min))
            link(dve.tensor_scalar(last_b[:, :], last_m[:, :], 7, None, ALU.arith_shift_right))
            link(dve.tensor_copy(last_f[:, :], last_b[:, :]))
            link(dve.tensor_tensor(end_f[:, :], last_f[:, :], tile_f[:, :], ALU.add))
            for k in range(NBLK):
                link(dve.tensor_scalar(lt[:, :], end_f[:, :], step_f[:, k:k + 1], 0.0, ALU.is_lt, ALU.add,
                                       accum_out=t_f[:, k:k + 1]))
            link(dve.tensor_copy(t_i[:, :], t_f[:, :]))
            link(dve.tensor_tensor(b_f[:, :], step_f[:, :], t_f[:, :], ALU.subtract))
            assert n[0] == T_READY
            link(dve.tensor_scalar(b_n[:, :], b_f[:, :], float(nb - 1), None, ALU.min))
            for w, width in enumerate((QW, OW, MW)):
                link(dve.tensor_scalar(b_s[:, w, :], b_n[:, :], float(width), None, ALU.mult))
            assert n[0] == B_READY
            dve.wait_ge(bt, 3)
            for w in range(3):
                dve.tensor_copy(b_rows[:, w, :], ps[0][0:NBLK, w, :]).then_inc(br, 1)

            two = 0
            for k in range(NBLK):
                q = k % 2
                dve.wait_ge(gat[q], 64 * (k // 2 + 1))
                if k:
                    dve.wait_ge(tr, C * k)
                dve.tensor_copy(rows_sf[:, :], rows_s[:, q, :]).then_inc(rf, 1)
                dve.tensor_copy(rows_df[:, :], rows_d[:, q, :]).then_inc(rf, 1)
                dve.wait_ge(rf, 3 * k + 2)
                dve.scalar_tensor_tensor(out=rows_dl[:, :], in0=b_n[:, k:k + 1].to_broadcast((P, R)), scalar=-float(P),
                                         in1=rows_df[:, :], op0=ALU.mult, op1=ALU.add).then_inc(rf, 1)
                if k >= 2:
                    dve.wait_ge(st[q], 64 * (k // 2))
                for r in range(C):
                    dve.wait_ge(tr, C * k + r + 1)
                    dve.tensor_copy(o_src[:, q, :, r], ps[r][:, 0, :]).then_inc(ev, 1)
                    dve.tensor_copy(o_dl[:, q, :, r], ps[r][:, 1, :]).then_inc(ev, 1)
                    dve.tensor_copy(o_w[:, q, :, r], ps[r][:, 2, :]).then_inc(ev, 1)
                dve.wait_ge(atc, 3 * C * (k + 1))
                for (i, kk), t in terms.items():
                    if len(t) == 2:
                        (j, w), (j2, w2) = t
                        buf = second[:, two % N_TWO, :]
                        dve.tensor_scalar(buf, at(4 + j2), w2, None, ALU.mult).then_inc(tw, 1)
                        two += 1
                        dve.wait_ge(tw, two)
                        dve.scalar_tensor_tensor(out=o_co[:, q, :, 3 * kk + i], in0=at(4 + j), scalar=w, in1=buf,
                                                 op0=ALU.mult, op1=ALU.add).then_inc(coz, 1)



def node_phase(nc, sem, env, kind):
    NBE = env["NBE"]
    ident = env["ident"]
    qtab, otab = env["qtab"], env["otab"]
    W = env["weights"]
    KB = blocks_per_batch(NBE)
    HB = NBE // KB // 2
    name = f"n{kind}_"
    with ExitStack() as c:
        def sb(nm, shape, dt=F32):
            return c.enter_context(nc.sbuf_tensor(name + nm, shape, dt))

        we_o = sb("we_o", [P, D]) if kind else None
        if kind < 2:
            we_q = sb("we_q", [P, D])
            wqe = sb("wqe", [P, D + H])
            bqe = sb("bqe", [P, D + H])
            w3 = sb("w3", [P, 3 * D])
            b3 = sb("b3", [P, 3 * D])
            wt = sb("wt", [P, 2, D])
            hT = sb("hT", [P, 2, D])
            kvs = sb("kvs", [P, 2, KB, 3 * D])
            pT = c.enter_context(nc.psum_tensor(name + "pT", [P, 2, 512], F32))
            pq = c.enter_context(nc.psum_tensor(name + "pq", [P, 2, 512], F32))
            pk = c.enter_context(nc.psum_tensor(name + "pk", [P, 2, 512], F32))
        if kind != 1:
            xin = sb("xin", [P, 2, KB, D])
            stat = sb("stat", [P, 2, KB, 6])
            mv = sb("mv", [P, 2, KB, 2])
            sd = sb("sd", [P, 2, KB])
            rs = sb("rs", [P, 2, KB])
            nb = sb("nb", [P, 2, KB])
        if kind:
            sin = sb("sin", [P, 2, KB, D])
            den = sb("den", [P, KB, H])
            rec = sb("rec", [P, KB, H])
            pwr = sb("pwr", [P, KB, H])
            t1 = sb("t1", [P, KB, D])
            t2 = sb("t2", [P, KB, D])
            t3 = sb("t3", [P, KB, D])
        h = sb("h", [P, 2, KB, D])
        x1 = sb("x1", [P, 2, KB, D]) if kind == 2 else None
        eps = sb("eps", [P, 1])

        wl = sem(name + "weights"); wx = sem(name + "wx"); xl = [sem(name + f"x{q}") for q in range(2)]
        ch = sem(name + "dve"); sq = sem(name + "sqrt"); hr = sem(name + "h"); tt = sem(name + "tr")
        hs = sem(name + "hT"); mm = sem(name + "proj"); kd = sem(name + "kvs"); qd = sem(name + "q")
        st = [sem(name + f"st{q}") for q in range(2)]
        ez = sem(name + "eps")
        N_ROWS = {0: 0, 1: 6, 2: 8}[kind]
        N_STAT = 2 if kind != 1 else 0
        per = N_ROWS + (N_STAT + 2 if kind != 1 else 0)
        k_aggr = min(max(1, (KB - 1) // 3), KB - 1)
        ZERO = [(NBE // KB) * j // 14 * (KB * OW) for j in (8, 11)]
        k_norm = min(k_aggr + 2, KB - 1)
        loads = {0: 1, 1: 1, 2: 2}[kind]
        block = c.enter_context(nc.Block())

        def rows(ap, m, q):
            return ap[bass.ds((2 * m + q) * (KB * P), KB * P), :].rearrange("(k p) n -> p k n", p=P)

        def done(m, q, k):
            return (2 * m + q) * KB + (k + 1)

        def following(m, q):
            return (m, 1) if q == 0 else (m + 1, 0)

        def whole(eng, batch):
            batch(0, 0, 0, False)
            batch(0, 1, 1, False)
            with eng.Fori(1, HB - 1) as m:
                batch(m, 0, 2, False)
                batch(m, 1, 2, False)
            batch(HB - 1, 0, 2, False)
            batch(HB - 1, 1, 2, True)

        @block.sync
        def _(sp):
            if kind < 2:
                l = kind + 1

                def row(ap):
                    return ap.rearrange("(a n) -> a n", a=1).partition_broadcast(P)
                sp.dma_start(wqe[:, 0:D], W[f"Wq{l}"]).then_inc(wl, 16)
                sp.dma_start(bqe[:, 0:D], row(W[f"bq{l}"])).then_inc(wl, 16)
                for i, k in enumerate("kvs"):
                    sp.dma_start(w3[:, i * D:(i + 1) * D], W[f"W{k}{l}"]).then_inc(wl, 16)
                    sp.dma_start(b3[:, i * D:(i + 1) * D], row(W[f"b{k}{l}"])).then_inc(wl, 16)
                sp.dma_start(we_q[:, :], W[f"We{l}"].partition_broadcast(P)).then_inc(wl, 16)
            if kind > 0:
                sp.dma_start(we_o[:, :], W[f"We{kind}"].partition_broadcast(P)).then_inc(wl, 16)

            def batch(m, q, n, last):
                if n == 2:
                    sp.wait_ge(hr, done(m - 1, q, KB - 1))
                    sp.nop(nofuse=True)
                if kind != 1:
                    sp.dma_start(xin[:, q, :, :], rows(env["x_p"], m, q)).then_inc(xl[q], 16)
                if kind > 0:
                    sp.dma_start(sin[:, q, :, :], rows(env["skip_d"][kind - 1], m, q)).then_inc(xl[q], 16)
            whole(sp, batch)

        @block.gpsimd
        def _(pool):
            if kind == 0:
                pool.memset(otab[:, :], 0.0)

            def batch(m, q, n, last):
                if kind < 2:
                    pool.wait_ge(kd, done(m, q, KB - 1))
                    pool.nop(nofuse=True)
                    pool.dma_start(rows(env["kv_d"][kind], m, q), kvs[:, q, :, 0:2 * D]).then_inc(st[q], 16)
                    pool.dma_start(rows(env["skip_d"][kind], m, q), kvs[:, q, :, 2 * D:3 * D]).then_inc(st[q], 16)
                    if kind == 1 and isinstance(m, int) and m == HB - 1:
                        pool.wait_ge(ch, (2 * m + q + 1) * per)
                        pool.memset(otab[:, 0:ZERO[0]] if q == 0 else otab[:, ZERO[0]:ZERO[1]], 0.0)
                else:
                    pool.wait_ge(hr, done(m, q, KB - 1))
                    pool.nop(nofuse=True)
                    pool.dma_start(rows(env["h_d"], m, q), h[:, q, :, :]).then_inc(st[q], 16)
                    pool.dma_start(rows(env["x1_d"], m, q), x1[:, q, :, :]).then_inc(st[q], 16)
            whole(pool, batch)
            for q in range(2):
                pool.wait_ge(st[q], 32 * HB)

        @block.tensor
        def _(pe):
            if kind == 2:
                return

            def turn(m, q, k, first):
                i = (q * KB + k) % 2
                pe.wait_ge(hr, done(m, q, k))
                if not first:
                    pe.wait_ge(hs, done(m, q, k - 2))
                pe.transpose(pT[:, i, 0:D], h[:, q, k, :], ident[:, :]).then_inc(tt, 1)

            def project(m, q, k, first):
                i = (q * KB + k) % 2
                pe.wait_ge(hs, done(m, q, k))
                if not first:
                    pe.wait_ge(qd, done(m, q, k - 2))
                pe.matmul(pk[:, i, 0:3 * D], hT[:, i, :], w3[:, :], start=True, stop=True)
                pe.matmul(pq[:, i, 0:D + H], hT[:, i, :], wqe[:, :], start=True, stop=True).then_inc(mm, 1)

            def batch(m, q, n, last):
                for k in range(KB):
                    if k + 1 < KB:
                        turn(m, q, k + 1, n == 0 and k == 0)
                    elif not last:
                        turn(*following(m, q), 0, n == 0 and KB == 1)
                    project(m, q, k, n * KB + k < 2)

            pe.wait_ge(wx, 4)
            turn(0, 0, 0, True)
            whole(pe, batch)

        def deviations(act, m, q):
            act.wait_ge(ch, (2 * m + q) * per + (N_ROWS + N_STAT))
            act.activation(sd[:, q, :], mv[:, q, :, 1], ACT.Sqrt, bias=eps[:, 0:1]).then_inc(sq, 1)

        def normalise(act, m, q, n, blocks):
            if blocks[0] == 0:
                act.wait_ge(ch, (2 * m + q) * per + per)
                if kind == 0 and n == 2:
                    act.wait_ge(tt, done(m - 1, q, KB - 1))
                if kind == 2 and n == 2:
                    act.wait_ge(st[q], m * 32)
            for k in blocks:
                s, b = rs[:, q, k:k + 1], nb[:, q, k:k + 1]
                if kind == 0:
                    act.activation(h[:, q, k, :], xin[:, q, k, :], ACT.Relu, scale=s, bias=b).then_inc(hr, 1)
                else:
                    act.activation(h[:, q, k, 0:MUL], x1[:, q, k, 0:MUL], ACT.Relu, scale=s, bias=b)
                    act.activation(h[:, q, k, MUL:D].rearrange("p (i u) -> p i u", i=3),
                                   x1[:, q, k, MUL:D].rearrange("p (u i) -> p i u", i=3), ACT.Relu,
                                   scale=s, bias=b).then_inc(hr, 1)

        @block.scalar
        def _(act):
            act.wait_ge(ez, 1)

            def batch(m, q, n, last):
                if kind == 2:
                    deviations(act, m, q)
                    normalise(act, m, q, n, range(KB))
                    return
                for k in range(KB):
                    if kind == 0 and k == k_norm and not last:
                        deviations(act, *following(m, q))
                    i = (q * KB + k) % 2
                    act.wait_ge(tt, done(m, q, k))
                    if n * KB + k >= 2:
                        act.wait_ge(mm, done(m, q, k - 2))
                    act.activation(hT[:, i, :], pT[:, i, 0:D], ACT.Copy).then_inc(hs, 1)
                    if kind == 0 and k + 2 < KB:
                        normalise(act, m, q, n, [k + 2])
                    if kind == 0 and k == max(KB - 2, k_norm) and not last:
                        normalise(act, *following(m, q), min(n + 1, 2), range(KB)[:2])

            if kind == 0:
                deviations(act, 0, 0)
                normalise(act, 0, 0, 0, range(KB)[:2])
            whole(act, batch)

        @block.vector
        def _(dve):
            dve.memset(eps[:, :], EPS).then_inc(ez, 1)
            dve.wait_ge(wl, 16 * {0: 9, 1: 10, 2: 1}[kind])
            if kind < 2:
                dve.tensor_tensor(wt[:, 0, :], wqe[:, 0:D], we_q[:, :], ALU.mult).then_inc(wx, 1)
                dve.tensor_tensor(wt[:, 1, :], bqe[:, 0:D], we_q[:, :], ALU.mult).then_inc(wx, 1)
                dve.wait_ge(wx, 2)
                dve.tensor_reduce(wqe[:, D:D + H], wt[:, 0, :].rearrange("p (h c) -> p h c", h=H), AX.X, ALU.add).then_inc(wx, 1)
                dve.tensor_reduce(bqe[:, D:D + H], wt[:, 1, :].rearrange("p (h c) -> p h c", h=H), AX.X, ALU.add).then_inc(wx, 1)
                dve.wait_ge(wx, 4)

            def heads(ap):
                return ap.rearrange("p k (h c) -> p k h c", h=H)

            def steps(m, q, n):
                def after(k):
                    dve.wait_ge(ch, (2 * m + q) * per + k)

                def tab(col, w):
                    return otab[:, bass.ds((2 * m + q) * (KB * OW), KB * OW)].rearrange("p (k w) -> p k w", w=OW)[:, :, col:col + w]

                def denominators():
                    dve.wait_ge(xl[q], (m + 1) * (16 * loads))
                    if n:
                        after(0)
                    dve.tensor_scalar(den[:, :, :], tab(D, H), 1e-30, None, ALU.max).then_inc(ch, 1)

                def reciprocals():
                    after(1)
                    dve.reciprocal(rec[:, :, :], den[:, :, :]).then_inc(ch, 1)

                def weight_sums():
                    after(2)
                    dve.tensor_tensor(pwr[:, :, :], tab(D + H, H), rec[:, :, :], ALU.mult).then_inc(ch, 1)

                def v_part():
                    r4 = rec[:, :, :].unsqueeze(3).to_broadcast((P, KB, H, CH))
                    dve.tensor_tensor(heads(t1[:, :, :]), heads(tab(0, D)), r4, ALU.mult).then_inc(ch, 1)

                def e_part():
                    after(3)
                    p4 = pwr[:, :, :].unsqueeze(3).to_broadcast((P, KB, H, CH))
                    we = we_o[:, :].rearrange("p (h c) -> p h c", h=H).unsqueeze(1).to_broadcast((P, KB, H, CH))
                    dve.tensor_tensor(heads(t2[:, :, :]), we, p4, ALU.mult).then_inc(ch, 1)

                def both():
                    after(5)
                    if kind == 1 and n:
                        dve.wait_ge(hr, (2 * m + q) * KB)
                    dve.tensor_tensor(t3[:, :, :], t1[:, :, :], t2[:, :, :], ALU.add).then_inc(ch, 1)

                def with_skip():
                    after(6)
                    if kind == 1:
                        if n == 2:
                            dve.wait_ge(tt, done(m - 1, q, KB - 1))
                        dve.tensor_tensor(h[:, q, :, :], t3[:, :, :], sin[:, q, :, :], ALU.add).then_inc(hr, KB)
                    else:
                        dve.tensor_tensor(t1[:, :, :], t3[:, :, :], sin[:, q, :, :], ALU.add).then_inc(ch, 1)

                def residual():
                    after(7)
                    if n == 2:
                        dve.wait_ge(st[q], m * 32)
                    dve.tensor_tensor(x1[:, q, :, :], t1[:, :, :], xin[:, q, :, :], ALU.add).then_inc(ch, 1)

                def stats():
                    if kind == 0:
                        dve.wait_ge(xl[q], (m + 1) * (16 * loads))
                    else:
                        after(8)
                    rows_in = x1 if kind == 2 else xin
                    for k in range(KB):
                        last = dve.bn_stats(stat[:, q, k, :], rows_in[:, q, k, :])
                    last.then_inc(ch, 1)

                def aggregate():
                    after(N_ROWS + 1)
                    dve.nop(nofuse=True)
                    for k in range(KB):
                        last = dve.bn_aggr(mv[:, q, k, :], stat[:, q, k, :])
                    last.then_inc(ch, 1)

                def inverse():
                    dve.wait_ge(sq, 2 * m + (q + 1))
                    dve.reciprocal(rs[:, q, :], sd[:, q, :]).then_inc(ch, 1)

                def shift():
                    after(N_ROWS + 3)
                    dve.scalar_tensor_tensor(out=nb[:, q, :], in0=mv[:, q, :, 0], scalar=-1.0, in1=rs[:, q, :],
                                             op0=ALU.mult, op1=ALU.mult).then_inc(ch, 1)

                if kind == 0:
                    return [(0, stats), (k_aggr, aggregate), (k_norm, inverse), (k_norm, shift)]
                made = [denominators, reciprocals, weight_sums, v_part, e_part, both, with_skip]
                if kind == 2:
                    made += [residual, stats, aggregate, inverse, shift]
                return [(i * max(KB - 1, 1) // len(made), s) for i, s in enumerate(made)]

            def evacuate(m, q, k, n):
                i = (q * KB + k) % 2
                dve.wait_ge(mm, done(m, q, k))
                if k == 0 and n == 2:
                    dve.wait_ge(st[q], m * 32)
                dve.tensor_tensor(kvs[:, q, k, :], pk[:, i, 0:3 * D], b3[:, :], ALU.add).then_inc(kd, 1)
                dve.tensor_tensor(qtab[:, bass.ds(((2 * m + q) * KB + k) * QW, D + H)], pq[:, i, 0:D + H], bqe[:, :],
                                  ALU.add).then_inc(qd, 1)

            def batch(m, q, n, last):
                if kind == 2:
                    for _, step in steps(m, q, n):
                        step()
                    return
                ahead = [] if last else steps(*following(m, q), min(n + 1, 2))
                for k in range(KB):
                    for place, step in ahead:
                        if place == k:
                            step()
                    evacuate(m, q, k, n)

            if kind < 2:
                for _, step in steps(0, 0, 0):
                    step()
            whole(dve, batch)
            if kind == 1:
                dve.memset(otab[:, ZERO[1]:NBE * OW], 0.0)



def attention_sems(sem):
    names = ("oh", "ohT", "ohTc", "qmm", "prod", "qwe", "red", "al1", "alpha", "d4", "aT", "dTs", "pen", "scan1",
             "rowsT", "rw", "rowv", "cr", "fe", "fac", "cols", "cin", "scan2", "mx", "mT", "da", "p", "pp", "pw",
             "ohf", "vp", "vals", "agg", "oadd", "facps", "facn", "resc", "init")
    s = {k: sem("a_" + k) for k in names}
    for k in ("idx", "dl", "bA", "w", "bB"):
        s["ld_" + k] = [sem(f"a_ld_{k}{q}") for q in range(2)]
    s["kv"] = [[sem(f"a_kv{q}_{c}") for c in range(NCH)] for q in range(2)]
    return s


def attention_pass(nc, env, L):
    G, SP = env["G"], env["SP"]
    ident, ident_b, iota_b = env["ident"], env["ident_b"], env["iota_b"]
    qtab, otab = env["qtab"], env["otab"]
    S = env["att"]
    kv_d = env["kv_d"][L]
    name = f"e{L}_"
    R4 = H * T
    NR = 9
    LAG = 5
    with ExitStack() as c:
        def sb(nm, shape, dt=F32):
            return c.enter_context(nc.sbuf_tensor(name + nm, shape, dt))

        def psum(nm, shape, dt=F32):
            return c.enter_context(nc.psum_tensor(name + nm, shape, dt))

        kv = sb("kv", [P, 2 * T, 2 * D])
        idx = sb("idx", [P, 2 * T], I32)
        dl = sb("dl", [P, 2, T])
        wq = sb("wq", [P, 2, T])
        bA = sb("bA", [1, 2 * NCH], I32)
        bB = sb("bB", [1, 2 * NCH], I32)
        oh = sb("oh", [P, 2 * T, P], BF16)
        ohT = sb("ohT", [P, 2, C, P])
        ohf = sb("ohf", [P, 2, C, P])
        vals = sb("vals", [P, 2, C, OW])
        prod = sb("prod", [P, C, D])
        alpha = sb("alpha", [P, 2, H, T])
        qw = sb("qw", [P, 2, H, T])
        tmp = sb("tmp", [P, H, T])
        d4 = sb("d4", [P, H, T])
        pp = sb("pp", [P, 2, T, 2 * H])
        dTs = sb("dTs", [R4, P])
        pen = sb("pen", [R4, P + 1])
        f1 = sb("f1", [R4, P])
        b1 = sb("b1", [R4, P])
        cin = sb("cin", [R4, 2])
        mx = sb("mx", [R4, P])
        rw = sb("rw", [1, 4, H, T])
        fx = sb("fx", [1, H, T + 1])
        lx = sb("lx", [1, H, T + 1])
        dlx = sb("dlx", [1, T + 1])
        pc = sb("pc", [1, T])
        ne = sb("ne", [1, T])
        pw = sb("pw", [1, T])
        pwx = sb("pwx", [1, H, T + 1])
        qbx = sb("qbx", [1, H, T])
        bf = sb("bf", [1, H, T])
        cr = sb("cr", [1, 2, H, T])
        dm = sb("dm", [1, H])
        cf = sb("cf", [1, 1])
        fe = sb("fe", [1, H])
        fac = sb("fac", [1, H])
        facn = sb("facn", [P, H])
        one = sb("one", [1, 1])

        ohT_ps = psum("ohT_ps", [P, 1024], BF16)
        q_ps = psum("q_ps", [P, 2, 512])
        agg = psum("agg", [P, 2, 512])
        turn = psum("turn", [P, 512])
        p_ps = psum("p_ps", [P, 512])
        small = psum("small", [P, 512])
        p2 = p_ps[:, 0:R4].rearrange("p (h t) -> p h t", h=H)
        fac_ps = small[:, R4:R4 + H]
        col_ps = small[0:R4, R4 + H:R4 + H + 2]
        row_ps = small[0:1, R4 + H + 2:R4 + H + 2 + 4 * R4]
        aT_ps = turn[0:R4, 0:P]
        dT_ps = turn[0:R4, P:2 * P]
        mT_ps = turn[:, 2 * P:2 * P + R4]

        def done(m, q, per, k):
            return (2 * m + q) * per + (L * G * per + k)

        def nth(m, n):
            return m * n + (L * (G // 2) * n + n)

        def prev(m, q, by=1):
            return (m, q - by) if q - by >= 0 else (m - 1, q - by + 2)

        block = c.enter_context(nc.Block())

        def turns(eng, turn):
            turn(0, 0, 0)
            turn(0, 1, 1)
            with eng.Fori(1, G // 2 - 1) as m:
                turn(m, 0, 2)
                turn(m, 1, 2)
            turn(G // 2 - 1, 0, G - 2)
            turn(G // 2 - 1, 1, G - 1)
            turn(G // 2, 0, G)
            turn(G // 2, 1, G + 1)

        def ahead(m, q, ch, by, g):
            if ch + by < NCH:
                return (m, q, ch + by)
            return None if g == G - 1 else (m, 1, ch + by - NCH) if q == 0 else (m + 1, 0, ch + by - NCH)

        def summed(m, q, ch, g):
            if ch >= LAG:
                return (*prev(m, q), ch - LAG) if 1 <= g <= G else None
            return (*prev(m, q, 2), ch - LAG + NCH) if 2 <= g <= G + 1 else None

        def before(m, q, u):
            if u:
                return (m, q, u - 1)
            return None if isinstance(m, int) and m == 0 and q == 0 else (*prev(m, q), NCH - 1)

        def early(m, q, ch):
            return isinstance(m, int) and m == 0 and q == 0 and ch < 2

        @block.sync
        def _(sp):
            def load(which, dst, src, m, q):
                sp.dma_start(dst, src).then_inc(S["ld_" + which][q], 16)

            def cols(m, q, n=T):
                return bass.ds((2 * m + q) * n, n)

            def first_loads(m, q):
                load("idx", idx[:, q * T:(q + 1) * T], env["idx_d"][:, cols(m, q)], m, q)
                load("dl", dl[:, q, :], env["dl_d"][:, cols(m, q)], m, q)
                load("bA", bA[:, q * NCH:(q + 1) * NCH], env["brow_d"][0:1, cols(m, q, NCH)], m, q)

            first_loads(0, 0)
            first_loads(0, 1)

            def turn(m, q, g):
                if g >= G:
                    return
                if 1 <= g < G - 1:
                    pm, pq = prev(m, q)
                    nm, nq = (m, 1) if q == 0 else (m + 1, 0)
                    sp.wait_ge(S["prod"], done(pm, pq, NCH, NCH))
                    sp.nop(nofuse=True)
                    sp.wait_ge(S["d4"], done(pm, pq, 1, 1))
                    sp.nop(nofuse=True)
                    first_loads(nm, nq)
                pm, pq = prev(m, q, 2)
                if g >= 2:
                    sp.wait_ge(S["pw"], done(pm, pq, 1, 1))
                    sp.nop(nofuse=True)
                load("w", wq[:, q, :], env["ew_d"][:, cols(m, q)], m, q)
                if g >= 2:
                    sp.wait_ge(S["oadd"], done(pm, pq, NCH, NCH))
                    sp.nop(nofuse=True)
                load("bB", bB[:, q * NCH:(q + 1) * NCH], env["brow_d"][1:2, cols(m, q, NCH)], m, q)

            turns(sp, turn)

        @block.gpsimd
        def _(pool):
            def gathers(m, q, first):
                for ch in range(NCH):
                    if not first:
                        pm, pq = prev(m, q, 2)
                        pool.wait_ge(S["vals"], done(pm, pq, NCH, ch + 1))
                    if ch == 0:
                        pool.wait_ge(S["ld_idx"][q], nth(m, 16))
                    pool.nop(nofuse=True)
                    for r in range(C):
                        s = q * T + ch * C + r
                        pool.indirect_dma_start(
                            out=kv[:, s, :], out_offset=None, in_=kv_d,
                            in_offset=bass.IndirectOffsetOnAxis(ap=idx[:, s:s + 1], axis=0)).then_inc(S["kv"][q][ch], 16)

            gathers(0, 0, True)
            gathers(0, 1, True)
            with pool.Fori(1, G // 2) as m:
                gathers(m, 0, False)
                gathers(m, 1, False)

        @block.tensor
        def _(pe):
            def turn_onehot(m, q, ch):
                pe.wait_ge(S["oh"], done(m, q, NCH, ch + 1))
                for r in range(C):
                    last = pe.transpose(ohT_ps[:, r * P:(r + 1) * P], oh[:, q * T + ch * C + r, :], ident_b[:, :])
                last.then_inc(S["ohT"], 1)

            def q_rows(m, q, ch):
                if ch == 0:
                    pe.wait_ge(S["ld_bA"][q], nth(m, 16))
                    pe.nop(nofuse=True)
                col = nc.values_load(bA[0:1, q * NCH + ch:q * NCH + ch + 1], engines=(mybir.EngineType.PE,), min_val=0,
                                     max_val=(env["NBE"] - 1) * QW, skip_runtime_bounds_check_because=CLAMPED)
                pe.wait_ge(S["ohTc"], done(m, q, NCH, ch + 1))
                for r in range(C):
                    last = pe.matmul(q_ps[:, ch % 2, r * QW:r * QW + D + H], ohT[:, ch % 2, r, :],
                                     qtab[:, bass.ds(col, D + H)], start=True, stop=True)
                last.then_inc(S["qmm"], 1)

            def sums(m, q, ch):
                pe.wait_ge(S["vp"], done(m, q, NCH, ch + 1))
                pe.wait_ge(S["vals"], done(m, q, NCH, ch + 1))
                for r in range(C):
                    last = pe.matmul(agg[:, ch % 2, 0:OW], ohf[:, ch % 2, r, :], vals[:, ch % 2, r, :],
                                     start=(r == 0), stop=(r == C - 1))
                last.then_inc(S["agg"], 1)

            def turn(m, q, g):
                hm, hq = prev(m, q)
                chain = 1 <= g <= G
                for ch in range(NCH):
                    if g < G and ahead(m, q, ch, 1, g):
                        q_rows(*ahead(m, q, ch, 1, g))
                    if chain and ch == 0:
                        pe.wait_ge(S["alpha"], done(hm, hq, 1, 1))
                        pe.wait_ge(S["d4"], done(hm, hq, 1, 1))
                        pe.transpose(aT_ps, alpha[:, hq, :, :].rearrange("p h t -> p (h t)"), ident[:, :])
                        pe.transpose(dT_ps, d4[:, :, :].rearrange("p h t -> p (h t)"), ident[:, :]).then_inc(S["aT"], 1)
                    if chain and ch == 1:
                        pe.wait_ge(S["scan1"], done(hm, hq, 2, 2))
                        for j, col in enumerate((f1[:, P - 1:P], b1[:, 0:1], dTs[:, 0:1], dTs[:, P - 1:P])):
                            last = pe.transpose(row_ps[0:1, j * R4:(j + 1) * R4], col, ident[0:R4, 0:R4])
                        last.then_inc(S["rowsT"], 1)
                    if chain and ch == 3:
                        pe.wait_ge(S["cr"], done(hm, hq, 2, 2))
                        for j in range(2):
                            last = pe.matmul(col_ps[:, j:j + 1], cr[0:1, j, :, :].rearrange("p h t -> p (h t)"), one[0:1, 0:1],
                                             start=True, stop=True)
                        last.then_inc(S["cols"], 1)
                    if chain and ch == 4:
                        pe.wait_ge(S["mx"], done(hm, hq, 1, 1))
                        pe.transpose(mT_ps, mx[:, :], ident[0:R4, 0:R4]).then_inc(S["mT"], 1)
                    if chain and ch == 5:
                        pe.wait_ge(S["ohf"], done(hm, hq, NCH, 1))
                        pe.wait_ge(S["fac"], done(hm, hq, 1, 1))
                        pe.matmul(fac_ps, ohf[0:1, 0, 0, :], fac[0:1, :], start=True, stop=True).then_inc(S["facps"], 1)
                    if g < G and ahead(m, q, ch, 2, g):
                        turn_onehot(*ahead(m, q, ch, 2, g))
                    if summed(m, q, ch, g):
                        sums(*summed(m, q, ch, g))

            turn_onehot(0, 0, 0)
            pe.wait_ge(S["ohTc"], done(0, 0, NCH, 1))
            turn_onehot(0, 0, 1)
            q_rows(0, 0, 0)
            turns(pe, turn)

        @block.scalar
        def _(act):
            def copy_ohT(m, q, ch):
                act.wait_ge(S["ohT"], done(m, q, NCH, ch + 1))
                if not early(m, q, ch):
                    cm, cq = (m, q) if ch >= 2 else prev(m, q)
                    act.wait_ge(S["qmm"], done(cm, cq, NCH, (ch - 2) % NCH + 1))
                act.activation(ohT[:, ch % 2, :, :].rearrange("p r n -> p (r n)"), ohT_ps[:, 0:C * P],
                               ACT.Copy).then_inc(S["ohTc"], 1)

            def onehots_32(m, q, u):
                if not early(m, q, u):
                    cm, cq = (m, q) if u >= 2 else prev(m, q)
                    act.wait_ge(S["agg"], done(cm, cq, NCH, (u - 2) % NCH + 1))
                act.activation(ohf[:, u % 2, :, :], oh[:, q * T + u * C:q * T + (u + 1) * C, :],
                               ACT.Copy).then_inc(S["ohf"], 1)

            def weights_in(m, q, u):
                if u == 0:
                    act.wait_ge(S["pw"], done(m, q, 1, 1))
                act.activation(vals[:, u % 2, :, D:OW], pp[:, q, u * C:(u + 1) * C, :], ACT.Copy).then_inc(S["vp"], 1)

            def turn(m, q, g):
                hm, hq = prev(m, q)
                chain = 1 <= g <= G
                for ch in range(NCH):
                    if g < G:
                        if ch == 0 and g >= 2:
                            pm, pq = prev(m, q, 2)
                            act.wait_ge(S["alpha"], done(pm, pq, 1, 1))
                        act.wait_ge(S["prod"], done(m, q, NCH, ch + 1))
                        act.activation(qw[:, q, :, ch * C:(ch + 1) * C].rearrange("p h r -> p r h"),
                                       q_ps[:, ch % 2, 0:C * QW].rearrange("p (r w) -> p r w", w=QW)[:, :, D:D + H],
                                       ACT.Copy).then_inc(S["qwe"], 1)
                    if chain and ch == 0:
                        act.wait_ge(S["aT"], done(hm, hq, 1, 1))
                        act.activation(dTs[:, :], dT_ps, ACT.Copy, scale=KEY).then_inc(S["dTs"], 1)
                    if chain and ch == 1:
                        act.wait_ge(S["rowsT"], done(hm, hq, 1, 1))
                        act.activation(rw[0:1, :, :, :].rearrange("p k h t -> p (k h t)"), row_ps[0:1, 0:4 * R4],
                                       ACT.Copy).then_inc(S["rw"], 1)
                    if chain and ch == 3:
                        act.wait_ge(S["cols"], done(hm, hq, 1, 1))
                        act.activation(cin[:, :], col_ps, ACT.Copy).then_inc(S["cin"], 1)
                        act.wait_ge(S["rowv"], done(hm, hq, NR, 8))
                        act.activation(fe[0:1, :], dm[0:1, :], ACT.Exp, scale=SCALE).then_inc(S["fe"], 1)
                    if chain and ch == LAG:
                        weights_in(hm, hq, 0)
                    nxt = summed(m, q, ch + 1, g) if ch + 1 < NCH else \
                        summed(*((m, 1) if q == 0 else (m + 1, 0)), 0, g + 1)
                    if nxt:
                        onehots_32(*nxt)
                        if nxt[2]:
                            weights_in(*nxt)
                    if g < G and ahead(m, q, ch, 2, g):
                        copy_ohT(*ahead(m, q, ch, 2, g))
                    if chain and ch == 4:
                        act.wait_ge(S["da"], done(hm, hq, 1, 1))
                        act.activation(p2, tmp[:, :, :], ACT.Exp, scale=SCALE).then_inc(S["p"], 1)
                        act.activation(pp[:, hq, :, 0:H].rearrange("p t h -> p h t"), tmp[:, :, :], ACT.Exp,
                                       scale=SCALE).then_inc(S["pp"], 1)

            copy_ohT(0, 0, 0)
            copy_ohT(0, 0, 1)
            turns(act, turn)

        @block.vector
        def _(dve):
            def onehots(m, q, ch):
                if ch == 0:
                    dve.wait_ge(S["ld_dl"][q], nth(m, 16))
                if not (isinstance(m, int) and m == 0):
                    pm, pq = prev(m, q, 2)
                    dve.wait_ge(S["ohf"], done(pm, pq, NCH, ch + 1))
                for r in range(C):
                    s = ch * C + r
                    last = dve.tensor_scalar(oh[:, q * T + s, :], iota_b[:, :], dl[:, q, s:s + 1], None, ALU.is_equal)
                last.then_inc(S["oh"], 1)

            def products(m, q, ch):
                if not (isinstance(m, int) and m == 0 and q == 0 and ch == 0):
                    cm, cq = (m, q) if ch else prev(m, q)
                    dve.wait_ge(S["red"], done(cm, cq, NCH, (ch - 1) % NCH + 1))
                dve.wait_ge(S["kv"][q][ch], nth(m, 16 * C))
                dve.wait_ge(S["qmm"], done(m, q, NCH, ch + 1))
                s = q * T + ch * C
                dve.tensor_tensor(prod[:, :, :], kv[:, s:s + C, 0:D],
                                  q_ps[:, ch % 2, 0:C * QW].rearrange("p (r w) -> p r w", w=QW)[:, :, 0:D],
                                  ALU.mult).then_inc(S["prod"], 1)

            def reduces(m, q, ch):
                dve.wait_ge(S["prod"], done(m, q, NCH, ch + 1))
                dve.tensor_reduce(alpha[:, q, :, ch * C:(ch + 1) * C].rearrange("p h r -> p r h"),
                                  prod[:, :, :].rearrange("p r (h c) -> p r h c", h=H), AX.X, ALU.add).then_inc(S["red"], 1)

            def weighted(m, q, ch):
                cm, cq = (m, q) if ch >= 2 else prev(m, q)
                if ch == 0:
                    dve.wait_ge(S["p"], done(m, q, 1, 1))
                if not early(m, q, ch):
                    dve.wait_ge(S["agg"], done(cm, cq, NCH, (ch - 2) % NCH + 1))
                s = q * T + ch * C
                pb = p2[:, :, ch * C:(ch + 1) * C].rearrange("p h r -> p r h").unsqueeze(3).to_broadcast((P, C, H, CH))
                dve.tensor_tensor(vals[:, ch % 2, :, 0:D].rearrange("p r (h c) -> p r h c", h=H),
                                  kv[:, s:s + C, D:2 * D].rearrange("p r (h c) -> p r h c", h=H), pb,
                                  ALU.mult).then_inc(S["vals"], 1)

            def block_column(m, q, ch):
                return nc.values_load(bB[0:1, q * NCH + ch:q * NCH + ch + 1], engines=(mybir.EngineType.DVE,), min_val=0,
                                      max_val=(env["NBE"] - 1) * OW, skip_runtime_bounds_check_because=CLAMPED)

            def add_sums(m, q, ch, col):
                dve.wait_ge(S["agg"], done(m, q, NCH, ch + 1))
                if ch:
                    dve.wait_ge(S["oadd"], done(m, q, NCH, ch))
                else:
                    dve.wait_ge(S["resc"], done(m, q, 2, 2))
                ob = otab[:, bass.ds(col, OW)]
                dve.tensor_tensor(ob, agg[:, ch % 2, 0:OW], ob, ALU.add).then_inc(S["oadd"], 1)

            def scores(m, q):
                dve.wait_ge(S["ld_w"][q], nth(m, 16))
                dve.wait_ge(S["qwe"], done(m, q, NCH, NCH))
                wb = wq[:, q, :].unsqueeze(1).to_broadcast((P, H, T))
                dve.tensor_tensor(tmp[:, :, :], qw[:, q, :, :], wb, ALU.mult).then_inc(S["al1"], 1)
                dve.wait_ge(S["al1"], done(m, q, 1, 1))
                dve.wait_ge(S["red"], done(m, q, NCH, NCH))
                dve.tensor_tensor(alpha[:, q, :, :], alpha[:, q, :, :], tmp[:, :, :], ALU.add).then_inc(S["alpha"], 1)
                dve.tensor_copy(d4[:, :, :], dl[:, q, :].unsqueeze(1).to_broadcast((P, H, T))).then_inc(S["d4"], 1)

            def row_keys(m, q):
                dve.wait_ge(S["dTs"], done(m, q, 1, 1))
                dve.tensor_tensor(pen[:, 1:P], dTs[:, 0:P - 1], dTs[:, 1:P], ALU.subtract).then_inc(S["pen"], 1)

            def row_scans(m, q):
                dve.wait_ge(S["pen"], done(m, q, 1, 1))
                dve.tensor_tensor_scan(f1[:, :], pen[:, 0:P], aT_ps, -BIG, ALU.add, ALU.max).then_inc(S["scan1"], 1)
                dve.tensor_tensor_scan(b1[:, ::-1], pen[:, P:0:-1], aT_ps[:, ::-1], -BIG, ALU.add,
                                       ALU.max).then_inc(S["scan1"], 1)

            def carries(m, q, step):
                def wide(ap, n):
                    return ap.unsqueeze(1).to_broadcast((1, H, n))

                flat = lambda ap: ap.rearrange("p h t -> p (h t)")
                d_first, d_last = rw[0:1, 2, 0, :], rw[0:1, 3, 0, :]
                if step == 1:
                    dve.wait_ge(S["rw"], done(m, q, 1, 1))
                else:
                    dve.wait_ge(S["rowv"], done(m, q, NR, step - 1))
                if step == 1:
                    dve.tensor_copy(fx[0:1, :, 1:T + 1], rw[0:1, 0, :, :])
                    last = dve.tensor_copy(dlx[0:1, 1:T + 1], d_last)
                elif step == 2:
                    dve.tensor_tensor(pw[0:1, :], d_first, d_last, ALU.subtract)
                    last = dve.tensor_tensor(ne[0:1, :], dlx[0:1, 0:T], d_first, ALU.not_equal)
                elif step == 3:
                    dve.tensor_scalar(cf[0:1, :], ne[0:1, 0:1], -1.0, 1.0, ALU.mult, ALU.add)
                    last = dve.tensor_scalar(pc[0:1, :], ne[0:1, :], -BIG, None, ALU.mult)
                elif step == 4:
                    dve.tensor_tensor(qbx[0:1, :, 0:T - 1], wide(pw[0:1, 0:T - 1], T - 1), wide(pc[0:1, 1:T], T - 1), ALU.add)
                    last = dve.tensor_tensor(pwx[0:1, :, 1:T + 1], wide(pw[0:1, :], T), wide(pc[0:1, :], T), ALU.add)
                elif step == 5:
                    last = dve.tensor_tensor_scan(flat(bf[0:1, :, :])[:, ::-1], flat(qbx[0:1, :, :])[:, ::-1],
                                                  rw[0:1, 1, :, :].rearrange("p h t -> p (h t)")[:, ::-1], -BIG, ALU.add, ALU.max)
                elif step == 6:
                    last = dve.tensor_tensor_scan(flat(lx[0:1, :, :]), flat(pwx[0:1, :, :]), flat(fx[0:1, :, :]), 0.0,
                                                  ALU.add, ALU.max)
                elif step == 7:
                    dve.tensor_tensor(cr[0:1, 1, :, 0:T - 1], bf[0:1, :, 1:T], wide(pc[0:1, 1:T], T - 1), ALU.add).then_inc(S["cr"], 1)
                    dve.tensor_tensor(cr[0:1, 0, :, :], lx[0:1, :, 0:T], wide(pc[0:1, :], T), ALU.add).then_inc(S["cr"], 1)
                    last = dve.tensor_tensor(dm[0:1, :], fx[0:1, :, 0], bf[0:1, :, 0], ALU.subtract)
                elif step == 8:
                    last = dve.tensor_scalar(dm[0:1, :], dm[0:1, :], 0.0, cf[0:1, 0:1], ALU.min, ALU.mult)
                else:
                    dve.tensor_copy(fx[0:1, :, 0], lx[0:1, :, T])
                    last = dve.tensor_copy(dlx[0:1, 0:1], dlx[0:1, T:T + 1])
                last.then_inc(S["rowv"], 1)

            def full_scans(m, q):
                dve.wait_ge(S["cin"], done(m, q, 1, 1))
                dve.tensor_tensor_scan(f1[:, :], pen[:, 0:P], aT_ps, cin[:, 0:1], ALU.add, ALU.max).then_inc(S["scan2"], 1)
                dve.tensor_tensor_scan(b1[:, ::-1], pen[:, P:0:-1], aT_ps[:, ::-1], cin[:, 1:2], ALU.add,
                                       ALU.max).then_inc(S["scan2"], 1)

            def maxima(m, q):
                dve.wait_ge(S["scan2"], done(m, q, 2, 2))
                dve.tensor_tensor(mx[:, :], f1[:, :], b1[:, :], ALU.max).then_inc(S["mx"], 1)
                dve.wait_ge(S["fe"], done(m, q, 1, 1))
                dve.tensor_scalar(fac[0:1, :], fe[0:1, :], -1.0, None, ALU.add).then_inc(S["fac"], 1)

            def below_max(m, q):
                dve.wait_ge(S["mT"], done(m, q, 1, 1))
                dve.tensor_tensor(tmp[:, :, :].rearrange("p h t -> p (h t)"), alpha[:, q, :, :].rearrange("p h t -> p (h t)"),
                                  mT_ps, ALU.subtract).then_inc(S["da"], 1)

            def times_weight(m, q):
                dve.wait_ge(S["ld_bB"][q], nth(m, 16))
                dve.wait_ge(S["pp"], done(m, q, 1, 1))
                wb = wq[:, q, :].unsqueeze(2).to_broadcast((P, T, H))
                dve.tensor_tensor(pp[:, q, :, H:2 * H], pp[:, q, :, 0:H], wb, ALU.mult).then_inc(S["pw"], 1)

            def factor(m, q):
                dve.wait_ge(S["facps"], done(m, q, 1, 1))
                dve.tensor_scalar(facn[:, :], fac_ps, 1.0, None, ALU.add).then_inc(S["facn"], 1)

            def rescale(m, q, col):
                dve.wait_ge(S["facn"], done(m, q, 1, 1))
                if before(m, q, 0):
                    pm, pq, _ = before(m, q, 0)
                    dve.wait_ge(S["oadd"], done(pm, pq, NCH, NCH))
                ov = otab[:, bass.ds(col, D)].rearrange("p (h c) -> p h c", h=H)
                op = otab[:, bass.ds(col + D, 2 * H)].rearrange("p (k h) -> p k h", h=H)
                dve.tensor_tensor(ov, ov, facn[:, :].unsqueeze(2).to_broadcast((P, H, CH)), ALU.mult).then_inc(S["resc"], 1)
                dve.tensor_tensor(op, op, facn[:, :].unsqueeze(1).to_broadcast((P, 2, H)), ALU.mult).then_inc(S["resc"], 1)

            places = {(0, 4): (row_keys,), (0, 5): (row_scans,), (1, 4): (1,), (1, 5): (2,), (2, 1): (3,), (2, 2): (4,),
                      (2, 3): (5, 6), (2, 4): (7,), (2, 5): (8,), (3, 1): (9,), (3, 4): (full_scans,), (3, 5): (maxima,),
                      (4, 4): (below_max,), (5, 1): (times_weight,), (5, 4): (factor,)}

            def turn(m, q, g):
                hm, hq = prev(m, q)

                def chain(ch, place):
                    if 1 <= g <= G:
                        for piece in places.get((ch, place), ()):
                            if isinstance(piece, int):
                                carries(hm, hq, piece)
                            else:
                                piece(hm, hq)

                for ch in range(NCH):
                    now = summed(m, q, ch, g)
                    was = before(*now) if now else None
                    if g < G:
                        products(m, q, ch)
                    chain(ch, 1)
                    if was:
                        col = block_column(*was)
                    if now and now[2] == 0:
                        col0 = block_column(*now)
                    if g < G and ahead(m, q, ch, 2, g):
                        onehots(*ahead(m, q, ch, 2, g))
                    chain(ch, 2)
                    if now:
                        weighted(*now)
                    chain(ch, 3)
                    if g < G:
                        reduces(m, q, ch)
                    chain(ch, 4)
                    if was:
                        add_sums(*was, col)
                    chain(ch, 5)
                    if now and now[2] == 0:
                        rescale(hm, hq, col0)
                if g < G:
                    scores(m, q)

            dve.memset(pen[:, :], 0.0)
            dve.memset(fx[0:1, :, :], 0.0)
            dve.memset(dlx[0:1, :], -BIG)
            dve.memset(pwx[0:1, :, :], -BIG)
            dve.memset(qbx[0:1, :, :], -BIG)
            dve.memset(cr[0:1, :, :, :], -BIG)
            dve.memset(one[0:1, :], 1.0).then_inc(S["init"], 1)
            dve.wait_ge(S["init"], L + 1)
            onehots(0, 0, 0)
            onehots(0, 0, 1)
            turns(dve, turn)
            col = block_column(G // 2 - 1, 1, NCH - 1)
            add_sums(G // 2 - 1, 1, NCH - 1, col)



def message_pass(nc, sem, env):
    G, NBE = env["G"], env["NBE"]
    iota_b = env["iota_b"]
    mtab = env["mtab"]
    with ExitStack() as c:
        def sb(nm, shape, dt=F32):
            return c.enter_context(nc.sbuf_tensor("m_" + nm, shape, dt))

        hv = sb("hv", [P, 2 * T, D])
        idx = sb("idx", [P, 2 * T], I32)
        dl = sb("dl", [P, 2, T])
        co = sb("co", [P, 2, T, NCOEF])
        bB = sb("bB", [1, 2 * NCH], I32)
        oh = sb("oh", [P, 2, C, P])
        vals = sb("vals", [P, 2, C, MW])
        apart = sb("apart", [P, 2, C, P])
        one = sb("one", [P, 1])
        prod0 = sb("prod0", [P, 2, C, 4, MUL])
        prod12 = c.enter_context(nc.psum_tensor("m_prod12", [P, 4, 512], F32))
        co_ps = c.enter_context(nc.psum_tensor("m_co_ps", [P, 2, 512], F32))
        agg = c.enter_context(nc.psum_tensor("m_agg", [P, 2, 512], F32))
        cp = co_ps[:, :, 0:T * NCOEF].rearrange("p q (t k) -> p q t k", k=NCOEF)

        ld = [sem(f"m_ld{q}") for q in range(2)]
        li = [sem(f"m_li{q}") for q in range(2)]
        hs = env["att"]["kv"]
        earlier = 2 * (G // 2) * 16 * C
        cs = sem("m_coef"); sq = sem("m_apart"); a0 = sem("m_a0"); a1 = sem("m_a1"); pr = sem("m_prod")
        p01 = sem("m_first_two"); rd = sem("m_vec"); ag = sem("m_agg_s"); ad = sem("m_add"); z = sem("m_zero")

        def done(m, q, per, k):
            return (2 * m + q) * per + k

        def prev(m, q, by=1):
            return (m, q - by) if q - by >= 0 else (m - 1, q - by + 2)

        ZERO = NBE * MW - (NBE * MW * 4 // 7 // P) * P
        block = c.enter_context(nc.Block())

        LAST = min(max(env["NT"] + ceil_div(env["n_nodes"], P) - 1 - (G - 1) * NCH, 2), NCH)

        def whole(eng, group):
            group(0, 0, 0, NCH)
            group(0, 1, 1, NCH)
            with eng.Fori(1, G // 2 - 1) as m:
                group(m, 0, 2, NCH)
                group(m, 1, 2, NCH)
            group(G // 2 - 1, 0, 2, NCH)
            group(G // 2 - 1, 1, 2, LAST)

        def back(m, q, ch):
            return (m, q, ch - 1) if ch >= 2 else (*prev(m, q), NCH + ch - 1)

        @block.sync
        def _(sp):
            def group(m, q, n, chunks):
                cols = bass.ds((2 * m + q) * T, T)
                if n == 2:
                    pm, pq = prev(m, q, 2)
                    sp.wait_ge(a1, done(pm, pq, NCH, NCH))
                    sp.nop(nofuse=True)
                sp.dma_start(idx[:, q * T:(q + 1) * T], env["idx_d"][:, cols]).then_inc(li[q], 16)
                if n == 2:
                    sp.wait_ge(ad, done(pm, pq, NCH, NCH))
                    sp.nop(nofuse=True)
                    sp.wait_ge(a0, done(pm, pq, NCH, NCH))
                    sp.nop(nofuse=True)
                    sp.wait_ge(cs, done(pm, pq, 1, 1))
                    sp.nop(nofuse=True)
                sp.dma_start(dl[:, q, :], env["dl_d"][:, cols]).then_inc(ld[q], 16)
                sp.dma_start(co[:, q, :, :], env["coef_d"][:, cols, :]).then_inc(ld[q], 16)
                sp.dma_start(bB[:, q * NCH:(q + 1) * NCH], env["brow_d"][2:3, bass.ds((2 * m + q) * NCH, NCH)]).then_inc(ld[q], 16)
            whole(sp, group)

        @block.gpsimd
        def _(pool):
            def group(m, q, n, chunks):
                for ch in range(chunks):
                    if n == 2:
                        pm, pq = prev(m, q, 2)
                        pool.wait_ge(rd, done(pm, pq, NCH, ch + 1))
                        pool.wait_ge(a0, done(pm, pq, NCH, ch + 1))
                    if ch == 0:
                        pool.wait_ge(li[q], m * 16 + 16)
                    pool.nop(nofuse=True)
                    for r in range(C):
                        s = q * T + ch * C + r
                        pool.indirect_dma_start(
                            out=hv[:, s, :], out_offset=None, in_=env["h_d"],
                            in_offset=bass.IndirectOffsetOnAxis(ap=idx[:, s:s + 1], axis=0)).then_inc(hs[q][ch], 16)
            whole(pool, group)

        @block.scalar
        def _(act):
            n = (NBE * MW - ZERO) // P
            act.activation(mtab[:, ZERO:NBE * MW].rearrange("p (n w) -> p n w", w=P),
                           iota_b[:, :].unsqueeze(1).to_broadcast((P, n, P)), ACT.Copy, scale=0.0).then_inc(z, 1)
            act.wait_ge(z, 2)

            def group(m, q, n, chunks):
                act.wait_ge(ld[q], m * 48 + 48)
                if n == 2:
                    pm, pq = prev(m, q, 2)
                    act.wait_ge(rd, done(pm, pq, NCH, NCH))
                act.activation(co_ps[:, q, 0:T * NCOEF], co[:, q, :, :].rearrange("p t k -> p (t k)"),
                               ACT.Copy).then_inc(cs, 1)
                for ch in range(chunks):
                    if n or ch >= 2:
                        act.wait_ge(ag, done(*back(m, q, ch)[:2], NCH, back(m, q, ch)[2]))
                    for r in range(C):
                        s = ch * C + r
                        last = act.activation(apart[:, ch % 2, r, :], iota_b[:, :], ACT.Square, scale=-1.0, bias=dl[:, q, s:s + 1])
                    last.then_inc(sq, 1)
                    act.wait_ge(hs[q][ch], m * (16 * C) + (16 * C + earlier))
                    for r in range(C):
                        s = ch * C + r
                        act.activation(vals[:, ch % 2, r, 0:D], hv[:, q * T + s, :], ACT.Copy, scale=co[:, q, s, 12:13])
                    for k in range(3):
                        act.activation(vals[:, ch % 2, C - 1, D + k * MUL:D + (k + 1) * MUL], hv[:, q * T + s, 0:MUL], ACT.Copy,
                                       scale=co[:, q, s, 9 + k:10 + k])
                    act.wait_ge(sq, done(m, q, NCH, ch + 1))
                    act.activation(oh[:, ch % 2, :, :], apart[:, ch % 2, :, :], ACT.Relu, scale=-1.0, bias=one[:, 0:1]).then_inc(a0, 1)
            whole(act, group)

        @block.tensor
        def _(pe):
            pe.wait_ge(z, 2)

            def group(m, q, n, chunks):
                for ch in range(chunks):
                    pe.wait_ge(a0, done(m, q, NCH, ch + 1))
                    pe.wait_ge(rd, done(m, q, NCH, ch + 1))
                    if n or ch >= 2:
                        bm, bq, bc = back(m, q, ch)
                        pe.wait_ge(ad, done(bm, bq, NCH, bc))
                    for r in range(C):
                        last = pe.matmul(agg[:, ch % 2, 0:MW], oh[:, ch % 2, r, :], vals[:, ch % 2, r, :],
                                         start=(r == 0), stop=(r == C - 1))
                    last.then_inc(ag, 1)
            whole(pe, group)

        @block.vector
        def _(dve):
            dve.memset(one[:, :], 1.0)
            dve.memset(mtab[:, 0:ZERO], 0.0).then_inc(z, 1)
            dve.wait_ge(z, 2)

            def block_column(m, q, ch):
                return nc.values_load(bB[0:1, q * NCH + ch:q * NCH + ch + 1], engines=(mybir.EngineType.DVE,), min_val=0,
                                      max_val=(NBE - 1) * MW, skip_runtime_bounds_check_because=CLAMPED)

            def add_sums(m, q, ch, col):
                dve.wait_ge(ag, done(m, q, NCH, ch + 1))
                if not (isinstance(m, int) and m == 0 and q == 0 and ch == 0):
                    dve.wait_ge(ad, done(m, q, NCH, ch))
                mb = mtab[:, bass.ds(col, MW)]
                dve.tensor_tensor(mb, agg[:, ch % 2, 0:MW], mb, ALU.add).then_inc(ad, 1)

            def group(m, q, n, chunks):
                dve.wait_ge(ld[q], m * 48 + 48)
                dve.wait_ge(cs, done(m, q, 1, 1))
                for ch in range(chunks):
                    if n or ch >= 2:
                        bm, bq, bc = back(m, q, ch)
                        dve.wait_ge(ag, done(bm, bq, NCH, bc))
                    dve.wait_ge(hs[q][ch], m * (16 * C) + (16 * C + earlier))
                    s0 = ch * C
                    here = slice(q * T + s0, q * T + s0 + C)
                    for i in range(3):
                        p = prod0[:, ch % 2, :, :, :] if i == 0 else \
                            prod12[:, 2 * (ch % 2) + i - 1, 0:C * D].rearrange("p (r k u) -> p r k u", r=C, k=4)
                        dve.tensor_tensor(p, hv[:, here, MUL + i * MUL:MUL + (i + 1) * MUL].unsqueeze(2)
                                          .to_broadcast((P, C, 4, MUL)),
                                          cp[:, q, s0:s0 + C, i:12:3].unsqueeze(3).to_broadcast((P, C, 4, MUL)),
                                          ALU.mult).then_inc(pr, 1)
                    dve.tensor_tensor(vals[:, ch % 2, 0:C - 1, D:D + 96].rearrange("p r (k u) -> p r k u", k=3),
                                      hv[:, q * T + s0:q * T + s0 + C - 1, 0:MUL].unsqueeze(2).to_broadcast((P, C - 1, 3, MUL)),
                                      cp[:, q, s0:s0 + C - 1, 9:12].unsqueeze(3).to_broadcast((P, C - 1, 3, MUL)),
                                      ALU.mult).then_inc(a1, 1)
                    before = (bm, bq, bc - 1) if n or ch >= 2 else None
                    if before:
                        col = block_column(*before)
                    out = vals[:, ch % 2, :, D + 96:MW]
                    flat = lambda i: prod12[:, 2 * (ch % 2) + i, 0:C * D].rearrange("p (r w) -> p r w", r=C)
                    dve.wait_ge(pr, done(m, q, 3 * NCH, 3 * ch + 3))
                    dve.tensor_tensor(out, prod0[:, ch % 2, :, :, :].rearrange("p r k u -> p r (k u)"), flat(0), ALU.add).then_inc(p01, 1)
                    if before:
                        add_sums(*before, col)
                    dve.wait_ge(p01, done(m, q, NCH, ch + 1))
                    dve.tensor_tensor(out, out, flat(1), ALU.add).then_inc(rd, 1)

            whole(dve, group)
            for ch in (LAST - 2, LAST - 1):
                col = block_column(G // 2 - 1, 1, ch)
                add_sums(G // 2 - 1, 1, ch, col)



def final_phase(nc, sem, env):
    NBE = env["NBE"]
    ident, mtab = env["ident"], env["mtab"]
    W = env["weights"]
    KB = blocks_per_batch(NBE)
    HB = NBE // KB // 2
    r10 = 1.0 / float(np.sqrt(10.0))
    n0 = float(np.sqrt(1.0 / 64)) * r10
    n1 = float(np.sqrt(3.0 / 96)) * r10
    r3 = 1.0 / float(np.sqrt(3.0))
    cst = [n0, n1 * r3, n1 * r3, n0 * r3, n1]
    rows = ([(0, 0, 0, 1)] + [(32 + 32 * k, 2, 32 + k, 3) for k in range(3)] + [(128 + 32 * k, 1, 32 + k, 3) for k in range(3)]
            + [(224 + 32 * k, 4, 32 + k, 3) for k in range(3)] + [(320, 3, 0, 1)])
    with ExitStack() as c:
        def sb(nm, shape, dt=F32):
            return c.enter_context(nc.sbuf_tensor("f_" + nm, shape, dt))

        wraw = sb("wraw", [P, 3, MUL])
        wbig = sb("wbig", [P, 3, D])
        mT = sb("mT", [P, 2, 3, P])
        rows_now = sb("rows_now", [P, 2, MW])
        x1 = sb("x1", [P, 2, KB, D])
        y = sb("y", [P, 2, KB, D])
        pT = c.enter_context(nc.psum_tensor("f_pT", [P, 2, 512], F32))
        po = c.enter_context(nc.psum_tensor("f_po", [P, 2, 512], F32))
        wl = sem("f_wl"); wz = sem("f_wz"); wb = sem("f_wb"); xl = [sem(f"f_x{q}") for q in range(2)]
        rn = sem("f_rows"); tt = sem("f_tr"); mc = sem("f_mT"); mm = sem("f_mm"); ys = sem("f_y"); st = [sem(f"f_st{q}") for q in range(2)]
        block = c.enter_context(nc.Block())
        KS = (128, 128, 96)

        def done(m, q, k):
            return (2 * m + q) * KB + (k + 1)

        def after(m, q, k, by):
            k += by
            while k >= KB:
                m, q, k = (m, 1, k - KB) if q == 0 else (m + 1, 0, k - KB)
            return None if isinstance(m, int) and m == HB else (m, q, k)

        def whole(eng, batch):
            batch(0, 0, 0)
            batch(0, 1, 1)
            with eng.Fori(1, HB - 1) as m:
                batch(m, 0, 2)
                batch(m, 1, 2)
            batch(HB - 1, 0, 2)
            batch(HB - 1, 1, 2)

        def dram_rows(ap, m, q):
            return ap[bass.ds((2 * m + q) * (KB * P), KB * P), :].rearrange("(k p) n -> p k n", p=P)

        @block.sync
        def _(sp):
            for r, k, _, _ in rows:
                sp.dma_start(wraw[r % P:r % P + MUL, r // P, :], W[f"w{k}"]).then_inc(wl, 16)

            def batch(m, q, n):
                if n == 2:
                    sp.wait_ge(ys, done(m - 1, q, KB - 1))
                    sp.nop(nofuse=True)
                sp.dma_start(x1[:, q, :, :], dram_rows(env["x1_d"], m, q)).then_inc(xl[q], 16)
            whole(sp, batch)

        @block.gpsimd
        def _(pool):
            def batch(m, q, n):
                pool.wait_ge(ys, done(m, q, KB - 1))
                pool.nop(nofuse=True)
                pool.dma_start(dram_rows(env["out"], m, q), y[:, q, :, :]).then_inc(st[q], 16)
            whole(pool, batch)
            for q in range(2):
                pool.wait_ge(st[q], 16 * HB)

        @block.tensor
        def _(pe):
            def turn(m, q, k, first):
                i = (q * KB + k) % 2
                pe.wait_ge(rn, done(m, q, k))
                if not first:
                    pe.wait_ge(mc, done(m, q, k - 2))
                for j, w in enumerate(KS):
                    last = pe.transpose(pT[0:w, i, j * P:(j + 1) * P], rows_now[:, i, j * P:j * P + w], ident[:, :])
                last.then_inc(tt, 1)

            def batch(m, q, n):
                for k in range(KB):
                    i = (q * KB + k) % 2
                    nxt = after(m, q, k, 1)
                    if nxt:
                        turn(*nxt, n * KB + k < 1)
                    pe.wait_ge(mc, done(m, q, k))
                    if n * KB + k >= 2:
                        pe.wait_ge(ys, done(m, q, k - 2))
                    for j, w in enumerate(KS):
                        last = pe.matmul(po[:, i, 0:D], mT[0:w, i, j, :], wbig[0:w, j, :], start=(j == 0), stop=(j == 2))
                    last.then_inc(mm, 1)

            pe.wait_ge(wb, len(rows))
            turn(0, 0, 0, True)
            whole(pe, batch)

        @block.scalar
        def _(act):
            def batch(m, q, n):
                for k in range(KB):
                    i = (q * KB + k) % 2
                    act.wait_ge(tt, done(m, q, k))
                    if n * KB + k >= 2:
                        act.wait_ge(mm, done(m, q, k - 2))
                    act.activation(mT[:, i, 0:2, :].rearrange("p j n -> p (j n)"), pT[:, i, 0:2 * P], ACT.Copy)
                    act.activation(mT[0:96, i, 2, :], pT[0:96, i, 2 * P:3 * P], ACT.Copy).then_inc(mc, 1)
            whole(act, batch)

        @block.vector
        def _(dve):
            dve.memset(wbig[:, :, :], 0.0).then_inc(wz, 1)
            dve.wait_ge(wz, 1)
            dve.wait_ge(wl, 16 * len(rows))
            for r, k, col, step in rows:
                o = wbig[r % P:r % P + MUL, r // P, col:col + step * (MUL - 1) + 1:step]
                dve.tensor_scalar(o, wraw[r % P:r % P + MUL, r // P, :], cst[k], None, ALU.mult).then_inc(wb, 1)

            def fetch(m, q, k, first):
                if not first:
                    dve.wait_ge(tt, done(m, q, k - 2))
                dve.tensor_copy(rows_now[:, (q * KB + k) % 2, :],
                                mtab[:, bass.ds(((2 * m + q) * KB + k) * MW, MW)]).then_inc(rn, 1)

            def batch(m, q, n):
                for k in range(KB):
                    nxt = after(m, q, k, 2)
                    if nxt:
                        fetch(*nxt, False)
                    dve.wait_ge(mm, done(m, q, k))
                    if k == 0:
                        dve.wait_ge(xl[q], m * 16 + 16)
                        if n == 2:
                            dve.wait_ge(st[q], m * 16)
                    dve.tensor_tensor(y[:, q, k, :], po[:, (q * KB + k) % 2, 0:D], x1[:, q, k, :], ALU.add).then_inc(ys, 1)

            fetch(0, 0, 0, True)
            fetch(*after(0, 0, 0, 1), True)
            whole(dve, batch)



def kernel(**inputs):
    import numpy as _np
    import concourse.bacc as _bacc
    from concourse import mybir as _mybir
    from concourse.bass_utils import run_bass_kernel_spmd as _run

    x = _np.asarray(inputs["x"])
    n_nodes, n_edges = x.shape[0], inputs["src"].shape[0]
    NBE, NT, _, _ = sizes(n_nodes, n_edges)

    def triples(a, fill):
        a = _np.asarray(a)
        out = _np.full(((NT + 1) * C * P,) + a.shape[1:], fill, a.dtype)
        out[:n_edges] = a
        return out.reshape((NT + 1, C * P) + a.shape[1:])

    x_p = _np.zeros((NBE * P, D), x.dtype)
    x_p[:n_nodes] = x
    dst_t = triples(inputs["dst"], (NBE + 1) * P)
    arrays = {
        "x_p": x_p,
        "src_t": triples(inputs["src"], 0),
        "dst_t": dst_t,
        "dlast": _np.ascontiguousarray(dst_t[:NT, -1][None, :]),
        "ew_t": triples(inputs["edge_weight"], 0),
        "attr_t": _np.ascontiguousarray(triples(inputs["edge_attr_9"], 0).transpose(0, 2, 1)).reshape(NT + 1, 9 * C * P),
    }
    wnames = {}
    for l in (1, 2):
        for k in ("Wq", "bq", "Wk", "bk", "Wv", "bv", "We", "Ws", "bs"):
            wnames[f"{k}{l}"] = f"L0_gnn_{k}{l}"
    for k in range(5):
        wnames[f"w{k}"] = f"L1_gnn_w{k}"
    for short, full in wnames.items():
        a = _np.ascontiguousarray(inputs[full])
        arrays["in_" + short] = a.reshape(MUL, MUL) if full.startswith("L1") else a

    nc = _bacc.Bacc("TRN2", target_bir_lowering=False, num_devices=1)
    aps = {n: nc.dram_tensor(n, a.shape, _mybir.dt.from_np(a.dtype), kind="ExternalInput").ap() for n, a in arrays.items()}
    out = nc.dram_tensor("out", (NBE * P, D), F32, kind="ExternalOutput").ap()
    weights = {short: aps["in_" + short] for short in wnames}
    weights["n_nodes"], weights["n_edges"] = n_nodes, n_edges
    build(nc, aps["x_p"], aps["src_t"], aps["dst_t"], aps["dlast"], aps["ew_t"], aps["attr_t"], weights, out)
    r = _run(nc, [arrays], core_ids=[0])
    return r.results[0]["out"][:n_nodes]
```
